# Optimizing a Trainium2 kernel written in Bass

```python
import numpy as np
import jax
import jax.numpy as jnp

def _softmax(x, axis=-1):
    return jax.nn.softmax(x, axis=axis)

def _gelu(x):
    return jax.nn.gelu(x, approximate=True)

def _silu(x):
    return jax.nn.silu(x)

def _sigmoid(x):
    return jax.nn.sigmoid(x)

def _layernorm(x, axis=-1, eps=1e-05):
    m = jnp.mean(x, axis=axis, keepdims=True)
    v = jnp.var(x, axis=axis, keepdims=True)
    return (x - m) / jnp.sqrt(v + eps)

def _scatter_add(tgt, idx, src, axis=0):
    return tgt.at[idx].add(src)

def _segment_sum(src, seg, n):
    return jax.ops.segment_sum(src, seg, n)
kernel_name = 'mk_gnn_preln_d4_gnn_r32_d9e126'

def setup_inputs(seed: int=0):
    np.random.seed(seed)
    _w = jnp.asarray

    def _rec_inputs():
        import jax
        import jax.numpy as jnp
        _gk = jax.random.key(seed)
        x = -0.0009044 + 1 * jax.random.normal(jax.random.fold_in(_gk, 1), (3125, 16), jnp.float32)
        src = jax.random.randint(jax.random.fold_in(_gk, 2), (100000,), 0, 3125, jnp.int32)
        dst = jnp.minimum((3125 * jax.random.uniform(jax.random.fold_in(_gk, 3), (100000,)) ** 2.0).astype(jnp.int32), 99999)
        _o = jnp.argsort(dst, stable=True)
        src = src[_o]
        dst = dst[_o]
        edge_attr_16 = -3.57403e-05 + 0.999761 * jax.random.normal(jax.random.fold_in(_gk, 12), (100000, 16), jnp.float32)
        edge_type_8 = jax.random.randint(jax.random.fold_in(_gk, 14), (100000,), 0, 8, jnp.int32)
        edge_weight = jax.random.uniform(jax.random.fold_in(_gk, 15), (100000,), jnp.float32, 0.0, 0.999998)
        return (x, src, dst, edge_attr_16, edge_type_8, edge_weight)
    x, src, dst, edge_attr_16, edge_type_8, edge_weight = _rec_inputs()

    def _L0_gnn_setup():
        import jax, jax.numpy as jnp
        import numpy as np
        N_NODES = 3125
        N_EDGES = 31250
        MSG_DIM = 16
        HID_DIM = 16
        N_EDGE_TYPE = 8
        key = jax.random.key(seed)
        ks = jax.random.split(key, 9)
        features = jax.random.normal(ks[0], (N_NODES, HID_DIM), dtype=jnp.float32)
        edge_src = jax.random.randint(ks[1], (N_EDGES,), 0, N_NODES, dtype=jnp.int32)
        edge_dst = jax.random.randint(ks[2], (N_EDGES,), 0, N_NODES, dtype=jnp.int32)
        edge_type = jax.random.randint(ks[3], (N_EDGES,), 0, N_EDGE_TYPE, dtype=jnp.int32)
        edge_emb = jax.random.normal(ks[4], (N_EDGE_TYPE, MSG_DIM * HID_DIM), dtype=jnp.float32) * 0.1
        s = 1.0 / np.sqrt(HID_DIM)
        w_ih = jax.random.uniform(ks[5], (3 * HID_DIM, MSG_DIM), minval=-s, maxval=s, dtype=jnp.float32)
        w_hh = jax.random.uniform(ks[6], (3 * HID_DIM, HID_DIM), minval=-s, maxval=s, dtype=jnp.float32)
        b_ih = jax.random.uniform(ks[7], (3 * HID_DIM,), minval=-s, maxval=s, dtype=jnp.float32)
        b_hh = jax.random.uniform(ks[8], (3 * HID_DIM,), minval=-s, maxval=s, dtype=jnp.float32)
        return {'features': features, 'edge_src': edge_src, 'edge_dst': edge_dst, 'edge_type': edge_type, 'edge_emb': edge_emb, 'w_ih': w_ih, 'w_hh': w_hh, 'b_ih': b_ih, 'b_hh': b_hh}
    _L0_gnn_all = _L0_gnn_setup()
    _L0_gnn_in = {k: v for k, v in _L0_gnn_all.items() if k in ('edge_emb', 'w_ih', 'w_hh', 'b_ih', 'b_hh')}
    del _L0_gnn_all

    def _L1_gnn_setup():
        import jax, jax.numpy as jnp
        import numpy as np
        N_NODES = 30000
        N_EDGES = 9375
        IN_FEATS = 16
        OUT_FEATS = 16
        EDGE_DIM = 16
        key = jax.random.key(seed)
        ks = jax.random.split(key, 8)
        feat = jax.random.normal(ks[0], (N_NODES, IN_FEATS), dtype=jnp.float32)
        efeat = jax.random.normal(ks[1], (N_EDGES, EDGE_DIM), dtype=jnp.float32)
        W_msg = jax.random.normal(ks[2], (EDGE_DIM, IN_FEATS * OUT_FEATS), dtype=jnp.float32) * 0.1
        b_msg = jnp.zeros((IN_FEATS * OUT_FEATS,), dtype=jnp.float32)
        W_attn = jax.random.normal(ks[3], (EDGE_DIM, IN_FEATS * OUT_FEATS), dtype=jnp.float32) * 0.1
        b_attn = jnp.zeros((IN_FEATS * OUT_FEATS,), dtype=jnp.float32)
        src = jax.random.randint(ks[4], (N_EDGES,), 0, N_NODES, dtype=jnp.int32)
        dst = jax.random.randint(ks[5], (N_EDGES,), 0, N_NODES, dtype=jnp.int32)
        return {'feat': feat, 'efeat': efeat, 'W_msg': W_msg, 'b_msg': b_msg, 'W_attn': W_attn, 'b_attn': b_attn, 'src': src, 'dst': dst}
    _L1_gnn_all = _L1_gnn_setup()
    _L1_gnn_in = {k: v for k, v in _L1_gnn_all.items() if k in ('W_msg', 'b_msg', 'W_attn', 'b_attn')}
    del _L1_gnn_all

    def _L2_gnn_setup():
        import jax, jax.numpy as jnp
        import numpy as np
        N_NODES = 50000
        N_EDGES = 25000
        IN_CH = 16
        HIDDEN = [128, 128, 128]
        OUT_CH = 16
        SELF_LOOP_W = 2.0

        def _glorot(key, fan_in, fan_out):
            s = jnp.sqrt(6.0 / (fan_in + fan_out))
            return jax.random.uniform(key, (fan_in, fan_out), jnp.float32, -s, s)

        def _gcn_norm(edge_index, edge_attr, n):
            src = jnp.concatenate([edge_index[0], jnp.arange(n, dtype=edge_index.dtype)])
            dst = jnp.concatenate([edge_index[1], jnp.arange(n, dtype=edge_index.dtype)])
            w = jnp.concatenate([edge_attr, jnp.full((n,), SELF_LOOP_W, edge_attr.dtype)])
            deg = jax.ops.segment_sum(w, dst, num_segments=n)
            dinv = jnp.where(deg > 0, jax.lax.rsqrt(jnp.where(deg > 0, deg, 1.0)), 0.0)
            norm = dinv[src] * w * dinv[dst]
            return (src, dst, norm)

        def _gcn_conv(x, src, dst, norm, w, b, n):
            h = x @ w
            msg = norm[:, None] * h[src]
            return jax.ops.segment_sum(msg, dst, num_segments=n) + b
        key = jax.random.key(seed)
        ks = jax.random.split(key, 12)
        x = jax.random.normal(ks[0], (N_NODES, IN_CH), jnp.float32)
        edge_index = jax.random.randint(ks[1], (2, N_EDGES), 0, N_NODES, jnp.int64)
        edge_attr = jax.random.uniform(ks[2], (N_EDGES,), jnp.float32)
        dims = [IN_CH] + HIDDEN + [OUT_CH]
        inp = {'x': x, 'edge_index': edge_index, 'edge_attr': edge_attr}
        for i in range(4):
            inp[f'w{i}'] = _glorot(ks[3 + i], dims[i], dims[i + 1])
            inp[f'b{i}'] = jnp.zeros((dims[i + 1],), jnp.float32)
        return inp
    _L2_gnn_all = _L2_gnn_setup()
    _L2_gnn_in = {k: v for k, v in _L2_gnn_all.items() if k in ('w0', 'b0', 'w1', 'b1', 'w2', 'b2', 'w3', 'b3')}
    del _L2_gnn_all

    def _L3_gnn_setup():
        import jax, jax.numpy as jnp
        import numpy as np
        STALK_DIM = 16
        N_NODES = 50000
        N_EDGES = 12500
        HIDDEN = 64
        key = jax.random.key(seed)
        k1, k2, k3, k4 = jax.random.split(key, 4)
        d = STALK_DIM
        x = jax.random.normal(k1, (N_NODES, d), dtype=jnp.float32)
        edge_index = jax.random.randint(k2, (2, N_EDGES), 0, N_NODES, dtype=jnp.int64)
        W1 = jax.random.normal(k3, (HIDDEN, 2 * d), dtype=jnp.float32) * (1.0 / np.sqrt(2 * d))
        b1 = jnp.zeros((HIDDEN,), dtype=jnp.float32)
        W2 = jax.random.normal(k4, (d, HIDDEN), dtype=jnp.float32) * (1.0 / np.sqrt(HIDDEN))
        b2 = jnp.zeros((d,), dtype=jnp.float32)
        return {'x': x, 'edge_index': edge_index, 'W1': W1, 'b1': b1, 'W2': W2, 'b2': b2}
    _L3_gnn_all = _L3_gnn_setup()
    _L3_gnn_in = {k: v for k, v in _L3_gnn_all.items() if k in ('W1', 'b1', 'W2', 'b2')}
    del _L3_gnn_all
    return {'x': x, 'src': src, 'dst': dst, 'edge_attr_16': edge_attr_16, 'edge_type_8': edge_type_8, 'edge_weight': edge_weight, 'L0_gnn_edge_emb': _L0_gnn_in['edge_emb'], 'L0_gnn_w_ih': _L0_gnn_in['w_ih'], 'L0_gnn_w_hh': _L0_gnn_in['w_hh'], 'L0_gnn_b_ih': _L0_gnn_in['b_ih'], 'L0_gnn_b_hh': _L0_gnn_in['b_hh'], 'L1_gnn_W_msg': _L1_gnn_in['W_msg'], 'L1_gnn_b_msg': _L1_gnn_in['b_msg'], 'L1_gnn_W_attn': _L1_gnn_in['W_attn'], 'L1_gnn_b_attn': _L1_gnn_in['b_attn'], 'L2_gnn_w0': _L2_gnn_in['w0'], 'L2_gnn_b0': _L2_gnn_in['b0'], 'L2_gnn_w1': _L2_gnn_in['w1'], 'L2_gnn_b1': _L2_gnn_in['b1'], 'L2_gnn_w2': _L2_gnn_in['w2'], 'L2_gnn_b2': _L2_gnn_in['b2'], 'L2_gnn_w3': _L2_gnn_in['w3'], 'L2_gnn_b3': _L2_gnn_in['b3'], 'L3_gnn_W1': _L3_gnn_in['W1'], 'L3_gnn_b1': _L3_gnn_in['b1'], 'L3_gnn_W2': _L3_gnn_in['W2'], 'L3_gnn_b2': _L3_gnn_in['b2']}

def reference(x, src, dst, edge_attr_16, edge_type_8, edge_weight, L0_gnn_edge_emb, L0_gnn_w_ih, L0_gnn_w_hh, L0_gnn_b_ih, L0_gnn_b_hh, L1_gnn_W_msg, L1_gnn_b_msg, L1_gnn_W_attn, L1_gnn_b_attn, L2_gnn_w0, L2_gnn_b0, L2_gnn_w1, L2_gnn_b1, L2_gnn_w2, L2_gnn_b2, L2_gnn_w3, L2_gnn_b3, L3_gnn_W1, L3_gnn_b1, L3_gnn_W2, L3_gnn_b2):
    import jax
    import jax.numpy as jnp

    def _L0_gnn_ref(features, edge_src, edge_dst, edge_type, edge_emb, w_ih, w_hh, b_ih, b_hh):
        import jax, jax.numpy as jnp
        import numpy as np
        N_NODES = 3125
        N_EDGES = 31250
        MSG_DIM = 16
        HID_DIM = 16
        N_EDGE_TYPE = 8
        n_nodes = features.shape[0]
        A = edge_emb[edge_type].reshape(-1, MSG_DIM, HID_DIM)
        h_src = features[edge_src]
        msg = jnp.einsum('emh,eh->em', A, h_src)
        m = jax.ops.segment_sum(msg, edge_dst, num_segments=n_nodes)
        gi = m @ w_ih.T + b_ih
        gh = features @ w_hh.T + b_hh
        i_r, i_z, i_n = jnp.split(gi, 3, axis=-1)
        h_r, h_z, h_n = jnp.split(gh, 3, axis=-1)
        r = jax.nn.sigmoid(i_r + h_r)
        z = jax.nn.sigmoid(i_z + h_z)
        n = jnp.tanh(i_n + r * h_n)
        h_new = (1.0 - z) * n + z * features
        return h_new

    def _L1_gnn_ref(feat, efeat, W_msg, b_msg, W_attn, b_attn, src, dst):
        import jax, jax.numpy as jnp
        import numpy as np
        N_NODES = 30000
        N_EDGES = 9375
        IN_FEATS = 16
        OUT_FEATS = 16
        EDGE_DIM = 16
        N, in_f = feat.shape
        E = efeat.shape[0]
        w_m = (efeat @ W_msg + b_msg).reshape(E, in_f, -1)
        w_a = (efeat @ W_attn + b_attn).reshape(E, in_f, -1)
        h_src = feat[src][:, :, None]
        e1 = w_m * h_src
        e2 = w_a * h_src
        seg_max = jax.ops.segment_max(e2, dst, num_segments=N)
        ex = jnp.exp(e2 - seg_max[dst])
        denom = jax.ops.segment_sum(ex, dst, num_segments=N)
        attn = ex / denom[dst]
        ft = jax.ops.segment_sum(e1 * attn, dst, num_segments=N)
        return ft.sum(axis=1)

    def _L2_gnn_ref(x, edge_index, edge_attr, w0, b0, w1, b1, w2, b2, w3, b3):
        import jax, jax.numpy as jnp
        import numpy as np
        N_NODES = 50000
        N_EDGES = 25000
        IN_CH = 16
        HIDDEN = [128, 128, 128]
        OUT_CH = 16
        SELF_LOOP_W = 2.0

        def _glorot(key, fan_in, fan_out):
            s = jnp.sqrt(6.0 / (fan_in + fan_out))
            return jax.random.uniform(key, (fan_in, fan_out), jnp.float32, -s, s)

        def _gcn_norm(edge_index, edge_attr, n):
            src = jnp.concatenate([edge_index[0], jnp.arange(n, dtype=edge_index.dtype)])
            dst = jnp.concatenate([edge_index[1], jnp.arange(n, dtype=edge_index.dtype)])
            w = jnp.concatenate([edge_attr, jnp.full((n,), SELF_LOOP_W, edge_attr.dtype)])
            deg = jax.ops.segment_sum(w, dst, num_segments=n)
            dinv = jnp.where(deg > 0, jax.lax.rsqrt(jnp.where(deg > 0, deg, 1.0)), 0.0)
            norm = dinv[src] * w * dinv[dst]
            return (src, dst, norm)

        def _gcn_conv(x, src, dst, norm, w, b, n):
            h = x @ w
            msg = norm[:, None] * h[src]
            return jax.ops.segment_sum(msg, dst, num_segments=n) + b
        n = x.shape[0]
        src, dst, norm = _gcn_norm(edge_index, edge_attr, n)
        ws = [(w0, b0), (w1, b1), (w2, b2), (w3, b3)]
        for i, (w, b) in enumerate(ws):
            x = _gcn_conv(x, src, dst, norm, w, b, n)
            if i < len(ws) - 1:
                x = jax.nn.relu(x)
        return x

    def _L3_gnn_ref(x, edge_index, W1, b1, W2, b2):
        import jax, jax.numpy as jnp
        import numpy as np
        STALK_DIM = 16
        N_NODES = 50000
        N_EDGES = 12500
        HIDDEN = 64
        d = x.shape[1]
        n = x.shape[0]
        src, dst = (edge_index[0], edge_index[1])
        xs, xd = (x[src], x[dst])

        def reflection(a, b):
            h = jax.nn.relu(jnp.concatenate([a, b], axis=1) @ W1.T + b1)
            return h @ W2.T + b2

        def householder(v):
            vn = v / jnp.maximum(jnp.linalg.norm(v, axis=1, keepdims=True), 1e-12)
            return jnp.eye(d, dtype=v.dtype)[None] - 2.0 * vn[:, :, None] * vn[:, None, :]
        F_s = householder(reflection(xs, xd))
        F_d = householder(reflection(xd, xs))
        L_sd = -jnp.einsum('eki,ekj->eij', F_s, F_d)
        ones_e = jnp.ones(src.shape[0], dtype=x.dtype)
        deg = jnp.zeros(n, dtype=x.dtype).at[src].add(ones_e).at[dst].add(ones_e)
        deg_inv_sqrt = 1.0 / jnp.sqrt(jnp.maximum(deg, 1e-05))
        coef = deg_inv_sqrt[src] * deg_inv_sqrt[dst]
        msg_s = coef[:, None] * jnp.einsum('eij,ej->ei', L_sd, xd)
        msg_d = coef[:, None] * jnp.einsum('eji,ej->ei', L_sd, xs)
        out = x - jnp.zeros_like(x).at[src].add(msg_s) - jnp.zeros_like(x).at[dst].add(msg_d)
        return jax.nn.relu(out)
    edge_index = jnp.stack([src, dst])
    h = jnp.maximum(_layernorm(x, axis=-1), 0.0)
    x = x + _L0_gnn_ref(h, src, dst, edge_type_8, L0_gnn_edge_emb, L0_gnn_w_ih, L0_gnn_w_hh, L0_gnn_b_ih, L0_gnn_b_hh)
    h = jnp.maximum(_layernorm(x, axis=-1), 0.0)
    x = x + _L1_gnn_ref(h, edge_attr_16, L1_gnn_W_msg, L1_gnn_b_msg, L1_gnn_W_attn, L1_gnn_b_attn, src, dst)
    h = jnp.maximum(_layernorm(x, axis=-1), 0.0)
    x = x + _L2_gnn_ref(h, edge_index, edge_weight, L2_gnn_w0, L2_gnn_b0, L2_gnn_w1, L2_gnn_b1, L2_gnn_w2, L2_gnn_b2, L2_gnn_w3, L2_gnn_b3)
    h = jnp.maximum(_layernorm(x, axis=-1), 0.0)
    x = x + _L3_gnn_ref(h, edge_index, L3_gnn_W1, L3_gnn_b1, L3_gnn_W2, L3_gnn_b2)
    return x

_drawn_inputs = setup_inputs


def setup_inputs(seed=0):
    import zlib

    import numpy as np

    out = dict(_drawn_inputs(seed))
    spreads = {'L1_gnn_b_msg': (0.0, 0.1),
     'L1_gnn_b_attn': (0.0, 0.1),
     'L2_gnn_b0': (0.0, 0.1),
     'L2_gnn_b1': (0.0, 0.1),
     'L2_gnn_b2': (0.0, 0.1),
     'L2_gnn_b3': (0.0, 0.1),
     'L3_gnn_b1': (0.0, 2.0),
     'L3_gnn_b2': (0.0, 2.0)}
    factors = {'edge_weight': 200.0, 'L3_gnn_W1': 4.564, 'L3_gnn_W2': 4.555}
    for name, (base, spread) in spreads.items():
        noise = np.random.default_rng([zlib.crc32(name.encode()), seed]).standard_normal(out[name].shape)
        drawn = base * np.exp(spread * noise) if base else spread * noise
        out[name] = jnp.asarray(drawn.astype(out[name].dtype))
    for name, factor in factors.items():
        out[name] = (out[name] * factor).astype(out[name].dtype)
    return out
```

```python
from contextlib import ExitStack

import concourse.bass as bass
from concourse import mybir

ALU = mybir.AluOpType
ACT = mybir.ActivationFunctionType
AX = mybir.AxisListType
F32 = mybir.dt.float32
I32 = mybir.dt.int32
BF16 = mybir.dt.bfloat16
FP16 = mybir.dt.float16

P = 128
N, E, D = 3125, 100000, 16
NB = -(-N // P)
NP = NB * P
TAIL = N - (NB - 1) * P
EP, EC = 125, 800
NS = 4
SC = EC // NS
TB = 8
NT = -(-((E + NB * (P - 1)) // P) // (2 * TB)) * 2 * TB
SLOTS = NT * P
IT = NT // (2 * TB)

ONE, WGT, SRC, TIX, LO, SRCC, KEY, LOE, REC = 16, 17, 18, 19, 20, 21, 22, 23, 24
CENTRE = N // 2
FAR = -3.0e38

GROUPS = [(0, 6), (6, 5), (11, 5)]


class Net:
    pass


def makers(nc, ctx, stage):
    def sb(name, shape, dt=F32):
        return ctx.enter_context(nc.sbuf_tensor(f"{stage}_{name}", shape, dt))

    def ps(name, shape, dt=F32):
        return ctx.enter_context(nc.psum_tensor(f"{stage}_{name}", shape, dt))

    def sem(name):
        made = nc.alloc_semaphore(f"{stage}_{name}")
        ctx.callback(PAST.append, made)
        return made

    return sb, ps, sem


PAST = []


def renew_semaphores(nc):
    nc.clear_and_free_semaphores(list(PAST))
    PAST.clear()
    with nc.Block():
        pass




def record_keys(nc, a, m):
    with ExitStack() as ctx:
        sb, ps, sem = makers(nc, ctx, "rec")
        dst_i, src_i, typ_i, tmp_i = (sb(n, [EP, EC], I32) for n in ("dst_i", "src_i", "typ_i", "tmp_i"))
        tmp2_i = sb("tmp2_i", [EP, EC], I32)
        wgt = sb("wgt", [EP, EC])
        feat = sb("feat", [EP, EC * D // 4])
        rows = sb("rows", [100, 2, 8, EP])
        turned = ps("turned", [100, 2, 4, P])
        idx_in, feat_in, feat_free = sem("idx_in"), sem("feat_in"), sem("feat_free")
        keys, mid, rec = sem("keys"), sem("mid"), sem("rec")
        turned_s, rows_s, rows_out, consts = sem("turned_s"), sem("rows_s"), sem("rows_out"), sem("consts")
        hole = sb("hole", [P, 48 * REC])
        holes_s, hole_s = sem("holes_s"), sem("hole_s")
        edges = m.slots_sb[0:EP, 0:EC * REC].rearrange("p (c k) -> p c k", k=REC)
        feats = a["edge_attr_16"].rearrange("(p c) d -> p (c d)", p=EP)
        block = ctx.enter_context(nc.Block())

        @block.sync
        def _(sp):
            sp.dma_start(dst_i[:, :], a["dst"].rearrange("(p c) -> p c", p=EP)).then_inc(idx_in, 16)
            sp.dma_start(src_i[:, :], a["src"].rearrange("(p c) -> p c", p=EP)).then_inc(idx_in, 16)
            sp.dma_start(typ_i[:, :], a["edge_type_8"].rearrange("(p c) -> p c", p=EP)).then_inc(idx_in, 16)
            sp.dma_start(wgt[:, :], a["edge_weight"].rearrange("(p c) -> p c", p=EP)).then_inc(idx_in, 16)
            q = EC * D // 4
            for c in range(4):
                if c:
                    sp.wait_ge(feat_free, c)
                sp.dma_start(feat[:, :], feats[:, c * q:(c + 1) * q]).then_inc(feat_in, 16)
            sp.wait_ge(rows_s, 4)
            for k, dram in ((0, m.key_rows), (1, m.hi_rows)):
                sp.dma_start(dram.rearrange("(g t) p -> t g p", g=8), rows[:, k, :, :]).then_inc(rows_out, 16)
            sp.wait_ge(hole_s, 4)
            whole = m.slots.rearrange("(p c n) k -> p c (n k)", p=P, n=48)
            sp.dma_start(whole, hole[:, None, :].to_broadcast([P, NT // 48, 48 * REC])).then_inc(holes_s, 16)
            sp.wait_ge(rows_out, 32)
            sp.wait_ge(holes_s, 16)

        @block.gpsimd
        def _(pool):
            pool.iota(m.iota_row[:, :], pattern=[[1, P]], base=0, channel_multiplier=0,
                      allow_small_or_imprecise_dtypes=True).then_inc(consts, 1)
            pool.iota(m.iota_col[:, :], pattern=[[0, 1]], base=0, channel_multiplier=1,
                      allow_small_or_imprecise_dtypes=True).then_inc(consts, 1)
            pool.iota(m.iota_tiles[:, :], pattern=[[1, NT]], base=0, channel_multiplier=0,
                      allow_small_or_imprecise_dtypes=True).then_inc(consts, 1)
            pool.memset(m.zero_row[:, :], 0.0).then_inc(consts, 1)

        @block.vector
        def _(dve):
            dve.wait_ge(consts, 3)
            nc.vector.tensor_scalar(m.ident[:, :], m.iota_row[:, :], m.iota_col[:, 0:1], None, ALU.is_equal).then_inc(keys, 1)
            nc.vector.tensor_scalar(m.below[:, :], m.iota_row[:, :], m.iota_col[:, 0:1], None, ALU.is_lt).then_inc(keys, 1)
            nc.vector.tensor_scalar(m.above[:, :], m.iota_row[:, :], m.iota_col[:, 0:1], None, ALU.is_gt).then_inc(keys, 1)
            hv = hole[:, :].rearrange("p (n k) -> p n k", k=REC)
            nc.vector.memset(hole[:, :], 0.0).then_inc(hole_s, 1)
            dve.wait_ge(hole_s, 1)
            nc.vector.memset(hv[:, :, LO], -1.0).then_inc(hole_s, 1)
            nc.vector.memset(hv[:, :, KEY], -1.0).then_inc(hole_s, 1)
            nc.vector.memset(hv[:, :, SRCC], -3.0 * CENTRE).then_inc(hole_s, 1)
            dve.wait_ge(idx_in, 64)
            nc.vector.tensor_single_scalar(tmp_i[:, :], dst_i[:, :], 7, ALU.logical_shift_right).then_inc(mid, 1)
            nc.vector.tensor_single_scalar(tmp2_i[:, :], dst_i[:, :], P - 1, ALU.bitwise_and).then_inc(mid, 1)
            nc.vector.tensor_copy(m.key_f[:, :], dst_i[:, :]).then_inc(keys, 1)
            dve.wait_ge(mid, 2)
            nc.vector.tensor_copy(m.hi_f[:, :], tmp_i[:, :]).then_inc(keys, 1)
            nc.vector.tensor_copy(m.lo_f[:, :], tmp2_i[:, :]).then_inc(mid, 1)
            dve.wait_ge(mid, 3)
            dve.wait_ge(keys, 5)
            nc.vector.tensor_copy(edges[:, :, LO], m.lo_f[:, :]).then_inc(rec, 1)
            nc.vector.tensor_copy(edges[:, :, KEY], m.key_f[:, :]).then_inc(rec, 1)
            nc.vector.tensor_single_scalar(tmp_i[:, :], src_i[:, :], 7, ALU.logical_shift_right).then_inc(mid, 1)
            nc.vector.tensor_single_scalar(tmp2_i[:, :], src_i[:, :], P - 1, ALU.bitwise_and).then_inc(mid, 1)
            dve.wait_ge(mid, 5)
            nc.vector.tensor_copy(m.src_hi_f[:, :], tmp_i[:, :]).then_inc(rec, 1)
            nc.vector.tensor_copy(m.src_lo_f[:, :], tmp2_i[:, :]).then_inc(rec, 1)
            nc.vector.tensor_copy(edges[:, :, SRC], src_i[:, :]).then_inc(rec, 1)
            nc.vector.tensor_scalar(edges[:, :, SRCC], src_i[:, :], -float(CENTRE), None, ALU.add).then_inc(rec, 1)
            nc.vector.scalar_tensor_tensor(edges[:, :, TIX], src_i[:, :], 8.0, typ_i[:, :], ALU.mult, ALU.add).then_inc(rec, 1)
            nc.vector.tensor_copy(edges[:, :, WGT], wgt[:, :]).then_inc(rec, 1)
            nc.vector.memset(edges[:, :, ONE], 1.0).then_inc(rec, 1)
            nc.vector.memset(edges[:, :, LOE], 0.0).then_inc(rec, 1)
            for k in range(2):
                for half in range(2):
                    dve.wait_ge(turned_s, 2 * k + half + 1)
                    nc.vector.tensor_copy(rows[:, k, 4 * half:4 * half + 4, :], turned[:, half, :, 0:EP]).then_inc(rows_s, 1)

        @block.tensor
        def _(pe):
            pe.wait_ge(keys, 5)
            for k, what in enumerate((m.key_f, m.hi_f)):
                for half in range(2):
                    if k:
                        pe.wait_ge(rows_s, half + 1)
                    for g in range(4):
                        c = 100 * (4 * half + g)
                        last = nc.tensor.transpose(turned[:, half, g, 0:EP], what[:, c:c + 100], m.ident[0:EP, 0:EP])
                    last.then_inc(turned_s, 1)

        @block.scalar
        def _(act):
            for c in range(4):
                act.wait_ge(feat_in, 16 * (c + 1))
                nc.scalar.copy(edges[:, c * SC:(c + 1) * SC, 0:D],
                               feat[:, :].rearrange("p (c d) -> p c d", d=D)).then_inc(feat_free, 1)


def histogram(nc, m):
    with ExitStack() as ctx:
        sb, ps, sem = makers(nc, ctx, "hist")
        hot_lo, hot_slo = sb("hot_lo", [EP, 2, NS, P], BF16), sb("hot_slo", [EP, 2, NS, P], BF16)
        hot_hi, hot_shi = sb("hot_hi", [EP, 2, NS, NB], BF16), sb("hot_shi", [EP, 2, NS, NB], BF16)
        by_dst, by_src, small = ps("by_dst", [NB, NS * P]), ps("by_src", [NB, P]), ps("small", [P, 512])
        blk_ps = ps("blk_ps", [1, 2, 512])
        cnt, tot, incl, one = sb("cnt", [NB, NS, P]), sb("tot", [NB, P]), sb("incl", [NB, P]), sb("one", [NB, P])
        tiles_i, tiles, start = sb("tiles_i", [NB, 2], I32), sb("tiles", [NB, 1]), sb("start", [NB, 2])
        deg, past, blk_f = sb("deg", [NB, P]), sb("past", [NB, NT]), sb("blk_f", [1, NT])
        root = sb("root", [P, NB])
        hot_d = [sem("hot_d0"), sem("hot_d1")]
        hot_s = [sem("hot_s0"), sem("hot_s1")]
        used_d = [sem("used_d0"), sem("used_d1")]
        used_s = [sem("used_s0"), sem("used_s1")]
        counted, step, mm, root_s = sem("counted"), sem("step"), sem("mm"), sem("root_s")
        block = ctx.enter_context(nc.Block())

        def column(t, s):
            return t[:, :].rearrange("p (j s) -> p j s", j=NS)[:, :, bass.ds(s, 1)]

        def one_hots(eng, lo, hi, lo_f, hi_f, s, h):
            eng.tensor_tensor(lo[:, h], column(lo_f, s).to_broadcast([EP, NS, P]),
                              m.iota_row[0:EP, None, :].to_broadcast([EP, NS, P]), ALU.is_equal)
            return eng.tensor_tensor(hi[:, h], column(hi_f, s).to_broadcast([EP, NS, NB]),
                                     m.iota_row[0:EP, None, 0:NB].to_broadcast([EP, NS, NB]), ALU.is_equal)

        @block.vector
        def _(dve):
            nc.vector.memset(one[:, :], 1.0).then_inc(step, 1)
            with dve.Fori(0, SC // 2) as i:
                for h in range(2):
                    dve.wait_ge(used_d[h], i + 1)
                    one_hots(nc.vector, hot_lo, hot_hi, m.lo_f, m.hi_f, 2 * i + h, h).then_inc(hot_d[h], 1)
                    dve.wait_ge(used_s[h], i + 1)
                    one_hots(nc.vector, hot_slo, hot_shi, m.src_lo_f, m.src_hi_f, 2 * i + h, h).then_inc(hot_s[h], 1)
            dve.wait_ge(counted, 1)
            nc.vector.tensor_copy(cnt[:, :, :], by_dst[:, :].rearrange("p (j l) -> p j l", j=NS)).then_inc(step, 1)
            dve.wait_ge(step, 2)
            nc.vector.tensor_reduce(tot[:, :], cnt[:, :, :].rearrange("p j l -> p l j"), AX.X, ALU.add).then_inc(step, 1)
            dve.wait_ge(step, 3)
            nc.vector.tensor_tensor_scan(incl[:, :], one[:, :], tot[:, :], 0.0, ALU.mult, ALU.add).then_inc(step, 1)
            nc.vector.tensor_tensor(deg[:, :], tot[:, :], by_src[:, :], ALU.add).then_inc(step, 1)
            dve.wait_ge(step, 5)
            nc.vector.tensor_scalar(tiles_i[:, 0:1], incl[:, P - 1:P], float(P - 1), None, ALU.add).then_inc(step, 1)
            dve.wait_ge(step, 6)
            nc.vector.tensor_single_scalar(tiles_i[:, 1:2], tiles_i[:, 0:1], 7, ALU.logical_shift_right).then_inc(step, 1)
            dve.wait_ge(step, 7)
            nc.vector.tensor_copy(tiles[:, :], tiles_i[:, 1:2]).then_inc(step, 1)
            dve.wait_ge(mm, 1)
            nc.vector.tensor_copy(start[:, 0:1], small[0:NB, 0:1]).then_inc(step, 1)
            nc.vector.tensor_tensor(incl[:, :], incl[:, :], tot[:, :], ALU.subtract).then_inc(step, 1)
            dve.wait_ge(step, 10)
            nc.vector.tensor_tensor(start[:, 1:2], start[:, 0:1], tiles[:, :], ALU.add).then_inc(step, 1)
            nc.vector.scalar_tensor_tensor(m.first[:, 0, :], start[:, 0:1].to_broadcast([NB, P]), float(P), incl[:, :],
                                           ALU.mult, ALU.add).then_inc(step, 1)
            for j in range(1, NS):
                dve.wait_ge(step, 11 + j)
                nc.vector.tensor_tensor(m.first[:, j, :], m.first[:, j - 1, :], cnt[:, j - 1, :], ALU.add).then_inc(step, 1)
            nc.vector.tensor_scalar(past[:, :], m.iota_tiles[0:NB, :], start[:, 1:2], None, ALU.is_ge).then_inc(step, 1)
            dve.wait_ge(mm, 2)
            h = NT // 2
            nc.vector.tensor_scalar(blk_f[:, :].rearrange("o (a t) -> o a t", a=2), blk_ps[:, :, 0:h], float(NB - 1), None,
                                    ALU.min).then_inc(step, 1)
            dve.wait_ge(step, 17)
            nc.vector.tensor_copy(m.blk[:, :], blk_f[:, :]).then_inc(step, 1)
            nc.vector.tensor_scalar(root[:, :], small[:, 64:64 + NB], 1e-5, None, ALU.max).then_inc(step, 1)
            dve.wait_ge(root_s, 1)
            nc.vector.reciprocal(m.dis[:, :], m.dis[:, :]).then_inc(step, 1)

        @block.scalar
        def _(act):
            act.wait_ge(step, 19)
            nc.scalar.activation(m.dis[:, :], root[:, :], ACT.Sqrt).then_inc(root_s, 1)

        @block.tensor
        def _(pe):
            for ap in (by_dst[:, :], by_src[:, :]):
                nc.tensor.matmul(ap, m.zero_row[0:1, 0:NB], m.zero_row[0:1, 0:ap.shape[1]], start=True, stop=True,
                                 skip_group_check=True)
            for h in range(2):
                pe.sem_inc(used_d[h], 1)
                pe.sem_inc(used_s[h], 1)
            with pe.Fori(0, SC // 2) as i:
                for h in range(2):
                    pe.wait_ge(hot_d[h], i + 1)
                    for j in range(NS):
                        last = nc.tensor.matmul(by_dst[:, j * P:(j + 1) * P], hot_hi[:, h, j, :], hot_lo[:, h, j, :],
                                                start=False, stop=True, skip_group_check=True)
                    last.then_inc(used_d[h], 1)
                    pe.wait_ge(hot_s[h], i + 1)
                    for j in range(NS):
                        last = nc.tensor.matmul(by_src[:, :], hot_shi[:, h, j, :], hot_slo[:, h, j, :],
                                                start=False, stop=True, skip_group_check=True)
                    last.then_inc(used_s[h], 1)
            for h in range(2):
                pe.wait_ge(used_d[h], SC // 2 + 1)
                pe.wait_ge(used_s[h], SC // 2 + 1)
            pe.sem_inc(counted, 1)
            pe.wait_ge(step, 8)
            nc.tensor.matmul(small[0:NB, 0:1], m.above[0:NB, 0:NB], tiles[:, :], start=True, stop=True)
            nc.tensor.matmul(small[:, 64:64 + NB], deg[:, :], m.ident[0:NB, 0:NB], start=True, stop=True).then_inc(mm, 1)
            pe.wait_ge(step, 16)
            h = NT // 2
            for k in range(2):
                last = nc.tensor.matmul(blk_ps[:, k, 0:h], one[:, 0:1], past[:, k * h:(k + 1) * h], start=True, stop=True)
            last.then_inc(mm, 1)


def rank_and_scatter(nc, m):
    with ExitStack() as ctx:
        sb, ps, sem = makers(nc, ctx, "rank")
        pair = lambda n: [sem(n + "0"), sem(n + "1")]
        key_row, hi_row = sb("key_row", [EP, 2, NS, EP]), sb("hi_row", [NB, 2, NS, EP])
        hot_lo, hot_hi = sb("hot_lo", [EP, 2, NS, P], BF16), sb("hot_hi", [EP, 2, NS, NB], BF16)
        hot_hi_t = sb("hot_hi_t", [NB, 2, NS, EP])
        next_sb, next_ps = sb("next_sb", [NB, 2, NS * P]), ps("next_ps", [NB, NS * P])
        found = [ps("found0", [EP, NS, P]), ps("found1", [EP, NS, P])]
        picked, same = sb("picked", [EP, NS, P]), sb("same", [EP, NS, EP])
        base, local, pos = sb("base", [EP, NS]), sb("local", [EP, NS]), sb("pos", [EP, 4, NS], I32)
        row_i = sb("row_i", [EP, 2, NS], I32)
        staged = sb("staged", [EP, 2, NS, REC])
        row_in, row_used = pair("row_in"), pair("row_used")
        hots, looked, counted = pair("hots"), pair("looked"), pair("counted")
        state, at_row, rec_in, sent = pair("state"), pair("at_row"), pair("rec_in"), pair("sent")
        chain, seeded, loads = sem("chain"), sem("seeded"), sem("loads")
        edges = m.slots_sb[0:EP, 0:EC * REC].rearrange("p (j s k) -> p j s k", j=NS, k=REC)
        key_rows = m.key_rows.rearrange("(j s) p -> s j p", j=NS)
        hi_rows = m.hi_rows.rearrange("(j s) p -> s j p", j=NS)
        turns = SC // 2
        block = ctx.enter_context(nc.Block())

        def column(t, s):
            return t[:, :].rearrange("p (j s) -> p j s", j=NS)[:, :, bass.ds(s, 1)]

        @block.sync
        def _(sp):
            with sp.Fori(0, turns) as i:
                for h in range(2):
                    sp.wait_ge(row_used[h], i + 1)
                    sp.dma_start(key_row[:, h], key_rows[bass.ds(2 * i + h, 1)].to_broadcast([EP, NS, EP])).then_inc(row_in[h], 16)
                    sp.dma_start(hi_row[:, h], hi_rows[bass.ds(2 * i + h, 1)].to_broadcast([NB, NS, EP])).then_inc(row_in[h], 16)

        @block.vector
        def _(dve):
            for h in range(2):
                dve.sem_inc(row_used[h], 1)
            with dve.Fori(0, turns) as i:
                for h in range(2):
                    s = 2 * i + h
                    dve.wait_ge(counted[h], i + 1)
                    nc.vector.tensor_tensor(hot_lo[:, h], column(m.lo_f, s).to_broadcast([EP, NS, P]),
                                            m.iota_row[0:EP, None, :].to_broadcast([EP, NS, P]), ALU.is_equal)
                    nc.vector.tensor_tensor(hot_hi[:, h], column(m.hi_f, s).to_broadcast([EP, NS, NB]),
                                            m.iota_row[0:EP, None, 0:NB].to_broadcast([EP, NS, NB]), ALU.is_equal)
                    dve.wait_ge(row_in[h], (i + 1) * 32)
                    nc.vector.tensor_scalar(hot_hi_t[:, h], hi_row[:, h], m.iota_col[0:NB, 0:1], None,
                                            ALU.is_equal).then_inc(hots[h], 1)
                    nc.vector.tensor_tensor(same[:, :, :], key_row[:, h], column(m.key_f, s).to_broadcast([EP, NS, EP]),
                                            ALU.is_equal).then_inc(row_used[h], 1)
                    dve.wait_ge(row_used[h], i + 2)
                    nc.vector.tensor_tensor(same[:, :, :], same[:, :, :], m.below[0:EP, None, 0:EP].to_broadcast([EP, NS, EP]),
                                            ALU.mult).then_inc(chain, 1)
                    dve.wait_ge(chain, 6 * s + 1)
                    nc.vector.tensor_reduce(local[:, :], same[:, :, :], AX.X, ALU.add).then_inc(chain, 1)
                    dve.wait_ge(looked[h], i + 1)
                    nc.vector.tensor_tensor(picked[:, :, :], found[h][:, :, :], hot_lo[:, h], ALU.mult).then_inc(chain, 1)
                    dve.wait_ge(chain, 6 * s + 3)
                    nc.vector.tensor_reduce(base[:, :], picked[:, :, :], AX.X, ALU.add).then_inc(chain, 1)
                    dve.wait_ge(chain, 6 * s + 4)
                    nc.vector.tensor_tensor(pos[:, 0, :], base[:, :], local[:, :], ALU.add).then_inc(chain, 1)
                    dve.wait_ge(chain, 6 * s + 5)
                    nc.vector.tensor_single_scalar(pos[:, 1, :], pos[:, 0, :], 7, ALU.logical_shift_right)
                    nc.vector.tensor_single_scalar(pos[:, 2, :], pos[:, 0, :], P - 1, ALU.bitwise_and).then_inc(chain, 1)
                    dve.wait_ge(chain, 6 * s + 6)
                    dve.wait_ge(sent[h], i * 64 + 16)
                    nc.vector.scalar_tensor_tensor(row_i[:, h], pos[:, 2, :], float(NT), pos[:, 1, :], ALU.mult,
                                                   ALU.add).then_inc(at_row[h], 1)

        @block.scalar
        def _(act):
            act.wait_ge(seeded, 1)
            with act.Fori(0, turns) as i:
                for h in range(2):
                    s = 2 * i + h
                    act.wait_ge(counted[1 - h], i + 1 + h)
                    nc.scalar.copy(next_sb[:, h], next_ps[:, :]).then_inc(state[h], 1)
                    act.wait_ge(sent[h], i * 64 + 16)
                    nc.scalar.copy(staged[:, h], edges[:, :, bass.ds(s, 1), :].rearrange("p j o k -> p j (o k)")).then_inc(rec_in[h], 1)

        @block.tensor
        def _(pe):
            nc.tensor.matmul(next_ps[:, :], m.ident[0:NB, 0:NB], m.first[:, :, :].rearrange("p j l -> p (j l)"),
                             start=True, stop=True, skip_group_check=True).then_inc(seeded, 1)
            for h in range(2):
                pe.sem_inc(counted[h], 1)
            with pe.Fori(0, turns) as i:
                for h in range(2):
                    pe.wait_ge(hots[h], i + 1)
                    pe.wait_ge(state[h], i + 1)
                    for j in range(NS):
                        last = nc.tensor.matmul(found[h][:, j, :], hot_hi_t[:, h, j, :], next_sb[:, h, j * P:(j + 1) * P],
                                                start=True, stop=True, skip_group_check=True)
                    last.then_inc(looked[h], 1)
                    for j in range(NS):
                        last = nc.tensor.matmul(next_ps[:, j * P:(j + 1) * P], hot_hi[:, h, j, :], hot_lo[:, h, j, :],
                                                start=False, stop=True, skip_group_check=True)
                    last.then_inc(counted[h], 1)

        @block.gpsimd
        def _(pool):
            for h in range(2):
                pool.dma_start(m.spare[h:h + 1, :], m.zero_row[0:1, 0:D]).then_inc(sent[h], 16)
            with pool.Fori(0, turns) as i:
                for h in range(2):
                    pool.wait_ge(rec_in[h], i + 1)
                    pool.sem_inc(m.pool_passed, 1)
                    pool.wait_ge(at_row[h], i + 1)
                    pool.sem_inc(m.pool_passed, 1)
                    for j in range(NS):
                        pool.indirect_dma_start(m.slots, bass.IndirectOffsetOnAxis(ap=row_i[:, h, j:j + 1], axis=0),
                                                staged[:, h, j, :], None).then_inc(sent[h], 16)
            for h in range(2):
                pool.wait_ge(sent[h], turns * 64 + 16)


def weights(nc, a, m):
    with ExitStack() as ctx:
        sb, ps, sem = makers(nc, ctx, "wts")
        zeroed, loaded = sem("zeroed"), sem("loaded")
        block = ctx.enter_context(nc.Block())

        @block.vector
        def _(dve):
            for t in (m.gru_i, m.gru_h, *m.pair_w, m.mlp2):
                nc.vector.memset(t[tuple(slice(None) for _ in t.shape)], 0.0).then_inc(zeroed, 1)
            nc.vector.memset(m.x[:, NB - 1, :], 0.0).then_inc(zeroed, 1)

        @block.sync
        def _(sp):
            sp.wait_ge(zeroed, 7)
            n = 0

            def load(dst, src):
                nonlocal n
                n += 1
                sp.dma_start(dst, src).then_inc(loaded, 16)

            with nc.allow_non_contiguous_dma(reason="small weights, turned while they load"):
                load(m.x[:, 0:NB - 1, :], a["x"][0:(NB - 1) * P, :].rearrange("(b q) d -> q b d", q=P))
                load(m.x[0:TAIL, NB - 1, :], a["x"][(NB - 1) * P:N, :])
                for t in range(8):
                    load(m.emb[:, t * D:(t + 1) * D], a["L0_gnn_edge_emb"][t].rearrange("(m h) -> h m", h=D))
                for dst, w, b, halves in ((m.gru_i, "L0_gnn_w_ih", "L0_gnn_b_ih", ((0, 3 * D, 0),)),
                                          (m.gru_h, "L0_gnn_w_hh", "L0_gnn_b_hh", ((0, 2 * D, 0), (2 * D, 3 * D, 3 * D)))):
                    for lo, hi, at in halves:
                        load(dst[0:D, at:at + hi - lo], a[w][lo:hi, :].rearrange("g k -> k g"))
                        load(dst[D:D + 1, at:at + hi - lo], a[b][None, lo:hi])
                for (i0, ni), t in zip(GROUPS, m.pair_w):
                    for il in range(ni):
                        c = slice((i0 + il) * D, (i0 + il + 1) * D)
                        for k, (w, b) in enumerate((("L1_gnn_W_msg", "L1_gnn_b_msg"), ("L1_gnn_W_attn", "L1_gnn_b_attn"))):
                            r = il * (D + 1)
                            load(t[r:r + D, k, il * D:(il + 1) * D], a[w][:, c])
                            load(t[r + D:r + D + 1, k, il * D:(il + 1) * D], a[b][None, c])
                for k in range(4):
                    load(m.conv_w[k][:, :], a[f"L2_gnn_w{k}"])
                    load(m.conv_b[k][:, :], a[f"L2_gnn_b{k}"][:, None])
                w1, w2 = a["L3_gnn_W1"], a["L3_gnn_W2"]
                load(m.mlp1[:, 0:64], w1.rearrange("h k -> k h"))
                load(m.mlp1[0:D, 64:P], w1[:, D:2 * D].rearrange("h k -> k h"))
                load(m.mlp1[D:2 * D, 64:P], w1[:, 0:D].rearrange("h k -> k h"))
                for k in range(2):
                    load(m.mlp_b1[64 * k:64 * k + 64, :], a["L3_gnn_b1"][:, None])
                    load(m.mlp2[64 * k:64 * k + 64, k * D:(k + 1) * D], w2.rearrange("o h -> h o"))
                    load(m.mlp_b2[:, k * D:(k + 1) * D], a["L3_gnn_b2"][None, :].to_broadcast([P, D]))
            sp.wait_ge(loaded, 16 * n)


def segments(nc, m):
    g8 = NT // 8
    with ExitStack() as ctx:
        sb, ps, sem = makers(nc, ctx, "seg")
        turned, back = ps("turned", [g8, 8, P]), ps("back", [P, 8, P])
        rows, ends_t = sb("rows", [g8, 8, P]), sb("ends_t", [g8, 8, P])
        around = sb("around", [P, 3, NT])
        start, end, edge = sb("start", [P, NT]), sb("end", [P, NT]), sb("edge", [1, 2])
        in_s, turned_s, rows_s, out_s, edge_s = sem("in"), sem("turned_s"), sem("rows_s"), sem("out"), sem("edge_s")
        near, flags, saved, reread, back_s, step = sem("near"), sem("flags"), sem("saved"), sem("reread"), sem("back_s"), sem("step")
        slot = m.slots_sb[:, :].rearrange("q (t k) -> q t k", k=REC)
        block = ctx.enter_context(nc.Block())

        @block.sync
        def _(sp):
            sp.dma_start(m.slots_sb[:, :], m.slots.rearrange("(q t) k -> q (t k)", q=P)).then_inc(in_s, 16)
            sp.wait_ge(edge_s, 1)
            sp.dma_start(m.slot_keys[None, 0:1], edge[:, 0:1]).then_inc(out_s, 16)
            sp.dma_start(m.slot_keys[None, SLOTS + 1:SLOTS + 2], edge[:, 1:2]).then_inc(out_s, 16)
            sp.wait_ge(rows_s, 1)
            sp.dma_start(m.slot_keys[1:SLOTS + 1].rearrange("(g t q) -> t g q", g=8, q=P), rows[:, :, :]).then_inc(out_s, 16)
            sp.wait_ge(out_s, 48)
            for k in range(3):
                sp.dma_start(around[:, k, :], m.slot_keys[k:k + SLOTS].rearrange("(q c) -> q c", q=P)).then_inc(near, 16)
            sp.wait_ge(flags, 2)
            sp.dma_start(m.far_row.rearrange("(q c) -> q c", q=P), start[:, :]).then_inc(saved, 16)
            sp.dma_start(m.end_row.rearrange("(q c) -> q c", q=P), end[:, :]).then_inc(saved, 16)
            sp.wait_ge(saved, 32)
            sp.dma_start(ends_t[:, :, :], m.end_row.rearrange("(g t q) -> t g q", g=8, q=P)).then_inc(reread, 16)

        @block.tensor
        def _(pe):
            pe.wait_ge(in_s, 16)
            for g in range(8):
                last = nc.tensor.transpose(turned[:, g, :], slot[:, g * g8:(g + 1) * g8, KEY], m.ident[:, :])
            last.then_inc(turned_s, 1)
            pe.wait_ge(reread, 16)
            for g in range(8):
                last = nc.tensor.transpose(back[:, g, 0:g8], ends_t[:, g, :], m.ident[0:g8, 0:g8])
            last.then_inc(back_s, 1)

        @block.vector
        def _(dve):
            nc.vector.memset(edge[:, :], -5.0).then_inc(edge_s, 1)
            dve.wait_ge(turned_s, 1)
            nc.vector.tensor_copy(rows[:, :, :], turned[:, :, :]).then_inc(rows_s, 1)
            dve.wait_ge(near, 48)
            nc.vector.tensor_tensor(start[:, :], around[:, 1, :], around[:, 0, :], ALU.not_equal).then_inc(step, 1)
            nc.vector.tensor_tensor(end[:, :], around[:, 1, :], around[:, 2, :], ALU.not_equal).then_inc(flags, 1)
            dve.wait_ge(step, 1)
            nc.vector.tensor_scalar(start[:, :], start[:, :], FAR, None, ALU.mult).then_inc(flags, 1)
            dve.wait_ge(back_s, 1)
            loe = slot[:, :, LOE].rearrange("q (g t) -> q g t", g=8)
            low = slot[:, :, LO].rearrange("q (g t) -> q g t", g=8)
            nc.vector.scalar_tensor_tensor(loe, low, 1.0, back[:, :, 0:g8], ALU.add, ALU.mult).then_inc(step, 1)
            dve.wait_ge(step, 2)
            nc.vector.tensor_scalar(loe, loe, -1.0, None, ALU.add).then_inc(step, 1)


def normalise(nc, m, stage):
    with ExitStack() as ctx:
        sb, ps, sem = makers(nc, ctx, stage)
        mean, var, sq, eps = sb("mean", [P, NB]), sb("var", [P, NB]), sb("sq", [P, NB, D]), sb("eps", [P, 1])
        step, var_s, root_s = sem("step"), sem("var_s"), sem("root_s")
        block = ctx.enter_context(nc.Block())
        wide = [P, NB, D]

        @block.vector
        def _(dve):
            nc.vector.memset(eps[:, :], 1e-5).then_inc(var_s, 1)
            nc.vector.tensor_reduce(mean[:, :], m.x[:, :, :], AX.X, ALU.add).then_inc(step, 1)
            dve.wait_ge(step, 1)
            nc.vector.tensor_scalar(mean[:, :], mean[:, :], 1.0 / D, None, ALU.mult).then_inc(step, 1)
            dve.wait_ge(step, 2)
            nc.vector.tensor_tensor(m.h[:, :, :], m.x[:, :, :], mean[:, :, None].to_broadcast(wide), ALU.subtract).then_inc(step, 1)
            dve.wait_ge(step, 3)
            nc.vector.tensor_tensor(sq[:, :, :], m.h[:, :, :], m.h[:, :, :], ALU.mult).then_inc(step, 1)
            dve.wait_ge(step, 4)
            nc.vector.tensor_reduce(var[:, :], sq[:, :, :], AX.X, ALU.add).then_inc(var_s, 1)
            dve.wait_ge(root_s, 1)
            nc.vector.reciprocal(var[:, :], var[:, :]).then_inc(step, 1)
            dve.wait_ge(step, 5)
            nc.vector.tensor_tensor(m.h[:, :, :], m.h[:, :, :], var[:, :, None].to_broadcast(wide), ALU.mult).then_inc(step, 1)
            dve.wait_ge(step, 6)
            nc.vector.tensor_scalar(m.h[:, :, :], m.h[:, :, :], 0.0, None, ALU.max).then_inc(step, 1)

        @block.scalar
        def _(act):
            act.wait_ge(var_s, 2)
            nc.scalar.activation(var[:, :], var[:, :], ACT.Sqrt, bias=eps[:, 0:1], scale=1.0 / D).then_inc(root_s, 1)


def type_table(nc, m):
    with ExitStack() as ctx:
        sb, ps, sem = makers(nc, ctx, "typ")
        turned = ps("turned", [D, NP])
        turned_s, rows_s, one = sem("turned_s"), sem("rows_s"), sem("one")
        block = ctx.enter_context(nc.Block())

        @block.tensor
        def _(pe):
            for b in range(NB):
                last = nc.tensor.transpose(turned[:, b * P:(b + 1) * P], m.h[:, b, :], m.ident[:, :])
            last.then_inc(turned_s, 1)

        @block.scalar
        def _(act):
            act.wait_ge(one, 1)
            act.wait_ge(turned_s, 1)
            nc.scalar.copy(m.ht[0:D, :], turned[:, :]).then_inc(rows_s, 1)

        @block.vector
        def _(dve):
            nc.vector.memset(m.ht[:, :], 1.0).then_inc(one, 1)
    with ExitStack() as ctx:
        sb, ps, sem = makers(nc, ctx, "tab")
        table, prod = ps("table", [P, NP]), sb("prod", [P, NP])
        made, out_s, saved = sem("made"), sem("out_s"), sem("saved")
        block = ctx.enter_context(nc.Block())

        @block.tensor
        def _(pe):
            for b in range(NB):
                last = nc.tensor.matmul(table[:, b * P:(b + 1) * P], m.ht[0:D, b * P:(b + 1) * P], m.emb[:, :], start=True,
                                        stop=True, skip_group_check=True)
            last.then_inc(made, 1)

        @block.scalar
        def _(act):
            act.wait_ge(made, 1)
            nc.scalar.copy(prod[:, :], table[:, :]).then_inc(out_s, 1)

        @block.sync
        def _(sp):
            sp.wait_ge(out_s, 1)
            sp.dma_start(m.typed.rearrange("(b q t) d -> q b (t d)", q=P, t=8),
                         prod[:, :].rearrange("q (b c) -> q b c", b=NB)).then_inc(saved, 16)
            sp.wait_ge(saved, 16)


def slot_field(m, t0, n, k):
    return m.slots_sb[:, :].rearrange("q (t k) -> q t k", k=REC)[:, bass.ds(t0, n), k]


def block_of(m, eng, t):
    return eng.value_load(m.blk[0:1, bass.ds(t, 1)], min_val=0, max_val=NB - 1)


def clear(nc, m, ap):
    rows, cols = ap.shape
    for c in range(0, cols, 512):
        w = min(512, cols - c)
        last = nc.tensor.matmul(ap[:, c:c + w], m.zero_row[0:1, 0:rows], m.zero_row[0:1, 0:w], start=True, stop=True,
                                skip_group_check=True)
    return last


def aggregate_typed(nc, m):
    with ExitStack() as ctx:
        sb, ps, sem = makers(nc, ctx, "at")
        pair = lambda n: [sem(n + "0"), sem(n + "1")]
        idx, hot = sb("idx", [P, 2, TB], I32), sb("hot", [P, 2, TB, P])
        ring, extra = sb("ring", [P, 2, TB, D]), sb("extra", [P, 2, TB, 2])
        sums = ps("sums", [P, 512])
        idx_s, hot_s, gathered, used = pair("idx_s"), pair("hot_s"), pair("gathered"), pair("used")
        done = sem("done")
        block = ctx.enter_context(nc.Block())

        @block.vector
        def _(dve):
            with dve.Fori(0, IT) as i:
                for h in range(2):
                    t0 = (2 * i + h) * TB
                    dve.wait_ge(used[h], i + 1)
                    nc.vector.tensor_copy(idx[:, h, :], slot_field(m, t0, TB, TIX)).then_inc(idx_s[h], 1)
                    nc.vector.tensor_copy(extra[:, h, :, 0], slot_field(m, t0, TB, WGT))
                    nc.vector.tensor_tensor(hot[:, h], slot_field(m, t0, TB, LO)[:, :, None].to_broadcast([P, TB, P]),
                                            m.iota_row[:, None, :].to_broadcast([P, TB, P]), ALU.is_equal).then_inc(hot_s[h], 1)
            for h in range(2):
                dve.wait_ge(used[h], IT + 1)
            nc.vector.tensor_copy(m.sums[:, :, :], sums[:, 0:NB * 20].rearrange("q (b c) -> q b c", b=NB)).then_inc(done, 1)

        @block.gpsimd
        def _(pool):
            with pool.Fori(0, IT) as i:
                for h in range(2):
                    pool.wait_ge(idx_s[h], i + 1)
                    pool.sem_inc(m.pool_passed, 1)
                    for j in range(TB):
                        pool.indirect_dma_start(ring[:, h, j, :], None, m.typed,
                                                bass.IndirectOffsetOnAxis(ap=idx[:, h, j:j + 1], axis=0)).then_inc(gathered[h], 16)

        @block.tensor
        def _(pe):
            clear(nc, m, sums[:, :])
            for h in range(2):
                pe.sem_inc(used[h], 1)
            with pe.Fori(0, IT) as i:
                for h in range(2):
                    t0 = (2 * i + h) * TB
                    pe.wait_ge(hot_s[h], i + 1)
                    pe.wait_ge(gathered[h], (i + 1) * 16 * TB)
                    for j in range(TB):
                        b = block_of(m, pe, t0 + j)
                        nc.tensor.matmul(sums[:, bass.ds(b * 20, D)], hot[:, h, j, :], ring[:, h, j, :], start=False, stop=True,
                                         skip_group_check=True)
                        last = nc.tensor.matmul(sums[:, bass.ds(b * 20 + D, 1)], hot[:, h, j, :], extra[:, h, j, 0:1], start=False,
                                                stop=True, skip_group_check=True)
                    last.then_inc(used[h], 1)


def gru(nc, m):
    with ExitStack() as ctx:
        sb, ps, sem = makers(nc, ctx, "gru")
        turned = ps("turned", [D, NP])
        mt = m.mt
        turned_s, one = sem("turned_s"), sem("one")
        block = ctx.enter_context(nc.Block())

        @block.tensor
        def _(pe):
            for b in range(NB):
                last = nc.tensor.transpose(turned[:, b * P:(b + 1) * P], m.sums[:, b, 0:D], m.ident[:, :])
            last.then_inc(turned_s, 1)

        @block.vector
        def _(dve):
            nc.vector.memset(mt[:, :], 1.0).then_inc(one, 1)
            dve.wait_ge(one, 1)
            dve.wait_ge(turned_s, 1)
            nc.vector.tensor_copy(mt[0:D, :], turned[:, :]).then_inc(one, 1)
    with ExitStack() as ctx:
        sb, ps, sem = makers(nc, ctx, "gat")
        gates = ps("gates", [P, 4, 8, 4 * D])
        rz, hn, tmp = sb("rz", [P, NB, 2 * D]), sb("hn", [P, NB, D]), sb("tmp", [P, NB, D])
        pos, safe = sb("pos", [P, NB]), sb("safe", [P, NB])
        made, act_s, step = sem("made"), sem("act_s"), sem("step")
        block = ctx.enter_context(nc.Block())
        gv = gates[:, :, :, :].rearrange("q a b c -> q (a b) c")[:, 0:NB, :]

        @block.tensor
        def _(pe):
            for b in range(NB):
                o = gates[:, b // 8, b % 8, :]
                nc.tensor.matmul(o, mt_block(m.mt, b), m.gru_i[:, :], start=b % 8 == 0, stop=False, skip_group_check=True)
                last = nc.tensor.matmul(o, mt_block(m.ht, b), m.gru_h[:, :], start=False, stop=True, skip_group_check=True)
            last.then_inc(made, 1)

        @block.scalar
        def _(act):
            act.wait_ge(made, 1)
            nc.scalar.activation(rz[:, :, :], gv[:, :, 0:2 * D], ACT.Sigmoid).then_inc(act_s, 1)
            act.wait_ge(step, 2)
            nc.scalar.activation(hn[:, :, :], hn[:, :, :], ACT.Tanh).then_inc(act_s, 1)
            act.wait_ge(step, 8)
            nc.scalar.activation(safe[:, :], safe[:, :], ACT.Sqrt).then_inc(act_s, 1)

        @block.vector
        def _(dve):
            dve.wait_ge(act_s, 1)
            nc.vector.tensor_tensor(hn[:, :, :], rz[:, :, 0:D], gv[:, :, 3 * D:4 * D], ALU.mult).then_inc(step, 1)
            dve.wait_ge(step, 1)
            nc.vector.tensor_tensor(hn[:, :, :], hn[:, :, :], gv[:, :, 2 * D:3 * D], ALU.add).then_inc(step, 1)
            dve.wait_ge(act_s, 2)
            nc.vector.tensor_tensor(tmp[:, :, :], m.h[:, :, :], hn[:, :, :], ALU.subtract).then_inc(step, 1)
            nc.vector.tensor_tensor(m.x[:, :, :], m.x[:, :, :], hn[:, :, :], ALU.add).then_inc(step, 1)
            nc.vector.tensor_scalar(safe[:, :], m.sums[:, :, D], 2.0, None, ALU.add).then_inc(step, 1)
            dve.wait_ge(step, 5)
            nc.vector.tensor_scalar(pos[:, :], safe[:, :], 0.0, None, ALU.is_gt).then_inc(step, 1)
            dve.wait_ge(step, 6)
            nc.vector.scalar_tensor_tensor(safe[:, :], safe[:, :], -1.0, pos[:, :], ALU.add, ALU.mult).then_inc(step, 1)
            dve.wait_ge(step, 7)
            nc.vector.tensor_scalar(safe[:, :], safe[:, :], 1.0, None, ALU.add).then_inc(step, 1)
            nc.vector.tensor_tensor(tmp[:, :, :], tmp[:, :, :], rz[:, :, D:2 * D], ALU.mult).then_inc(step, 1)
            dve.wait_ge(step, 9)
            nc.vector.tensor_tensor(m.x[:, :, :], m.x[:, :, :], tmp[:, :, :], ALU.add).then_inc(step, 1)
            dve.wait_ge(act_s, 3)
            nc.vector.reciprocal(safe[:, :], safe[:, :]).then_inc(step, 1)
            dve.wait_ge(step, 11)
            nc.vector.tensor_tensor(m.dinv[:, :], safe[:, :], pos[:, :], ALU.mult).then_inc(step, 1)


def mt_block(t, b):
    return t[:, b * P:(b + 1) * P]


def save_rows(nc, m, stage, pairs):
    with ExitStack() as ctx:
        sb, ps, sem = makers(nc, ctx, stage)
        saved = sem("saved")
        block = ctx.enter_context(nc.Block())

        @block.sync
        def _(sp):
            for table, rows in pairs:
                sp.dma_start(table.rearrange("(b q) d -> q b d", q=P), rows).then_inc(saved, 16)
            sp.wait_ge(saved, 16 * len(pairs))


HB = 4
HT = NT // HB


def batches(eng, total, first, last, body):
    assert (total - first - last) % 2 == 0 and first % 2 == 1
    for n in range(first):
        body(n // 2, n % 2)
    with eng.Fori(0, (total - first - last) // 2) as i:
        body(i + first // 2, 1)
        body(i + first // 2 + 1, 0)
    for n in range(total - last, total):
        body(n // 2, n % 2)


def inside(n, total=HT):
    return not isinstance(n, int) or 0 <= n < total


def wait(eng, sem, value):
    if not isinstance(value, int) or value > 0:
        eng.wait_ge(sem, value)


def records(m, t0, n, k0, k1):
    return m.slots_sb[:, :].rearrange("q (t k) -> q t k", k=REC)[:, bass.ds(t0, n), k0:k1]


def products(nc, m, ring, n, out):
    w = D + 1
    return nc.vector.tensor_tensor(out.rearrange("q t (i k) -> q t i k", k=w), ring[:, :, :, None].to_broadcast([P, HB, D, w]),
                                   records(m, n * HB, HB, 0, w)[:, :, None, :].to_broadcast([P, HB, D, w]), ALU.mult)


def one_hot(nc, m, field, n, out):
    return nc.vector.tensor_tensor(out, slot_field(m, n * HB, HB, field)[:, :, None].to_broadcast([P, HB, P]),
                                   m.iota_row[:, None, :].to_broadcast([P, HB, P]), ALU.is_equal)


def gather(nc, m, pool, table, idx, ring, idx_s, gathered, tiles, turns):
    with pool.Fori(0, turns) as i:
        for h in range(2):
            pool.wait_ge(idx_s, 2 * i + h + 1)
            pool.sem_inc(m.pool_passed, 1)
            for j in range(tiles):
                pool.indirect_dma_start(ring[:, h, j, :], None, table,
                                        bass.IndirectOffsetOnAxis(ap=idx[:, h, j:j + 1], axis=0)).then_inc(gathered[h], 16)


def segment_max(nc, m):
    with ExitStack() as ctx:
        sb, ps, sem = makers(nc, ctx, "mx")
        idx, ring = sb("idx", [P, 2, HB], I32), sb("ring", [P, 2, HB, D])
        prod, hot = sb("prod", [P, 2, HB, D * (D + 1)]), sb("hot", [P, 2, HB, P])
        prod_t, far = sb("prod_t", [102, 2, 3, 512]), sb("far", [P, 2, 512])
        run, run_e = sb("run", [96, 2, 3, 512]), sb("run_e", [P, 2, HB, 256])
        pt = [ps(f"pt{g}", [102, 512]) for g in range(3)]
        logit = [ps(f"logit{g}", [96, 512]) for g in range(3)]
        back, best = ps("back", [P, 2, 256]), ps("best", [P, 2, 256])
        gathered, far_in = [sem("gathered0"), sem("gathered1")], [sem("far_in0"), sem("far_in1")]
        idx_s, prod_s, pt_s, prod_t_s, logit_s = sem("idx_s"), sem("prod_s"), sem("pt_s"), sem("prod_t_s"), sem("logit_s")
        run_s, back_s, run_e_s, hot_s, best_s, kept = sem("run_s"), sem("back_s"), sem("run_e_s"), sem("hot_s"), sem("best_s"), sem("kept")
        cleared = sem("cleared")
        block = ctx.enter_context(nc.Block())

        @block.sync
        def _(sp):
            far_rows = m.far_row.rearrange("(c n) -> c n", n=512)

            def load(q, h):
                n = 2 * q + h
                wait(sp, run_s, n - 1)
                sp.dma_start(far[:, h], far_rows[bass.ds(n, 1)].to_broadcast([P, 512])).then_inc(far_in[h], 16)

            batches(sp, HT, 3, 1, load)

        @block.gpsimd
        def _(pool):
            gather(nc, m, pool, m.node16, idx, ring, idx_s, gathered, HB, HT // 2)

        @block.vector
        def _(dve):
            def indices(n, h):
                nc.vector.tensor_copy(idx[:, h, :], slot_field(m, n * HB, HB, SRC)).then_inc(idx_s, 1)

            def multiply(q, h):
                n = 2 * q + h
                dve.wait_ge(gathered[h], (q + 1) * 16 * HB)
                products(nc, m, ring[:, h], n, prod[:, h]).then_inc(prod_s, 1)
                if inside(n + 2):
                    dve.wait_ge(prod_s, n + 1)
                    indices(n + 2, h)

            def keep(n):
                for k in range(2):
                    dve.wait_ge(best_s, 2 * n + k + 1)
                    for j in range(2):
                        b = block_of(m, dve, n * HB + 2 * k + j)
                        row = m.top[:, bass.ds(b, 1), :].rearrange("q o c -> q (o c)")
                        wait(dve, kept, 4 * n + 2 * k + j)
                        nc.vector.tensor_tensor(row, row, best[:, j, :], ALU.subtract).then_inc(kept, 1)

            def turn(q, h):
                n = 2 * q + h
                dve.wait_ge(logit_s, n + 1)
                dve.wait_ge(far_in[h], (q + 1) * 16)
                wait(dve, run_s, n)
                for g, (_, ni) in enumerate(GROUPS):
                    r = 16 * ni
                    before = run[0:r, 1 - h, g, 511:512] if inside(n - 1) else 0.0
                    last = nc.vector.tensor_tensor_scan(run[0:r, h, g, :], far[0:r, h, :], logit[g][0:r, :], before, ALU.add, ALU.max)
                last.then_inc(run_s, 1)
                if inside(n + 2):
                    multiply(q + 1, h)
                one_hot(nc, m, LOE, n, hot[:, h]).then_inc(hot_s, 1)
                if inside(n - 1):
                    keep(n - 1)

            nc.vector.memset(m.top[:, :, :], 0.0).then_inc(cleared, 1)
            dve.wait_ge(cleared, 1)
            for h in range(2):
                indices(h, h)
            for h in range(2):
                multiply(0, h)
            batches(dve, HT, 1, 5, turn)
            keep(HT - 1)

        @block.scalar
        def _(act):
            def widen(n, h):
                act.wait_ge(pt_s, n + 1)
                for g, (_, ni) in enumerate(GROUPS):
                    last = nc.scalar.copy(prod_t[0:17 * ni, h, g, :], pt[g][0:17 * ni, :])
                last.then_inc(prod_t_s, 1)

            def turn(q, h):
                n = 2 * q + h
                if inside(n - 1):
                    for k in range(2):
                        act.wait_ge(back_s, 2 * (n - 1) + k + 1)
                        nc.scalar.copy(run_e[:, 1 - h, 2 * k:2 * k + 2, :], back[:, :, :]).then_inc(run_e_s, 1)
                if inside(n + 1):
                    widen(n + 1, 1 - h)

            widen(0, 0)
            batches(act, HT, 1, 1, turn)
            turn(HT // 2, 0)

        @block.tensor
        def _(pe):
            def turn_products(n, h):
                pe.wait_ge(prod_s, n + 1)
                wait(pe, prod_t_s, n)
                for g, (i0, ni) in enumerate(GROUPS):
                    for j in range(HB):
                        last = nc.tensor.transpose(pt[g][0:17 * ni, j * P:(j + 1) * P], prod[:, h, j, 17 * i0:17 * (i0 + ni)],
                                                   m.ident[:, :])
                last.then_inc(pt_s, 1)

            def turn_back(n, h, k):
                wait(pe, run_e_s, 2 * n + k)
                for j in range(2):
                    for g, (i0, ni) in enumerate(GROUPS):
                        last = nc.tensor.transpose(back[:, j, 16 * i0:16 * (i0 + ni)],
                                                   run[0:16 * ni, h, g, (2 * k + j) * P:(2 * k + j + 1) * P],
                                                   m.ident[0:16 * ni, 0:16 * ni])
                last.then_inc(back_s, 1)

            def select(n, h, k):
                pe.wait_ge(run_e_s, 2 * n + k + 1)
                wait(pe, kept, 4 * n + 2 * k)
                for j in range(2):
                    last = nc.tensor.matmul(best[:, j, :], hot[:, h, 2 * k + j, :], run_e[:, h, 2 * k + j, :], start=True,
                                            stop=True, skip_group_check=True)
                last.then_inc(best_s, 1)

            def turn(q, h):
                n = 2 * q + h
                if inside(n):
                    pe.wait_ge(prod_t_s, n + 1)
                    wait(pe, run_s, n)
                    for g, (_, ni) in enumerate(GROUPS):
                        last = nc.tensor.matmul(logit[g][0:16 * ni, :], m.pair_w[g][:, 1, :], prod_t[0:17 * ni, h, g, :],
                                                start=True, stop=True, skip_group_check=True)
                    last.then_inc(logit_s, 1)
                if inside(n - 1):
                    pe.wait_ge(run_s, n)
                    turn_back(n - 1, 1 - h, 0)
                    pe.wait_ge(hot_s, n)
                    turn_back(n - 1, 1 - h, 1)
                    select(n - 1, 1 - h, 0)
                    select(n - 1, 1 - h, 1)
                if inside(n + 1):
                    turn_products(n + 1, 1 - h)

            turn_products(0, 0)
            batches(pe, HT, 1, 1, turn)
            turn(HT // 2, 0)


def soft_sums(nc, m):
    with ExitStack() as ctx:
        sb, ps, sem = makers(nc, ctx, "sm")
        idx, ring = sb("idx", [P, 2, HB], I32), sb("ring", [P, 2, HB, D])
        prod, hot = sb("prod", [P, 2, HB, D * (D + 1)]), sb("hot", [P, 2, HB, P])
        prod_t, hot_t, both = sb("prod_t", [102, 3, 512]), sb("hot_t", [P, HB, P]), sb("both", [P, 2, 2, 256])
        pt = [ps(f"pt{g}", [102, 512]) for g in range(3)]
        ht_ps = ps("ht_ps", [P, HB, P])
        value = [ps("value0", [P, 2, 256]), ps("value1", [P, 2, 256])]
        part_sum = [ps("part0", [P, 512]), ps("part1", [P, 512])]
        gathered = [sem("gathered0"), sem("gathered1")]
        idx_s, prod_s, pt_s, prod_t_s, hot_s = sem("idx_s"), sem("prod_s"), sem("pt_s"), sem("prod_t_s"), sem("hot_s")
        value_s, exp_s, both_s, part_s, kept, cleared = sem("value_s"), sem("exp_s"), sem("both_s"), sem("part_s"), sem("kept"), sem("cleared")
        block = ctx.enter_context(nc.Block())

        @block.gpsimd
        def _(pool):
            gather(nc, m, pool, m.node16, idx, ring, idx_s, gathered, HB, HT // 2)

        @block.vector
        def _(dve):
            def indices(n, h):
                nc.vector.tensor_copy(idx[:, h, :], slot_field(m, n * HB, HB, SRC)).then_inc(idx_s, 1)

            def multiply(q, h):
                n = 2 * q + h
                dve.wait_ge(gathered[h], (q + 1) * 16 * HB)
                products(nc, m, ring[:, h], n, prod[:, h]).then_inc(prod_s, 1)
                one_hot(nc, m, LO, n, hot[:, h]).then_inc(hot_s, 1)
                if inside(n + 2):
                    dve.wait_ge(prod_s, n + 1)
                    indices(n + 2, h)

            def weigh(n, j):
                r = n * HB + j
                dve.wait_ge(exp_s, r + 1)
                nc.vector.tensor_tensor(both[:, j % 2, 1, :], value[j % 2][:, 0, :], both[:, j % 2, 0, :], ALU.mult).then_inc(both_s, 1)

            def add(n, j):
                r = n * HB + j
                b = block_of(m, dve, r)
                row = m.acc[:, bass.ds(b, 1), :].rearrange("q o c -> q (o c)")
                dve.wait_ge(part_s, r + 1)
                wait(dve, kept, r)
                nc.vector.tensor_tensor(row, row, part_sum[j % 2][:, :], ALU.add).then_inc(kept, 1)

            def turn(q, h):
                n = 2 * q + h
                weigh(n, 0)
                weigh(n, 1)
                add(n, 0)
                weigh(n, 2)
                add(n, 1)
                weigh(n, 3)
                add(n, 2)
                add(n, 3)
                if inside(n + 2):
                    multiply(q + 1, h)

            nc.vector.memset(m.acc[:, :, :], 0.0).then_inc(cleared, 1)
            dve.wait_ge(cleared, 1)
            for h in range(2):
                indices(h, h)
            for h in range(2):
                multiply(0, h)
            batches(dve, HT, 1, 5, turn)

        @block.scalar
        def _(act):
            def widen(n):
                act.wait_ge(pt_s, n + 1)
                for g, (_, ni) in enumerate(GROUPS):
                    nc.scalar.copy(prod_t[0:17 * ni, g, :], pt[g][0:17 * ni, :])
                nc.scalar.copy(hot_t[:, :, :], ht_ps[:, :, :]).then_inc(prod_t_s, 1)

            def turn(q, h):
                n = 2 * q + h
                for j in range(HB):
                    r = n * HB + j
                    act.wait_ge(value_s, r + 1)
                    wait(act, part_s, r - 1)
                    nc.scalar.activation(both[:, j % 2, 0, :], value[j % 2][:, 1, :], ACT.Exp).then_inc(exp_s, 1)
                if inside(n + 1):
                    widen(n + 1)

            widen(0)
            batches(act, HT, 1, 1, turn)

        @block.tensor
        def _(pe):
            def turn_products(n, h):
                pe.wait_ge(prod_s, n + 1)
                pe.wait_ge(hot_s, n + 1)
                wait(pe, prod_t_s, n)
                for g, (i0, ni) in enumerate(GROUPS):
                    for j in range(HB):
                        nc.tensor.transpose(pt[g][0:17 * ni, j * P:(j + 1) * P], prod[:, h, j, 17 * i0:17 * (i0 + ni)],
                                            m.ident[:, :])
                for j in range(HB):
                    last = nc.tensor.transpose(ht_ps[:, j, :], hot[:, h, j, :], m.ident[:, :])
                last.then_inc(pt_s, 1)

            def evaluate(n, j):
                r = n * HB + j
                b = block_of(m, pe, r)
                v = value[j % 2]
                wait(pe, both_s, r - 1)
                nc.tensor.matmul(v[:, 1, :], hot_t[:, j, :], m.top[:, bass.ds(b, 1), :].rearrange("q o c -> q (o c)"),
                                 start=True, stop=False, skip_group_check=True)
                for g, (i0, ni) in enumerate(GROUPS):
                    for k in range(2):
                        last = nc.tensor.matmul(v[:, k, 16 * i0:16 * (i0 + ni)], prod_t[0:17 * ni, g, j * P:(j + 1) * P],
                                                m.pair_w[g][:, k, :], start=False, stop=True, skip_group_check=True)
                last.then_inc(value_s, 1)

            def spread(n, h, j):
                r = n * HB + j
                pe.wait_ge(both_s, r + 1)
                wait(pe, kept, r - 1)
                nc.tensor.matmul(part_sum[j % 2][:, :], hot[:, h, j, :], both[:, j % 2, :, :].rearrange("q a c -> q (a c)"),
                                 start=True, stop=True, skip_group_check=True).then_inc(part_s, 1)

            def turn(q, h):
                n = 2 * q + h
                pe.wait_ge(prod_t_s, n + 1)
                evaluate(n, 0)
                evaluate(n, 1)
                spread(n, h, 0)
                evaluate(n, 2)
                spread(n, h, 1)
                evaluate(n, 3)
                spread(n, h, 2)
                if inside(n + 1):
                    turn_products(n + 1, 1 - h)
                spread(n, h, 3)

            turn_products(0, 0)
            batches(pe, HT, 1, 1, turn)


def attend(nc, m):
    with ExitStack() as ctx:
        sb, ps, sem = makers(nc, ctx, "att")
        none, total = sb("none", [P, NB, 256]), sb("total", [P, NB, D])
        step = sem("step")
        den, num = m.acc[:, :, 0:256], m.acc[:, :, 256:512]
        block = ctx.enter_context(nc.Block())

        @block.vector
        def _(dve):
            nc.vector.tensor_scalar(none[:, :, :], den, 0.0, None, ALU.is_equal).then_inc(step, 1)
            dve.wait_ge(step, 1)
            nc.vector.tensor_tensor(none[:, :, :], none[:, :, :], den, ALU.add).then_inc(step, 1)
            dve.wait_ge(step, 2)
            nc.vector.reciprocal(none[:, :, :], none[:, :, :]).then_inc(step, 1)
            dve.wait_ge(step, 3)
            nc.vector.tensor_tensor(none[:, :, :], none[:, :, :], num, ALU.mult).then_inc(step, 1)
            dve.wait_ge(step, 4)
            nc.vector.tensor_reduce(total[:, :, :], none[:, :, :].rearrange("q b (i o) -> q b o i", i=D), AX.X, ALU.add).then_inc(step, 1)
            dve.wait_ge(step, 5)
            nc.vector.tensor_tensor(m.x[:, :, :], m.x[:, :, :], total[:, :, :], ALU.add).then_inc(step, 1)


def convolve(nc, m, stage, table, width):
    with ExitStack() as ctx:
        sb, ps, sem = makers(nc, ctx, stage)
        idx, hot = sb("idx", [P, 2, TB], I32), sb("hot", [P, 2, TB, P])
        ring = sb("ring", [P, 2, TB, width])
        sums = ps("sums", [width, NP])
        gathered = [sem("gathered0"), sem("gathered1")]
        idx_s, step, hot_s, used, done = sem("idx_s"), sem("step"), sem("hot_s"), sem("used"), sem("done")
        block = ctx.enter_context(nc.Block())
        total = NT // TB

        @block.vector
        def _(dve):
            def turn(q, h):
                n = 2 * q + h
                wait(dve, used, n - 1)
                nc.vector.tensor_copy(idx[:, h, :], slot_field(m, n * TB, TB, SRC)).then_inc(idx_s, 1)
                nc.vector.tensor_tensor(hot[:, h], slot_field(m, n * TB, TB, LO)[:, :, None].to_broadcast([P, TB, P]),
                                        m.iota_row[:, None, :].to_broadcast([P, TB, P]), ALU.is_equal).then_inc(step, 1)
                dve.wait_ge(step, n + 1)
                nc.vector.tensor_tensor(hot[:, h], slot_field(m, n * TB, TB, WGT)[:, :, None].to_broadcast([P, TB, P]),
                                        hot[:, h], ALU.mult).then_inc(hot_s, 1)

            batches(dve, total, 3, 1, turn)
            dve.wait_ge(used, total)
            nc.vector.tensor_tensor(m.agg[0:width, :], sums[:, :], m.dinv_row[0:width, :], ALU.mult).then_inc(done, 1)

        @block.gpsimd
        def _(pool):
            gather(nc, m, pool, table, idx, ring, idx_s, gathered, TB, total // 2)

        @block.tensor
        def _(pe):
            for b in range(NB):
                nc.tensor.matmul(sums[:, b * P:(b + 1) * P], m.g[:, b, 0:width], m.twice[:, :], start=b % 4 == 0, stop=True,
                                 skip_group_check=True)
            with pe.Fori(0, total // 2) as i:
                for h in range(2):
                    n = 2 * i + h
                    pe.wait_ge(hot_s, n + 1)
                    pe.wait_ge(gathered[h], (i + 1) * 16 * TB)
                    for j in range(TB):
                        b = block_of(m, pe, n * TB + j)
                        last = nc.tensor.matmul(sums[:, bass.ds(b * P, P)], ring[:, h, j, :], hot[:, h, j, :], start=False,
                                                stop=True, skip_group_check=True)
                    last.then_inc(used, 1)


def dense(nc, m, stage, k):
    with ExitStack() as ctx:
        sb, ps, sem = makers(nc, ctx, stage)
        out = ps("out", [P, NP])
        made, done = sem("made"), sem("done")
        block = ctx.enter_context(nc.Block())

        @block.tensor
        def _(pe):
            for c in range(0, NP, 512):
                w = min(512, NP - c)
                last = nc.tensor.matmul(out[:, c:c + w], m.conv_w[k][:, :], m.agg[0:D, c:c + w], start=True, stop=True)
            last.then_inc(made, 1)

        @block.scalar
        def _(act):
            act.wait_ge(made, 1)
            nc.scalar.activation(m.hidden[:, :], out[:, :], ACT.Relu, bias=m.conv_b[k][:, 0:1]).then_inc(done, 1)


def project(nc, m, stage, k, table, width, activate):
    with ExitStack() as ctx:
        sb, ps, sem = makers(nc, ctx, stage)
        out = ps("out", [P, NB, width])
        made, scaled, saved, ready = sem("made"), sem("scaled"), sem("saved"), sem("ready")
        block = ctx.enter_context(nc.Block())

        @block.scalar
        def _(act):
            if activate:
                nc.scalar.activation(m.hidden[:, :], m.agg[:, :], ACT.Relu, bias=m.conv_b[k - 1][:, 0:1]).then_inc(ready, 1)

        @block.tensor
        def _(pe):
            if activate:
                pe.wait_ge(ready, 1)
            for b in range(NB):
                last = nc.tensor.matmul(out[:, b, :], m.hidden[:, b * P:(b + 1) * P], m.conv_w[k][:, :], start=True, stop=True,
                                        skip_group_check=True)
            last.then_inc(made, 1)

        @block.vector
        def _(dve):
            dve.wait_ge(made, 1)
            nc.vector.tensor_tensor(m.g[:, :, 0:width], out[:, :, :], m.dinv[:, :, None].to_broadcast([P, NB, width]),
                                    ALU.mult).then_inc(scaled, 1)

        @block.sync
        def _(sp):
            sp.wait_ge(scaled, 1)
            sp.dma_start(table.rearrange("(b q) d -> q b d", q=P), m.g[:, :, 0:width]).then_inc(saved, 16)
            sp.wait_ge(saved, 16)


def close_convolutions(nc, m):
    with ExitStack() as ctx:
        sb, ps, sem = makers(nc, ctx, "clo")
        out = ps("out", [P, 512])
        ready, made, done = sem("ready"), sem("made"), sem("done")
        block = ctx.enter_context(nc.Block())

        @block.scalar
        def _(act):
            nc.scalar.activation(m.hidden[0:D, :], m.agg[0:D, :], ACT.Identity, bias=m.conv_b[3][:, 0:1]).then_inc(ready, 1)

        @block.tensor
        def _(pe):
            pe.wait_ge(ready, 1)
            for b in range(NB):
                last = nc.tensor.transpose(out[:, b * D:(b + 1) * D], m.hidden[0:D, b * P:(b + 1) * P], m.ident[0:D, 0:D])
            last.then_inc(made, 1)

        @block.vector
        def _(dve):
            dve.wait_ge(made, 1)
            nc.vector.tensor_tensor(m.x[:, :, :], m.x[:, :, :], out[:, 0:NB * D].rearrange("q (b d) -> q b d", d=D),
                                    ALU.add).then_inc(done, 1)


def node_factors(nc, m):
    with ExitStack() as ctx:
        sb, ps, sem = makers(nc, ctx, "nf")
        saved, loaded, scaled = sem("saved"), sem("loaded"), sem("scaled")
        block = ctx.enter_context(nc.Block())

        @block.vector
        def _(dve):
            nc.vector.tensor_scalar(m.twice[:, :], m.ident[:, :], 2.0, None, ALU.mult).then_inc(scaled, 1)
            nc.vector.tensor_tensor(m.g[:, :, 0:D], m.h[:, :, :], m.dinv[:, :, None].to_broadcast([P, NB, D]), ALU.mult).then_inc(scaled, 1)

        @block.sync
        def _(sp):
            with nc.allow_non_contiguous_dma(reason="one factor to a node"):
                sp.dma_start(m.dinv_dram.rearrange("(b q) -> q b", q=P), m.dinv[:, :]).then_inc(saved, 16)
            sp.wait_ge(saved, 16)
            sp.dma_start(m.dinv_row[:, :], m.dinv_dram[None, :].to_broadcast([P, NP])).then_inc(loaded, 16)
            sp.wait_ge(scaled, 2)
            sp.dma_start(m.node16.rearrange("(b q) d -> q b d", q=P), m.g[:, :, 0:D]).then_inc(saved, 16)
            sp.wait_ge(saved, 32)
            sp.wait_ge(loaded, 16)


HW = D + 4


def sheaf_rows(nc, m):
    with ExitStack() as ctx:
        sb, ps, sem = makers(nc, ctx, "shr")
        filled, saved = sem("filled"), sem("saved")
        block = ctx.enter_context(nc.Block())

        @block.vector
        def _(dve):
            nc.vector.memset(m.wide[:, :, :], 0.0).then_inc(filled, 1)
            dve.wait_ge(filled, 1)
            nc.vector.tensor_copy(m.wide[:, :, 0:D], m.h[:, :, :]).then_inc(filled, 1)
            nc.vector.tensor_copy(m.wide[:, :, D], m.dis[:, :]).then_inc(filled, 1)

        @block.sync
        def _(sp):
            sp.wait_ge(filled, 3)
            sp.dma_start(m.node20.rearrange("(b q) d -> q b d", q=P), m.wide[:, :, :]).then_inc(saved, 16)
            sp.wait_ge(saved, 16)


def sheaf_messages(nc, m):
    with ExitStack() as ctx:
        sb, ps, sem = makers(nc, ctx, "sh")
        idx, ring = sb("idx", [P, 2, HB], I32), sb("ring", [P, 2, HB, HW])
        hot, hot_t = sb("hot", [P, 2, HB, P]), sb("hot_t", [P, HB, P])
        ends, ends_t, hid = sb("ends", [P, HB, 2, D]), sb("ends_t", [2 * D, HB, P]), sb("hid", [P, HB * P])
        vec, sq, swap = sb("vec", [P, HB, 2, D]), sb("sq", [P, HB, 2, D]), sb("swap", [P, HB, 2, D])
        norm, dot, coef, msg = sb("norm", [P, HB, 2]), sb("dot", [P, HB, 2]), sb("coef", [P, HB]), sb("msg", [P, HB, 2, D])
        rest = sb("rest", [P, HB, D])
        ht_ps, xd, et_ps, hid_ps = ps("ht_ps", [P, HB, P]), ps("xd", [P, HB, P]), ps("et_ps", [2 * D, HB, P]), ps("hid_ps", [P, HB * P])
        v_ps, sums = ps("v_ps", [P, HB, P]), ps("sums", [P, 512])
        gathered = [sem("gathered0"), sem("gathered1")]
        names = ("idx_s", "hot_s", "ht_s", "hot_t_s", "xd_s", "ends_s", "et_s", "ends_t_s", "hp_s", "hid_s", "v_s", "norm_s",
                 "root_s", "msg_s", "used", "chain", "part_s")
        idx_s, hot_s, ht_s, hot_t_s, xd_s, ends_s, et_s, ends_t_s, hp_s, hid_s, v_s, norm_s, root_s, msg_s, used, chain, part_s = map(sem, names)
        block = ctx.enter_context(nc.Block())
        STEPS = 17
        shape = [P, HB, 2, D]

        @block.gpsimd
        def _(pool):
            gather(nc, m, pool, m.node20, idx, ring, idx_s, gathered, HB, HT // 2)

        @block.vector
        def _(dve):
            def indices(n, h):
                nc.vector.tensor_copy(idx[:, h, :], slot_field(m, n * HB, HB, SRC)).then_inc(idx_s, 1)

            def turn(q, h):
                n = 2 * q + h
                c = [STEPS * n]

                def link(ins):
                    c[0] = c[0] + 1
                    ins.then_inc(chain, 1)
                    dve.wait_ge(chain, c[0])

                wait(dve, used, n)
                one_hot(nc, m, LO, n, hot[:, h]).then_inc(hot_s, 1)
                dve.wait_ge(gathered[h], (q + 1) * 16 * HB)
                dve.wait_ge(xd_s, n + 1)
                nc.vector.tensor_copy(ends[:, :, 0, :], ring[:, h, :, 0:D])
                nc.vector.tensor_copy(ends[:, :, 1, :], xd[:, :, 0:D]).then_inc(ends_s, 1)
                link(nc.vector.tensor_copy(coef[:, :], xd[:, :, D]))
                link(nc.vector.tensor_tensor(coef[:, :], ring[:, h, :, D], coef[:, :], ALU.mult))
                if inside(n + 2):
                    indices(n + 2, h)
                dve.wait_ge(v_s, n + 1)
                link(nc.vector.tensor_tensor(vec[:, :, :, :].rearrange("q t a d -> q t (a d)"), v_ps[:, :, 0:2 * D],
                                             m.mlp_b2[:, None, :].to_broadcast([P, HB, 2 * D]), ALU.add))
                link(nc.vector.tensor_tensor(sq[:, :, :, :], vec[:, :, :, :], vec[:, :, :, :], ALU.mult))
                nc.vector.tensor_reduce(norm[:, :, :], sq[:, :, :, :], AX.X, ALU.add).then_inc(norm_s, 1)
                dve.wait_ge(root_s, n + 1)
                link(nc.vector.tensor_scalar(norm[:, :, :], norm[:, :, :], 1e-12, None, ALU.max))
                link(nc.vector.reciprocal(norm[:, :, :], norm[:, :, :]))
                link(nc.vector.tensor_tensor(vec[:, :, :, :], vec[:, :, :, :], norm[:, :, :, None].to_broadcast(shape), ALU.mult))

                def reflect(y):
                    link(nc.vector.tensor_tensor(sq[:, :, :, :], vec[:, :, :, :], y, ALU.mult))
                    link(nc.vector.tensor_reduce(dot[:, :, :], sq[:, :, :, :], AX.X, ALU.add))
                    link(nc.vector.scalar_tensor_tensor(msg[:, :, :, :].rearrange("q t a d -> q (t a) d"),
                                                        vec[:, :, :, :].rearrange("q t a d -> q (t a) d"), 2.0,
                                                        dot[:, :, :].rearrange("q t a -> q (t a)")[:, :, None].to_broadcast([P, 2 * HB, D]),
                                                        ALU.mult, ALU.mult))

                reflect(ends[:, :, :, :])
                nc.vector.tensor_tensor(swap[:, :, 1, :], ends[:, :, 0, :], msg[:, :, 0, :], ALU.subtract)
                link(nc.vector.tensor_tensor(swap[:, :, 0, :], ends[:, :, 1, :], msg[:, :, 1, :], ALU.subtract))
                reflect(swap[:, :, :, :])
                link(nc.vector.tensor_tensor(msg[:, :, :, :], swap[:, :, :, :], msg[:, :, :, :], ALU.subtract))
                link(nc.vector.tensor_tensor(msg[:, :, :, :].rearrange("q t a d -> q t (a d)"),
                                             msg[:, :, :, :].rearrange("q t a d -> q t (a d)"),
                                             coef[:, :, None].to_broadcast([P, HB, 2 * D]), ALU.mult))
                nc.vector.tensor_copy(slot_parts(m, n, 0), msg[:, :, 0, :]).then_inc(msg_s, 1)
                dve.wait_ge(msg_s, n + 1)
                link(nc.vector.tensor_tensor(rest[:, :, :], msg[:, :, 0, :], slot_parts(m, n, 0), ALU.subtract))
                nc.vector.tensor_copy(slot_parts(m, n, 1), rest[:, :, :]).then_inc(part_s, 1)
                dve.wait_ge(part_s, n + 1)
                nc.vector.tensor_tensor(slot_parts(m, n, 2), rest[:, :, :], slot_parts(m, n, 1), ALU.subtract)
                return c[0]

            for h in range(2):
                indices(h, h)
            batches(dve, HT, 1, 3, turn)
            dve.wait_ge(used, HT)
            nc.vector.tensor_tensor(m.h[:, :, :], m.h[:, :, :], sums[:, 0:NB * D].rearrange("q (b d) -> q b d", d=D), ALU.add).then_inc(norm_s, 1)

        @block.scalar
        def _(act):
            with act.Fori(0, HT // 2) as i:
                for h in range(2):
                    n = 2 * i + h
                    act.wait_ge(ht_s, n + 1)
                    nc.scalar.copy(hot_t[:, :, :], ht_ps[:, :, :]).then_inc(hot_t_s, 1)
                    act.wait_ge(et_s, n + 1)
                    nc.scalar.copy(ends_t[:, :, :], et_ps[:, :, :]).then_inc(ends_t_s, 1)
                    act.wait_ge(hp_s, n + 1)
                    nc.scalar.activation(hid[:, :], hid_ps[:, :], ACT.Relu, bias=m.mlp_b1[:, 0:1]).then_inc(hid_s, 1)
                    act.wait_ge(norm_s, n + 1)
                    nc.scalar.activation(norm[:, :, :], norm[:, :, :], ACT.Sqrt).then_inc(root_s, 1)

        @block.tensor
        def _(pe):
            clear(nc, m, sums[:, :])
            with pe.Fori(0, HT // 2) as i:
                for h in range(2):
                    n = 2 * i + h
                    pe.wait_ge(hot_s, n + 1)
                    for j in range(HB):
                        last = nc.tensor.transpose(ht_ps[:, j, :], hot[:, h, j, :], m.ident[:, :])
                    last.then_inc(ht_s, 1)
                    blocks = [block_of(m, pe, n * HB + j) for j in range(HB)]
                    pe.wait_ge(hot_t_s, n + 1)
                    for j in range(HB):
                        last = nc.tensor.matmul(xd[:, j, 0:HW], hot_t[:, j, :],
                                                m.wide[:, bass.ds(blocks[j], 1), :].rearrange("q o c -> q (o c)"), start=True, stop=True,
                                                skip_group_check=True)
                    last.then_inc(xd_s, 1)
                    pe.wait_ge(ends_s, n + 1)
                    for j in range(HB):
                        last = nc.tensor.transpose(et_ps[:, j, :], ends[:, j, :, :].rearrange("q a d -> q (a d)"), m.ident[:, :])
                    last.then_inc(et_s, 1)
                    pe.wait_ge(ends_t_s, n + 1)
                    nc.tensor.matmul(hid_ps[:, :], m.mlp1[:, :], ends_t[:, :, :].rearrange("q t e -> q (t e)"), start=True,
                                     stop=True).then_inc(hp_s, 1)
                    pe.wait_ge(hid_s, n + 1)
                    for j in range(HB):
                        last = nc.tensor.matmul(v_ps[:, j, 0:2 * D], hid[:, j * P:(j + 1) * P], m.mlp2[:, :], start=True, stop=True,
                                                skip_group_check=True)
                    last.then_inc(v_s, 1)
                    pe.wait_ge(msg_s, n + 1)
                    for j in range(HB):
                        last = nc.tensor.matmul(sums[:, bass.ds(blocks[j] * D, D)], hot[:, h, j, :], msg[:, j, 1, :], start=False,
                                                stop=True, skip_group_check=True)
                    last.then_inc(used, 1)


def slot_parts(m, n, k):
    return m.parts[:, bass.ds(n * HB, HB), k * D:(k + 1) * D]


def to_sources(nc, m):
    with ExitStack() as outer:
        _, ps, _ = makers(nc, outer, "src")
        sums = ps("sums", [3 * D, NP])
        with ExitStack() as ctx:
            sb, _, sem = makers(nc, ctx, "srl")
            wide, hot = sb("wide", [P, N], FP16), sb("hot", [P, 2, N], BF16)
            ring = sb("ring", [P, 2, TB, 3 * D], BF16)
            iota_s, hot_s, used, ring_s = sem("iota_s"), sem("hot_s"), sem("used"), sem("ring_s")
            block = ctx.enter_context(nc.Block())

            @block.gpsimd
            def _(pool):
                pool.iota(wide[:, :], pattern=[[1, N]], base=-CENTRE, channel_multiplier=0,
                          allow_small_or_imprecise_dtypes=True).then_inc(iota_s, 1)

            @block.vector
            def _(dve):
                dve.wait_ge(iota_s, 1)

                def turn(q, h):
                    t = 2 * q + h
                    wait(dve, used, t - 1)
                    nc.vector.tensor_scalar(hot[:, h, :], wide[:, :], slot_field(m, t, 1, SRCC), None, ALU.is_equal).then_inc(hot_s, 1)

                batches(dve, NT, 3, 1, turn)

            @block.scalar
            def _(act):
                def turn(q, h):
                    n = 2 * q + h
                    wait(act, used, (n - 1) * TB)
                    nc.scalar.copy(ring[:, h], m.parts[:, bass.ds(n * TB, TB), :]).then_inc(ring_s, 1)

                batches(act, NT // TB, 3, 1, turn)

            @block.tensor
            def _(pe):
                clear(nc, m, sums[:, :])
                with pe.Fori(0, NT // TB // 2) as i:
                    for h in range(2):
                        pe.wait_ge(ring_s, 2 * i + h + 1)
                        for j in range(TB):
                            pe.wait_ge(hot_s, (2 * i + h) * TB + j + 1)
                            for c in range(0, N, 512):
                                w = min(512, N - c)
                                last = nc.tensor.matmul(sums[:, c:c + w], ring[:, h, j, :], hot[:, j % 2, c:c + w], start=False,
                                                        stop=True, skip_group_check=True)
                            last.then_inc(used, 1)
                pe.wait_ge(used, NT)
        with ExitStack() as ctx:
            sb, ps, sem = makers(nc, ctx, "srx")
            total = sb("total", [3 * D, NP])
            back = ps("back", [P, 10, 3 * D])
            copied, made, step = sem("copied"), sem("made"), sem("step")
            block = ctx.enter_context(nc.Block())

            @block.scalar
            def _(act):
                nc.scalar.copy(total[:, :], sums[:, :]).then_inc(copied, 1)

            @block.tensor
            def _(pe):
                pe.wait_ge(copied, 1)
                for b in range(NB):
                    if b % 10 == 0:
                        wait(pe, step, 3 * (b // 10))
                    last = nc.tensor.transpose(back[:, b % 10, :], total[:, b * P:(b + 1) * P], m.ident[0:3 * D, 0:3 * D])
                    if b % 10 == 9 or b == NB - 1:
                        last.then_inc(made, 1)

            @block.vector
            def _(dve):
                for n, b in enumerate(range(0, NB, 10)):
                    c = min(10, NB - b)
                    dve.wait_ge(made, n + 1)
                    for k in range(3):
                        wait(dve, step, 3 * n + k)
                        nc.vector.tensor_tensor(m.h[:, b:b + c, :], m.h[:, b:b + c, :], back[:, 0:c, k * D:(k + 1) * D],
                                                ALU.add).then_inc(step, 1)


def finish(nc, m, out):
    with ExitStack() as ctx:
        sb, ps, sem = makers(nc, ctx, "fin")
        done, saved = sem("done"), sem("saved")
        block = ctx.enter_context(nc.Block())

        @block.vector
        def _(dve):
            nc.vector.scalar_tensor_tensor(m.x[:, :, :].rearrange("q b d -> q (b d)"), m.h[:, :, :].rearrange("q b d -> q (b d)"), 0.0,
                                           m.x[:, :, :].rearrange("q b d -> q (b d)"), ALU.max, ALU.add).then_inc(done, 1)

        @block.sync
        def _(sp):
            sp.wait_ge(done, 1)
            sp.dma_start(out[0:(NB - 1) * P, :].rearrange("(b q) d -> q b d", q=P), m.x[:, 0:NB - 1, :]).then_inc(saved, 16)
            sp.dma_start(out[(NB - 1) * P:N, :], m.x[0:TAIL, NB - 1, :]).then_inc(saved, 16)
            sp.wait_ge(saved, 32)


_INS = ['x', 'src', 'dst', 'edge_attr_16', 'edge_type_8', 'edge_weight', 'L0_gnn_edge_emb', 'L0_gnn_w_ih', 'L0_gnn_w_hh',
        'L0_gnn_b_ih', 'L0_gnn_b_hh', 'L1_gnn_W_msg', 'L1_gnn_b_msg', 'L1_gnn_W_attn', 'L1_gnn_b_attn', 'L2_gnn_w0',
        'L2_gnn_b0', 'L2_gnn_w1', 'L2_gnn_b1', 'L2_gnn_w2', 'L2_gnn_b2', 'L2_gnn_w3', 'L2_gnn_b3', 'L3_gnn_W1',
        'L3_gnn_b1', 'L3_gnn_W2', 'L3_gnn_b2']

def build(nc, a, out):
    PAST.clear()
    m = Net()

    def dram(name, shape):
        return nc.dram_tensor(name, shape, F32).ap()

    m.key_rows, m.hi_rows = dram("key_rows", [EC, EP]), dram("hi_rows", [EC, EP])
    m.slots, m.spare = dram("slots", [SLOTS, REC]), dram("spare", [2, D])
    m.slot_keys, m.far_row, m.end_row = dram("slot_keys", [SLOTS + 2]), dram("far_row", [SLOTS]), dram("end_row", [SLOTS])
    m.typed, m.node16, m.node20 = dram("typed", [NP * 8, D]), dram("node16", [NP, D]), dram("node20", [NP, HW])
    m.node_h, m.node_g3 = dram("node_h", [NP, D]), dram("node_g3", [NP, D])
    m.node128 = [dram("node128a", [NP, P]), dram("node128b", [NP, P])]
    m.dinv_dram = dram("dinv_dram", [NP])
    with ExitStack() as ctx:
        def on(scope):
            return lambda name, shape, dt=F32: scope.enter_context(nc.sbuf_tensor(name, shape, dt))

        sb = on(ctx)
        m.pool_passed = ctx.enter_context(nc.semaphore("pool_passed"))
        m.slots_sb = sb("slots_sb", [P, NT * REC])
        m.ident, m.below, m.above, m.twice = (sb(n, [P, P]) for n in ("ident", "below", "above", "twice"))
        m.iota_row, m.iota_col = sb("iota_row", [P, P]), sb("iota_col", [P, 1])
        m.zero_row = sb("zero_row", [1, 512])
        m.blk = sb("blk", [1, NT], I32)
        m.dis, m.dinv = sb("dis", [P, NB]), sb("dinv", [P, NB])
        m.x, m.h = sb("x", [P, NB, D]), sb("h", [P, NB, D])
        m.emb = sb("emb", [D, 8 * D])
        m.gru_i, m.gru_h = sb("gru_i", [D + 1, 4 * D]), sb("gru_h", [D + 1, 4 * D])
        m.pair_w = [sb(f"pair_w{g}", [17 * ni, 2, 16 * ni]) for g, (_, ni) in enumerate(GROUPS)]
        shapes = [(D, P), (P, P), (P, P), (P, D)]
        m.conv_w = [sb(f"conv_w{k}", list(s)) for k, s in enumerate(shapes)]
        m.conv_b = [sb(f"conv_b{k}", [s[1], 1]) for k, s in enumerate(shapes)]
        m.mlp1, m.mlp_b1, m.mlp2, m.mlp_b2 = sb("mlp1", [2 * D, P]), sb("mlp_b1", [P, 1]), sb("mlp2", [P, 2 * D]), sb("mlp_b2", [P, 2 * D])
        with ExitStack() as scope:
            rb = on(scope)
            m.iota_tiles = rb("iota_tiles", [P, NT])
            m.key_f, m.hi_f, m.lo_f, m.src_hi_f, m.src_lo_f = (rb(n, [EP, EC]) for n in ("key_f", "hi_f", "lo_f", "src_hi_f", "src_lo_f"))
            m.first = rb("first", [NB, NS, P])
            record_keys(nc, a, m)
            histogram(nc, m)
            rank_and_scatter(nc, m)
        weights(nc, a, m)
        segments(nc, m)
        with ExitStack() as scope:
            rb = on(scope)
            m.ht, m.mt, m.sums = rb("ht", [D + 1, NP]), rb("mt", [D + 1, NP]), rb("sums", [P, NB, 20])
            normalise(nc, m, "n0")
            type_table(nc, m)
            aggregate_typed(nc, m)
            gru(nc, m)
        with ExitStack() as scope:
            rb = on(scope)
            m.top = rb("top", [P, NB, 256])
            normalise(nc, m, "n1")
            save_rows(nc, m, "s1", [(m.node16, m.h[:, :, :])])
            segment_max(nc, m)
            m.acc = rb("acc", [P, NB, 512])
            soft_sums(nc, m)
            attend(nc, m)
        renew_semaphores(nc)
        with ExitStack() as scope:
            rb = on(scope)
            m.g, m.agg, m.hidden, m.dinv_row = rb("g", [P, NB, P]), rb("agg", [P, NP]), rb("hidden", [P, NP]), rb("dinv_row", [P, NP])
            normalise(nc, m, "n2")
            node_factors(nc, m)
            convolve(nc, m, "c0", m.node16, D)
            dense(nc, m, "d0", 0)
            project(nc, m, "p1", 1, m.node128[0], P, False)
            convolve(nc, m, "c1", m.node128[0], P)
            project(nc, m, "p2", 2, m.node128[1], P, True)
            convolve(nc, m, "c2", m.node128[1], P)
            project(nc, m, "p3", 3, m.node_g3, D, True)
            convolve(nc, m, "c3", m.node_g3, D)
            close_convolutions(nc, m)
        with ExitStack() as scope:
            rb = on(scope)
            m.parts, m.wide = rb("parts", [P, NT, 3 * D], BF16), rb("wide", [P, NB, HW])
            normalise(nc, m, "n3")
            sheaf_rows(nc, m)
            sheaf_messages(nc, m)
            to_sources(nc, m)
            finish(nc, m, out)


def kernel(**inputs):
    import numpy as _np
    import concourse.bacc as _bacc
    from concourse import mybir as _mybir
    from concourse.bass_utils import run_bass_kernel_spmd as _run

    nc = _bacc.Bacc("TRN2", target_bir_lowering=False, num_devices=1)
    arrays, aps = {}, {}
    for name in _INS:
        arr = _np.ascontiguousarray(inputs[name])
        arrays[f"in_{name}"] = arr
        aps[name] = nc.dram_tensor(f"in_{name}", arr.shape, _mybir.dt.from_np(arr.dtype), kind="ExternalInput").ap()
    out = nc.dram_tensor("out_0", (N, D), _mybir.dt.float32, kind="ExternalOutput").ap()
    build(nc, aps, out)
    r = _run(nc, [arrays], core_ids=[0])
    return r.results[0]["out_0"]
```

```python
from contextlib import ExitStack

import concourse.bass as bass
from concourse import mybir

ALU = mybir.AluOpType
ACT = mybir.ActivationFunctionType
AX = mybir.AxisListType
F32 = mybir.dt.float32
I32 = mybir.dt.int32
BF16 = mybir.dt.bfloat16
FP16 = mybir.dt.float16

P = 128
N, E, D = 3125, 100000, 16
NB = -(-N // P)
NP = NB * P
TAIL = N - (NB - 1) * P
EP, EC = 125, 800
NS = 4
SC = EC // NS
TB = 8
NT = -(-2 * ((E + NB * (2 * P - 1)) // (2 * P)) // (2 * TB)) * 2 * TB
SLOTS = NT * P
IT = NT // (2 * TB)

ONE, FIELDS, REC = 16, 17, 24
WGT, SRC, TIX, LO, SRCC, KEY, LOE, NF = range(8)
K17 = D + 1
CENTRE = N // 2
FAR = -3.0e38

PARTS = [(0, 0), (1, 0), (2, 0), (0, 1), (1, 1), (0, 2)]
KP = len(PARTS) * K17


class Net:
    pass


def makers(nc, ctx, stage):
    def sb(name, shape, dt=F32):
        return ctx.enter_context(nc.sbuf_tensor(f"{stage}_{name}", shape, dt))

    def ps(name, shape, dt=F32):
        return ctx.enter_context(nc.psum_tensor(f"{stage}_{name}", shape, dt))

    def sem(name):
        made = nc.alloc_semaphore(f"{stage}_{name}")
        ctx.callback(PAST.append, made)
        return made

    return sb, ps, sem


PAST = []


def renew_semaphores(nc):
    nc.clear_and_free_semaphores(list(PAST))
    PAST.clear()
    with nc.Block():
        pass




def record_keys(nc, a, m):
    with ExitStack() as ctx:
        sb, ps, sem = makers(nc, ctx, "rec")
        dst_i, src_i, typ_i, tmp_i = (sb(n, [EP, EC], I32) for n in ("dst_i", "src_i", "typ_i", "tmp_i"))
        tmp2_i = sb("tmp2_i", [EP, EC], I32)
        wgt = sb("wgt", [EP, EC])
        feat = sb("feat", [EP, EC * D // 4])
        rows = sb("rows", [100, 2, 8, EP])
        turned = ps("turned", [100, 2, 4, P])
        idx_in, feat_in, feat_free = sem("idx_in"), sem("feat_in"), sem("feat_free")
        keys, mid, rec = sem("keys"), sem("mid"), sem("rec")
        turned_s, rows_s, rows_out, consts = sem("turned_s"), sem("rows_s"), sem("rows_out"), sem("consts")
        hole = sb("hole", [P, 32 * REC])
        holes_s, hole_s = sem("holes_s"), sem("hole_s")
        edges = m.edges[:, :].rearrange("p (c k) -> p c k", k=REC)
        feats = a["edge_attr_16"].rearrange("(p c) d -> p (c d)", p=EP)
        block = ctx.enter_context(nc.Block())

        @block.sync
        def _(sp):
            sp.dma_start(dst_i[:, :], a["dst"].rearrange("(p c) -> p c", p=EP)).then_inc(idx_in, 16)
            sp.dma_start(src_i[:, :], a["src"].rearrange("(p c) -> p c", p=EP)).then_inc(idx_in, 16)
            sp.dma_start(typ_i[:, :], a["edge_type_8"].rearrange("(p c) -> p c", p=EP)).then_inc(idx_in, 16)
            sp.dma_start(wgt[:, :], a["edge_weight"].rearrange("(p c) -> p c", p=EP)).then_inc(idx_in, 16)
            q = EC * D // 4
            for c in range(4):
                if c:
                    sp.wait_ge(feat_free, c)
                sp.dma_start(feat[:, :], feats[:, c * q:(c + 1) * q]).then_inc(feat_in, 16)
            sp.wait_ge(rows_s, 4)
            for k, dram in ((0, m.key_rows), (1, m.hi_rows)):
                sp.dma_start(dram.rearrange("(g t) p -> t g p", g=8), rows[:, k, :, :]).then_inc(rows_out, 16)
            sp.wait_ge(hole_s, 4)
            whole = m.slots.rearrange("(p c n) k -> p c (n k)", p=P, n=32)
            sp.dma_start(whole, hole[:, None, :].to_broadcast([P, NT // 32, 32 * REC])).then_inc(holes_s, 16)
            sp.wait_ge(rows_out, 32)
            sp.wait_ge(holes_s, 16)

        @block.gpsimd
        def _(pool):
            pool.iota(m.iota_row[:, :], pattern=[[1, P]], base=0, channel_multiplier=0,
                      allow_small_or_imprecise_dtypes=True).then_inc(consts, 1)
            pool.iota(m.iota_col[:, :], pattern=[[0, 1]], base=0, channel_multiplier=1,
                      allow_small_or_imprecise_dtypes=True).then_inc(consts, 1)
            pool.iota(m.iota_tiles[:, :], pattern=[[1, NT]], base=0, channel_multiplier=0,
                      allow_small_or_imprecise_dtypes=True).then_inc(consts, 1)
            pool.memset(m.zero_row[:, :], 0.0).then_inc(consts, 1)

        @block.vector
        def _(dve):
            dve.wait_ge(consts, 3)
            nc.vector.tensor_scalar(m.ident[:, :], m.iota_row[:, :], m.iota_col[:, 0:1], None, ALU.is_equal).then_inc(keys, 1)
            nc.vector.tensor_scalar(m.below[:, :], m.iota_row[:, :], m.iota_col[:, 0:1], None, ALU.is_lt).then_inc(keys, 1)
            nc.vector.tensor_scalar(m.above[:, :], m.iota_row[:, :], m.iota_col[:, 0:1], None, ALU.is_gt).then_inc(keys, 1)
            hv = hole[:, :].rearrange("p (n k) -> p n k", k=REC)
            nc.vector.memset(hole[:, :], 0.0).then_inc(hole_s, 1)
            dve.wait_ge(hole_s, 1)
            nc.vector.memset(hv[:, :, FIELDS + LO], -1.0).then_inc(hole_s, 1)
            nc.vector.memset(hv[:, :, FIELDS + KEY], -1.0).then_inc(hole_s, 1)
            nc.vector.memset(hv[:, :, FIELDS + SRCC], -3.0 * CENTRE).then_inc(hole_s, 1)
            dve.wait_ge(idx_in, 64)
            nc.vector.tensor_single_scalar(tmp_i[:, :], dst_i[:, :], 7, ALU.logical_shift_right).then_inc(mid, 1)
            nc.vector.tensor_single_scalar(tmp2_i[:, :], dst_i[:, :], P - 1, ALU.bitwise_and).then_inc(mid, 1)
            nc.vector.tensor_copy(m.key_f[:, :], dst_i[:, :]).then_inc(keys, 1)
            dve.wait_ge(mid, 2)
            nc.vector.tensor_copy(m.hi_f[:, :], tmp_i[:, :]).then_inc(keys, 1)
            nc.vector.tensor_copy(m.lo_f[:, :], tmp2_i[:, :]).then_inc(mid, 1)
            dve.wait_ge(mid, 3)
            dve.wait_ge(keys, 5)
            nc.vector.tensor_copy(edges[:, :, FIELDS + LO], m.lo_f[:, :]).then_inc(rec, 1)
            nc.vector.tensor_copy(edges[:, :, FIELDS + KEY], m.key_f[:, :]).then_inc(rec, 1)
            nc.vector.tensor_single_scalar(tmp_i[:, :], src_i[:, :], 7, ALU.logical_shift_right).then_inc(mid, 1)
            nc.vector.tensor_single_scalar(tmp2_i[:, :], src_i[:, :], P - 1, ALU.bitwise_and).then_inc(mid, 1)
            dve.wait_ge(mid, 5)
            nc.vector.tensor_copy(m.src_hi_f[:, :], tmp_i[:, :]).then_inc(rec, 1)
            nc.vector.tensor_copy(m.src_lo_f[:, :], tmp2_i[:, :]).then_inc(rec, 1)
            nc.vector.tensor_copy(edges[:, :, FIELDS + SRC], src_i[:, :]).then_inc(rec, 1)
            nc.vector.tensor_scalar(edges[:, :, FIELDS + SRCC], src_i[:, :], -float(CENTRE), None, ALU.add).then_inc(rec, 1)
            nc.vector.scalar_tensor_tensor(edges[:, :, FIELDS + TIX], src_i[:, :], 8.0, typ_i[:, :], ALU.mult, ALU.add).then_inc(rec, 1)
            nc.vector.tensor_copy(edges[:, :, FIELDS + WGT], wgt[:, :]).then_inc(rec, 1)
            nc.vector.memset(edges[:, :, ONE], 1.0).then_inc(rec, 1)
            nc.vector.memset(edges[:, :, FIELDS + LOE], 0.0).then_inc(rec, 1)
            for k in range(2):
                for half in range(2):
                    dve.wait_ge(turned_s, 2 * k + half + 1)
                    nc.vector.tensor_copy(rows[:, k, 4 * half:4 * half + 4, :], turned[:, half, :, 0:EP]).then_inc(rows_s, 1)

        @block.tensor
        def _(pe):
            pe.wait_ge(keys, 5)
            for k, what in enumerate((m.key_f, m.hi_f)):
                for half in range(2):
                    if k:
                        pe.wait_ge(rows_s, half + 1)
                    for g in range(4):
                        c = 100 * (4 * half + g)
                        last = nc.tensor.transpose(turned[:, half, g, 0:EP], what[:, c:c + 100], m.ident[0:EP, 0:EP])
                    last.then_inc(turned_s, 1)

        @block.scalar
        def _(act):
            for c in range(4):
                act.wait_ge(feat_in, 16 * (c + 1))
                nc.scalar.copy(edges[:, c * SC:(c + 1) * SC, 0:D],
                               feat[:, :].rearrange("p (c d) -> p c d", d=D)).then_inc(feat_free, 1)


def histogram(nc, m):
    with ExitStack() as ctx:
        sb, ps, sem = makers(nc, ctx, "hist")
        hot_lo, hot_slo = sb("hot_lo", [EP, 2, NS, P], BF16), sb("hot_slo", [EP, 2, NS, P], BF16)
        hot_hi, hot_shi = sb("hot_hi", [EP, 2, NS, NB], BF16), sb("hot_shi", [EP, 2, NS, NB], BF16)
        by_dst, by_src, small = ps("by_dst", [NB, NS * P]), ps("by_src", [NB, P]), ps("small", [P, 512])
        blk_ps = ps("blk_ps", [1, 2, 512])
        cnt, tot, incl, one = sb("cnt", [NB, NS, P]), sb("tot", [NB, P]), sb("incl", [NB, P]), sb("one", [NB, P])
        tiles_i, tiles, start = sb("tiles_i", [NB, 2], I32), sb("tiles", [NB, 1]), sb("start", [NB, 2])
        deg, past, blk_f = sb("deg", [NB, P]), sb("past", [NB, NT]), sb("blk_f", [1, NT])
        root = sb("root", [P, NB])
        hot_d = [sem("hot_d0"), sem("hot_d1")]
        hot_s = [sem("hot_s0"), sem("hot_s1")]
        used_d = [sem("used_d0"), sem("used_d1")]
        used_s = [sem("used_s0"), sem("used_s1")]
        counted, step, mm, root_s = sem("counted"), sem("step"), sem("mm"), sem("root_s")
        block = ctx.enter_context(nc.Block())

        def column(t, s):
            return t[:, :].rearrange("p (j s) -> p j s", j=NS)[:, :, bass.ds(s, 1)]

        def one_hots(eng, lo, hi, lo_f, hi_f, s, h):
            eng.tensor_tensor(lo[:, h], column(lo_f, s).to_broadcast([EP, NS, P]),
                              m.iota_row[0:EP, None, :].to_broadcast([EP, NS, P]), ALU.is_equal)
            return eng.tensor_tensor(hi[:, h], column(hi_f, s).to_broadcast([EP, NS, NB]),
                                     m.iota_row[0:EP, None, 0:NB].to_broadcast([EP, NS, NB]), ALU.is_equal)

        @block.vector
        def _(dve):
            nc.vector.memset(one[:, :], 1.0).then_inc(step, 1)
            with dve.Fori(0, SC // 2) as i:
                for h in range(2):
                    dve.wait_ge(used_d[h], i + 1)
                    one_hots(nc.vector, hot_lo, hot_hi, m.lo_f, m.hi_f, 2 * i + h, h).then_inc(hot_d[h], 1)
                    dve.wait_ge(used_s[h], i + 1)
                    one_hots(nc.vector, hot_slo, hot_shi, m.src_lo_f, m.src_hi_f, 2 * i + h, h).then_inc(hot_s[h], 1)
            dve.wait_ge(counted, 1)
            nc.vector.tensor_copy(cnt[:, :, :], by_dst[:, :].rearrange("p (j l) -> p j l", j=NS)).then_inc(step, 1)
            dve.wait_ge(step, 2)
            nc.vector.tensor_reduce(tot[:, :], cnt[:, :, :].rearrange("p j l -> p l j"), AX.X, ALU.add).then_inc(step, 1)
            dve.wait_ge(step, 3)
            nc.vector.tensor_tensor_scan(incl[:, :], one[:, :], tot[:, :], 0.0, ALU.mult, ALU.add).then_inc(step, 1)
            nc.vector.tensor_tensor(deg[:, :], tot[:, :], by_src[:, :], ALU.add).then_inc(step, 1)
            dve.wait_ge(step, 5)
            nc.vector.tensor_scalar(tiles_i[:, 0:1], incl[:, P - 1:P], float(2 * P - 1), None, ALU.add).then_inc(step, 1)
            dve.wait_ge(step, 6)
            nc.vector.tensor_single_scalar(tiles_i[:, 1:2], tiles_i[:, 0:1], 8, ALU.logical_shift_right).then_inc(step, 1)
            dve.wait_ge(step, 7)
            nc.vector.tensor_scalar(tiles[:, :], tiles_i[:, 1:2], 2.0, None, ALU.mult).then_inc(step, 1)
            dve.wait_ge(mm, 1)
            nc.vector.tensor_copy(start[:, 0:1], small[0:NB, 0:1]).then_inc(step, 1)
            nc.vector.tensor_tensor(incl[:, :], incl[:, :], tot[:, :], ALU.subtract).then_inc(step, 1)
            dve.wait_ge(step, 10)
            nc.vector.tensor_tensor(start[:, 1:2], start[:, 0:1], tiles[:, :], ALU.add).then_inc(step, 1)
            nc.vector.scalar_tensor_tensor(m.first[:, 0, :], start[:, 0:1].to_broadcast([NB, P]), float(P), incl[:, :],
                                           ALU.mult, ALU.add).then_inc(step, 1)
            for j in range(1, NS):
                dve.wait_ge(step, 11 + j)
                nc.vector.tensor_tensor(m.first[:, j, :], m.first[:, j - 1, :], cnt[:, j - 1, :], ALU.add).then_inc(step, 1)
            nc.vector.tensor_scalar(past[:, :], m.iota_tiles[0:NB, :], start[:, 1:2], None, ALU.is_ge).then_inc(step, 1)
            dve.wait_ge(mm, 2)
            h = NT // 2
            nc.vector.tensor_scalar(blk_f[:, :].rearrange("o (a t) -> o a t", a=2), blk_ps[:, :, 0:h], float(NB - 1), None,
                                    ALU.min).then_inc(step, 1)
            dve.wait_ge(step, 17)
            nc.vector.tensor_copy(m.blk[:, :], blk_f[:, :]).then_inc(step, 1)
            nc.vector.tensor_scalar(root[:, :], small[:, 64:64 + NB], 1e-5, None, ALU.max).then_inc(step, 1)
            dve.wait_ge(root_s, 1)
            nc.vector.reciprocal(m.dis[:, :], m.dis[:, :]).then_inc(step, 1)

        @block.scalar
        def _(act):
            act.wait_ge(step, 19)
            nc.scalar.activation(m.dis[:, :], root[:, :], ACT.Sqrt).then_inc(root_s, 1)

        @block.tensor
        def _(pe):
            for ap in (by_dst[:, :], by_src[:, :]):
                nc.tensor.matmul(ap, m.zero_row[0:1, 0:NB], m.zero_row[0:1, 0:ap.shape[1]], start=True, stop=True,
                                 skip_group_check=True)
            for h in range(2):
                pe.sem_inc(used_d[h], 1)
                pe.sem_inc(used_s[h], 1)
            with pe.Fori(0, SC // 2) as i:
                for h in range(2):
                    pe.wait_ge(hot_d[h], i + 1)
                    for j in range(NS):
                        last = nc.tensor.matmul(by_dst[:, j * P:(j + 1) * P], hot_hi[:, h, j, :], hot_lo[:, h, j, :],
                                                start=False, stop=True, skip_group_check=True)
                    last.then_inc(used_d[h], 1)
                    pe.wait_ge(hot_s[h], i + 1)
                    for j in range(NS):
                        last = nc.tensor.matmul(by_src[:, :], hot_shi[:, h, j, :], hot_slo[:, h, j, :],
                                                start=False, stop=True, skip_group_check=True)
                    last.then_inc(used_s[h], 1)
            for h in range(2):
                pe.wait_ge(used_d[h], SC // 2 + 1)
                pe.wait_ge(used_s[h], SC // 2 + 1)
            pe.sem_inc(counted, 1)
            pe.wait_ge(step, 8)
            nc.tensor.matmul(small[0:NB, 0:1], m.above[0:NB, 0:NB], tiles[:, :], start=True, stop=True)
            nc.tensor.matmul(small[:, 64:64 + NB], deg[:, :], m.ident[0:NB, 0:NB], start=True, stop=True).then_inc(mm, 1)
            pe.wait_ge(step, 16)
            h = NT // 2
            for k in range(2):
                last = nc.tensor.matmul(blk_ps[:, k, 0:h], one[:, 0:1], past[:, k * h:(k + 1) * h], start=True, stop=True)
            last.then_inc(mm, 1)


def rank_and_scatter(nc, m):
    with ExitStack() as ctx:
        sb, ps, sem = makers(nc, ctx, "rank")
        pair = lambda n: [sem(n + "0"), sem(n + "1")]
        key_row, hi_row = sb("key_row", [EP, 2, NS, EP]), sb("hi_row", [NB, 2, NS, EP])
        hot_lo, hot_hi = sb("hot_lo", [EP, 2, NS, P], BF16), sb("hot_hi", [EP, 2, NS, NB], BF16)
        hot_hi_t = sb("hot_hi_t", [NB, 2, NS, EP])
        next_sb, next_ps = sb("next_sb", [NB, 2, NS * P]), ps("next_ps", [NB, NS * P])
        found = [ps("found0", [EP, NS, P]), ps("found1", [EP, NS, P])]
        picked, same = sb("picked", [EP, NS, P]), sb("same", [EP, NS, EP])
        base, local, pos = sb("base", [EP, NS]), sb("local", [EP, NS]), sb("pos", [EP, 4, NS], I32)
        row_i = sb("row_i", [EP, 2, NS], I32)
        staged = sb("staged", [EP, 2, NS, REC])
        row_in, row_used = pair("row_in"), pair("row_used")
        hots, looked, counted = pair("hots"), pair("looked"), pair("counted")
        state, at_row, rec_in, sent = pair("state"), pair("at_row"), pair("rec_in"), pair("sent")
        chain, seeded, loads = sem("chain"), sem("seeded"), sem("loads")
        edges = m.edges[:, :].rearrange("p (j s k) -> p j s k", j=NS, k=REC)
        key_rows = m.key_rows.rearrange("(j s) p -> s j p", j=NS)
        hi_rows = m.hi_rows.rearrange("(j s) p -> s j p", j=NS)
        turns = SC // 2
        block = ctx.enter_context(nc.Block())

        def column(t, s):
            return t[:, :].rearrange("p (j s) -> p j s", j=NS)[:, :, bass.ds(s, 1)]

        @block.sync
        def _(sp):
            with sp.Fori(0, turns) as i:
                for h in range(2):
                    sp.wait_ge(row_used[h], i + 1)
                    sp.dma_start(key_row[:, h], key_rows[bass.ds(2 * i + h, 1)].to_broadcast([EP, NS, EP])).then_inc(row_in[h], 16)
                    sp.dma_start(hi_row[:, h], hi_rows[bass.ds(2 * i + h, 1)].to_broadcast([NB, NS, EP])).then_inc(row_in[h], 16)

        @block.vector
        def _(dve):
            for h in range(2):
                dve.sem_inc(row_used[h], 1)
            def one_hots(i, h):
                s = 2 * i + h
                dve.wait_ge(counted[h], i + 1)
                nc.vector.tensor_tensor(hot_lo[:, h], column(m.lo_f, s).to_broadcast([EP, NS, P]),
                                        m.iota_row[0:EP, None, :].to_broadcast([EP, NS, P]), ALU.is_equal)
                nc.vector.tensor_tensor(hot_hi[:, h], column(m.hi_f, s).to_broadcast([EP, NS, NB]),
                                        m.iota_row[0:EP, None, 0:NB].to_broadcast([EP, NS, NB]), ALU.is_equal)
                dve.wait_ge(row_in[h], (i + 1) * 32)
                nc.vector.tensor_scalar(hot_hi_t[:, h], hi_row[:, h], m.iota_col[0:NB, 0:1], None,
                                        ALU.is_equal).then_inc(hots[h], 1)

            def place(i, h):
                s = 2 * i + h
                for j in range(NS):
                    last = nc.vector.scalar_tensor_tensor(same[:, j, :], key_row[:, h, j, :], m.key_f[:, bass.ds(s + j * SC, 1)],
                                                          m.below[0:EP, 0:EP], ALU.is_equal, ALU.mult,
                                                          accum_out=local[:, j:j + 1])
                last.then_inc(row_used[h], 1)
                dve.wait_ge(looked[h], i + 1)
                nc.vector.tensor_tensor(picked[:, :, :], found[h][:, :, :], hot_lo[:, h], ALU.mult).then_inc(chain, 1)
                dve.wait_ge(chain, 4 * s + 1)
                nc.vector.tensor_reduce(base[:, :], picked[:, :, :], AX.X, ALU.add).then_inc(chain, 1)
                dve.wait_ge(chain, 4 * s + 2)
                dve.wait_ge(row_used[h], i + 2)
                nc.vector.tensor_tensor(pos[:, 0, :], base[:, :], local[:, :], ALU.add).then_inc(chain, 1)
                dve.wait_ge(chain, 4 * s + 3)
                nc.vector.tensor_single_scalar(pos[:, 1, :], pos[:, 0, :], 7, ALU.logical_shift_right)
                nc.vector.tensor_single_scalar(pos[:, 2, :], pos[:, 0, :], P - 1, ALU.bitwise_and).then_inc(chain, 1)
                dve.wait_ge(chain, 4 * s + 4)
                dve.wait_ge(sent[h], i * 64 + 16)
                nc.vector.scalar_tensor_tensor(row_i[:, h], pos[:, 2, :], float(NT), pos[:, 1, :], ALU.mult,
                                               ALU.add).then_inc(at_row[h], 1)

            one_hots(0, 0)
            with dve.Fori(0, turns - 1) as i:
                for h in range(2):
                    one_hots(i + h, 1 - h)
                    place(i, h)
            one_hots(turns - 1, 1)
            for h in range(2):
                place(turns - 1, h)

        @block.scalar
        def _(act):
            act.wait_ge(seeded, 1)
            with act.Fori(0, turns) as i:
                for h in range(2):
                    s = 2 * i + h
                    act.wait_ge(counted[1 - h], i + 1 + h)
                    nc.scalar.copy(next_sb[:, h], next_ps[:, :]).then_inc(state[h], 1)
                    act.wait_ge(sent[h], i * 64 + 16)
                    nc.scalar.copy(staged[:, h], edges[:, :, bass.ds(s, 1), :].rearrange("p j o k -> p j (o k)")).then_inc(rec_in[h], 1)

        @block.tensor
        def _(pe):
            nc.tensor.matmul(next_ps[:, :], m.ident[0:NB, 0:NB], m.first[:, :, :].rearrange("p j l -> p (j l)"),
                             start=True, stop=True, skip_group_check=True).then_inc(seeded, 1)
            for h in range(2):
                pe.sem_inc(counted[h], 1)
            with pe.Fori(0, turns) as i:
                for h in range(2):
                    pe.wait_ge(hots[h], i + 1)
                    pe.wait_ge(state[h], i + 1)
                    for j in range(NS):
                        last = nc.tensor.matmul(found[h][:, j, :], hot_hi_t[:, h, j, :], next_sb[:, h, j * P:(j + 1) * P],
                                                start=True, stop=True, skip_group_check=True)
                    last.then_inc(looked[h], 1)
                    for j in range(NS):
                        last = nc.tensor.matmul(next_ps[:, j * P:(j + 1) * P], hot_hi[:, h, j, :], hot_lo[:, h, j, :],
                                                start=False, stop=True, skip_group_check=True)
                    last.then_inc(counted[h], 1)

        @block.gpsimd
        def _(pool):
            for h in range(2):
                pool.dma_start(m.spare[h:h + 1, :], m.zero_row[0:1, 0:D]).then_inc(sent[h], 16)
            with pool.Fori(0, turns) as i:
                for h in range(2):
                    pool.wait_ge(rec_in[h], i + 1)
                    pool.sem_inc(m.pool_passed, 1)
                    pool.wait_ge(at_row[h], i + 1)
                    pool.sem_inc(m.pool_passed, 1)
                    for j in range(NS):
                        pool.indirect_dma_start(m.slots, bass.IndirectOffsetOnAxis(ap=row_i[:, h, j:j + 1], axis=0),
                                                staged[:, h, j, :], None).then_inc(sent[h], 16)
            for h in range(2):
                pool.wait_ge(sent[h], turns * 64 + 16)


def weights(nc, a, m):
    with ExitStack() as ctx:
        sb, ps, sem = makers(nc, ctx, "wts")
        zeroed, loaded, marks, step, all_in, spread = sem("zeroed"), sem("loaded"), sem("marks"), sem("step"), sem("all_in"), sem("spread")
        w_all, w_part = sb("w_all", [K17, 512]), sb("w_part", [K17, 3, 512], BF16)
        chan, row_i, row_f = sb("chan", [3 * D, 256]), sb("row_i", [3 * D, 1], I32), sb("row_f", [3 * D, 1])
        block = ctx.enter_context(nc.Block())

        @block.vector
        def _(dve):
            for t in (m.gru_i, m.gru_h, m.mlp2):
                nc.vector.memset(t[tuple(slice(None) for _ in t.shape)], 0.0).then_inc(zeroed, 1)
            nc.vector.memset(m.x[:, NB - 1, :], 0.0).then_inc(zeroed, 1)
            dve.wait_ge(marks, 2)
            nc.vector.tensor_single_scalar(row_i[:, :], row_i[:, :], D - 1, ALU.bitwise_and).then_inc(step, 1)
            dve.wait_ge(step, 1)
            nc.vector.tensor_copy(row_f[:, :], row_i[:, :]).then_inc(step, 1)
            dve.wait_ge(step, 2)
            nc.vector.tensor_scalar(m.widen[:, :], chan[:, :], row_f[:, 0:1], None, ALU.is_equal).then_inc(step, 1)
            dve.wait_ge(all_in, 1)
            nc.vector.tensor_copy(w_part[:, 0, :], w_all[:, :]).then_inc(step, 1)
            dve.wait_ge(step, 4)
            nc.vector.tensor_tensor(w_all[:, :], w_all[:, :], w_part[:, 0, :], ALU.subtract).then_inc(step, 1)
            dve.wait_ge(step, 5)
            nc.vector.tensor_copy(w_part[:, 1, :], w_all[:, :]).then_inc(step, 1)
            dve.wait_ge(step, 6)
            nc.vector.tensor_tensor(w_part[:, 2, :], w_all[:, :], w_part[:, 1, :], ALU.subtract).then_inc(step, 1)

        @block.gpsimd
        def _(pool):
            pool.iota(chan[:, :], pattern=[[1, D], [0, D]], base=0, channel_multiplier=0,
                      allow_small_or_imprecise_dtypes=True).then_inc(marks, 1)
            pool.iota(row_i[:, :], pattern=[[0, 1]], base=0, channel_multiplier=1).then_inc(marks, 1)

        @block.sync
        def _(sp):
            sp.wait_ge(zeroed, 4)
            n = 0

            def load(dst, src):
                nonlocal n
                n += 1
                sp.dma_start(dst, src).then_inc(loaded, 16)

            with nc.allow_non_contiguous_dma(reason="small weights, turned while they load"):
                load(m.x[:, 0:NB - 1, :], a["x"][0:(NB - 1) * P, :].rearrange("(b q) d -> q b d", q=P))
                load(m.x[0:TAIL, NB - 1, :], a["x"][(NB - 1) * P:N, :])
                for t in range(8):
                    load(m.emb[:, t * D:(t + 1) * D], a["L0_gnn_edge_emb"][t].rearrange("(m h) -> h m", h=D))
                for dst, w, b, halves in ((m.gru_i, "L0_gnn_w_ih", "L0_gnn_b_ih", ((0, 3 * D, 0),)),
                                          (m.gru_h, "L0_gnn_w_hh", "L0_gnn_b_hh", ((0, 2 * D, 0), (2 * D, 3 * D, 3 * D)))):
                    for lo, hi, at in halves:
                        load(dst[0:D, at:at + hi - lo], a[w][lo:hi, :].rearrange("g k -> k g"))
                        load(dst[D:D + 1, at:at + hi - lo], a[b][None, lo:hi])
                for k, (w, b) in enumerate((("L1_gnn_W_msg", "L1_gnn_b_msg"), ("L1_gnn_W_attn", "L1_gnn_b_attn"))):
                    load(w_all[0:D, k * 256:(k + 1) * 256], a[w])
                    load(w_all[D:K17, k * 256:(k + 1) * 256], a[b][None, :])
                for k in range(4):
                    load(m.conv_w[k][:, :], a[f"L2_gnn_w{k}"])
                    load(m.conv_b[k][:, :], a[f"L2_gnn_b{k}"][:, None])
                w1, w2 = a["L3_gnn_W1"], a["L3_gnn_W2"]
                load(m.mlp1[:, 0:64], w1.rearrange("h k -> k h"))
                load(m.mlp1[0:D, 64:P], w1[:, D:2 * D].rearrange("h k -> k h"))
                load(m.mlp1[D:2 * D, 64:P], w1[:, 0:D].rearrange("h k -> k h"))
                for k in range(2):
                    load(m.mlp_b1[64 * k:64 * k + 64, :], a["L3_gnn_b1"][:, None])
                    load(m.mlp2[64 * k:64 * k + 64, k * D:(k + 1) * D], w2.rearrange("o h -> h o"))
                    load(m.mlp_b2[:, k * D:(k + 1) * D], a["L3_gnn_b2"][None, :].to_broadcast([P, D]))
            sp.wait_ge(loaded, 16 * n)
            sp.sem_inc(all_in, 1)
            sp.wait_ge(step, 7)
            for r, (_, k) in enumerate(PARTS):
                sp.dma_start(m.w6[r * K17:(r + 1) * K17, :], w_part[:, k, :]).then_inc(spread, 16)
            sp.wait_ge(spread, 16 * len(PARTS))


def unpack(nc, m):
    with ExitStack() as ctx:
        sb, ps, sem = makers(nc, ctx, "un")
        rec, part = sb("rec", [P, 2, TB, REC]), sb("part", [P, 2, TB, KP], BF16)
        rest, out = sb("rest", [P, TB, K17]), sb("out", [KP, 2, TB * P], BF16)
        turned = [ps("turned0", [KP, TB * P], BF16), ps("turned1", [KP, TB * P], BF16)]
        rec_in, saved = [sem("rec_in0"), sem("rec_in1")], [sem("saved0"), sem("saved1")]
        kept, step, part_s, turned_s, out_s = sem("kept"), sem("step"), sem("part_s"), sem("turned_s"), sem("out_s")
        total = NT // TB
        slots = m.slots.rearrange("(q n t) k -> n q t k", q=P, t=TB)
        feats = m.feat_t.rearrange("k (c n) -> c k n", n=TB * P)
        block = ctx.enter_context(nc.Block())

        @block.sync
        def _(sp):
            def turn(q, h):
                n = 2 * q + h
                wait(sp, kept, n - 1)
                wait(sp, part_s, n - 1)
                sp.dma_start(rec[:, h], slots[bass.ds(n, 1)].rearrange("o q t k -> q (o t) k")).then_inc(rec_in[h], 16)

            batches(sp, total, 3, 1, turn)

        @block.vector
        def _(dve):
            nc.vector.tensor_copy(m.ident_bf[:, :], m.ident[:, :]).then_inc(step, 1)

            def turn(q, h):
                n = 2 * q + h
                x, p = rec[:, h, :, 0:K17], part[:, h]
                dve.wait_ge(rec_in[h], (q + 1) * 16)
                wait(dve, turned_s, n - 1)
                nc.vector.tensor_copy(p[:, :, 0:K17], x).then_inc(step, 1)
                dve.wait_ge(step, 3 * n + 2)
                nc.vector.tensor_tensor(rest[:, :, :], x, p[:, :, 0:K17], ALU.subtract).then_inc(step, 1)
                nc.vector.tensor_copy(p[:, :, 5 * K17:6 * K17], p[:, :, 0:K17])
                dve.wait_ge(step, 3 * n + 3)
                nc.vector.tensor_copy(p[:, :, K17:2 * K17], rest[:, :, :]).then_inc(step, 1)
                dve.wait_ge(step, 3 * n + 4)
                nc.vector.tensor_tensor(p[:, :, 2 * K17:3 * K17], rest[:, :, :], p[:, :, K17:2 * K17], ALU.subtract)
                nc.vector.tensor_copy(p[:, :, 3 * K17:5 * K17], p[:, :, 0:2 * K17]).then_inc(part_s, 1)

            batches(dve, total, 3, 1, turn)

        @block.tensor
        def _(pe):
            pe.wait_ge(step, 1)

            def turn(q, h):
                n = 2 * q + h
                pe.wait_ge(part_s, n + 1)
                wait(pe, out_s, n - 1)
                for j in range(TB):
                    last = nc.tensor.transpose(turned[h][:, j * P:(j + 1) * P], part[:, h, j, :], m.ident_bf[:, :])
                last.then_inc(turned_s, 1)

            batches(pe, total, 3, 1, turn)

        @block.scalar
        def _(act):
            def turn(q, h):
                n = 2 * q + h
                act.wait_ge(rec_in[h], (q + 1) * 16)
                nc.scalar.copy(m.fields[:, bass.ds(n * TB, TB), 0:LOE], rec[:, h, :, FIELDS:FIELDS + LOE]).then_inc(kept, 1)
                act.wait_ge(turned_s, n + 1)
                wait(act, saved[h], q * 16)
                nc.scalar.copy(out[:, h], turned[h][:, :]).then_inc(out_s, 1)
                act.wait_ge(out_s, n + 1)
                act.dma_start(feats[bass.ds(n, 1)].rearrange("o k n -> k (o n)"), out[:, h]).then_inc(saved[h], 16)

            batches(act, total, 3, 1, turn)
            for h in range(2):
                act.wait_ge(saved[h], total // 2 * 16)


def segments(nc, m):
    g8 = NT // 8
    with ExitStack() as ctx:
        sb, ps, sem = makers(nc, ctx, "seg")
        turned, back = ps("turned", [g8, 8, P]), ps("back", [P, 8, P])
        rows, ends_t = sb("rows", [g8, 8, P]), sb("ends_t", [g8, 8, P])
        around = sb("around", [P, 3, NT])
        start, end, edge = sb("start", [P, NT]), sb("end", [P, NT]), sb("edge", [1, 2])
        lows_s, turned_s, rows_s, out_s, edge_s = sem("lows_s"), sem("turned_s"), sem("rows_s"), sem("out"), sem("edge_s")
        near, flags, saved, reread, back_s, step = sem("near"), sem("flags"), sem("saved"), sem("reread"), sem("back_s"), sem("step")
        slot = m.fields
        lows, lows_t = sb("lows", [g8, 8, P], FP16), ps("lows_t", [g8, 8, P])
        block = ctx.enter_context(nc.Block())

        @block.sync
        def _(sp):
            sp.wait_ge(edge_s, 1)
            sp.dma_start(m.slot_keys[None, 0:1], edge[:, 0:1]).then_inc(out_s, 16)
            sp.dma_start(m.slot_keys[None, SLOTS + 1:SLOTS + 2], edge[:, 1:2]).then_inc(out_s, 16)
            sp.wait_ge(rows_s, 1)
            sp.dma_start(m.slot_keys[1:SLOTS + 1].rearrange("(g t q) -> t g q", g=8, q=P), rows[:, :, :]).then_inc(out_s, 16)
            sp.wait_ge(lows_s, 1)
            sp.dma_start(m.low_row.rearrange("(g t q) -> t g q", g=8, q=P), lows[:, :, :]).then_inc(out_s, 16)
            sp.wait_ge(out_s, 64)
            for k in range(3):
                sp.dma_start(around[:, k, :], m.slot_keys[k:k + SLOTS].rearrange("(q c) -> q c", q=P)).then_inc(near, 16)
            sp.wait_ge(flags, 2)
            sp.dma_start(m.far_row.rearrange("(q c) -> q c", q=P), start[:, :]).then_inc(saved, 16)
            sp.dma_start(m.end_row.rearrange("(q c) -> q c", q=P), end[:, :]).then_inc(saved, 16)
            sp.wait_ge(saved, 32)
            sp.dma_start(ends_t[:, :, :], m.end_row.rearrange("(g t q) -> t g q", g=8, q=P)).then_inc(reread, 16)

        @block.tensor
        def _(pe):
            for g in range(8):
                last = nc.tensor.transpose(turned[:, g, :], slot[:, g * g8:(g + 1) * g8, KEY], m.ident[:, :])
            last.then_inc(turned_s, 1)
            for g in range(8):
                last = nc.tensor.transpose(lows_t[:, g, :], slot[:, g * g8:(g + 1) * g8, LO], m.ident[:, :])
            last.then_inc(turned_s, 1)
            pe.wait_ge(reread, 16)
            for g in range(8):
                last = nc.tensor.transpose(back[:, g, 0:g8], ends_t[:, g, :], m.ident[0:g8, 0:g8])
            last.then_inc(back_s, 1)

        @block.vector
        def _(dve):
            nc.vector.memset(edge[:, :], -5.0).then_inc(edge_s, 1)
            dve.wait_ge(turned_s, 1)
            nc.vector.tensor_copy(rows[:, :, :], turned[:, :, :]).then_inc(rows_s, 1)
            dve.wait_ge(turned_s, 2)
            nc.vector.tensor_copy(lows[:, :, :], lows_t[:, :, :]).then_inc(lows_s, 1)
            dve.wait_ge(near, 48)
            nc.vector.tensor_tensor(start[:, :], around[:, 1, :], around[:, 0, :], ALU.not_equal).then_inc(step, 1)
            nc.vector.tensor_tensor(end[:, :], around[:, 1, :], around[:, 2, :], ALU.not_equal).then_inc(flags, 1)
            dve.wait_ge(step, 1)
            nc.vector.tensor_scalar(start[:, :], start[:, :], FAR, None, ALU.mult).then_inc(flags, 1)
            dve.wait_ge(back_s, 1)
            loe = slot[:, :, LOE].rearrange("q (g t) -> q g t", g=8)
            low = slot[:, :, LO].rearrange("q (g t) -> q g t", g=8)
            nc.vector.scalar_tensor_tensor(loe, low, 1.0, back[:, :, 0:g8], ALU.add, ALU.mult).then_inc(step, 1)
            dve.wait_ge(step, 2)
            nc.vector.tensor_scalar(loe, loe, -1.0, None, ALU.add).then_inc(step, 1)


def normalise(nc, m, stage):
    with ExitStack() as ctx:
        sb, ps, sem = makers(nc, ctx, stage)
        mean, var, sq, eps = sb("mean", [P, NB]), sb("var", [P, NB]), sb("sq", [P, NB, D]), sb("eps", [P, 1])
        step, var_s, root_s = sem("step"), sem("var_s"), sem("root_s")
        block = ctx.enter_context(nc.Block())
        wide = [P, NB, D]

        @block.vector
        def _(dve):
            nc.vector.memset(eps[:, :], 1e-5).then_inc(var_s, 1)
            nc.vector.tensor_reduce(mean[:, :], m.x[:, :, :], AX.X, ALU.add).then_inc(step, 1)
            dve.wait_ge(step, 1)
            nc.vector.tensor_scalar(mean[:, :], mean[:, :], 1.0 / D, None, ALU.mult).then_inc(step, 1)
            dve.wait_ge(step, 2)
            nc.vector.tensor_tensor(m.h[:, :, :], m.x[:, :, :], mean[:, :, None].to_broadcast(wide), ALU.subtract).then_inc(step, 1)
            dve.wait_ge(step, 3)
            nc.vector.tensor_tensor(sq[:, :, :], m.h[:, :, :], m.h[:, :, :], ALU.mult).then_inc(step, 1)
            dve.wait_ge(step, 4)
            nc.vector.tensor_reduce(var[:, :], sq[:, :, :], AX.X, ALU.add).then_inc(var_s, 1)
            dve.wait_ge(root_s, 1)
            nc.vector.reciprocal(var[:, :], var[:, :]).then_inc(step, 1)
            dve.wait_ge(step, 5)
            nc.vector.tensor_tensor(m.h[:, :, :], m.h[:, :, :], var[:, :, None].to_broadcast(wide), ALU.mult).then_inc(step, 1)
            dve.wait_ge(step, 6)
            nc.vector.tensor_scalar(m.h[:, :, :], m.h[:, :, :], 0.0, None, ALU.max).then_inc(step, 1)

        @block.scalar
        def _(act):
            act.wait_ge(var_s, 2)
            nc.scalar.activation(var[:, :], var[:, :], ACT.Sqrt, bias=eps[:, 0:1], scale=1.0 / D).then_inc(root_s, 1)


def type_table(nc, m):
    with ExitStack() as ctx:
        sb, ps, sem = makers(nc, ctx, "typ")
        turned = ps("turned", [D, NP])
        turned_s, rows_s, one = sem("turned_s"), sem("rows_s"), sem("one")
        block = ctx.enter_context(nc.Block())

        @block.tensor
        def _(pe):
            for b in range(NB):
                last = nc.tensor.transpose(turned[:, b * P:(b + 1) * P], m.h[:, b, :], m.ident[:, :])
            last.then_inc(turned_s, 1)

        @block.scalar
        def _(act):
            act.wait_ge(one, 1)
            act.wait_ge(turned_s, 1)
            nc.scalar.copy(m.ht[0:D, :], turned[:, :]).then_inc(rows_s, 1)

        @block.vector
        def _(dve):
            nc.vector.memset(m.ht[:, :], 1.0).then_inc(one, 1)
    with ExitStack() as ctx:
        sb, ps, sem = makers(nc, ctx, "tab")
        table, prod = ps("table", [P, NP]), sb("prod", [P, NP])
        made, out_s, saved = sem("made"), sem("out_s"), sem("saved")
        block = ctx.enter_context(nc.Block())

        @block.tensor
        def _(pe):
            for b in range(NB):
                last = nc.tensor.matmul(table[:, b * P:(b + 1) * P], m.ht[0:D, b * P:(b + 1) * P], m.emb[:, :], start=True,
                                        stop=True, skip_group_check=True)
            last.then_inc(made, 1)

        @block.scalar
        def _(act):
            act.wait_ge(made, 1)
            nc.scalar.copy(prod[:, :], table[:, :]).then_inc(out_s, 1)

        @block.sync
        def _(sp):
            sp.wait_ge(out_s, 1)
            sp.dma_start(m.typed.rearrange("(b q t) d -> q b (t d)", q=P, t=8),
                         prod[:, :].rearrange("q (b c) -> q b c", b=NB)).then_inc(saved, 16)
            sp.wait_ge(saved, 16)


def slot_field(m, t0, n, k):
    return m.fields[:, bass.ds(t0, n), k]


def block_of(m, eng, t):
    return eng.value_load(m.blk[0:1, bass.ds(t, 1)], min_val=0, max_val=NB - 1)


def clear(nc, m, ap):
    rows, cols = ap.shape
    for c in range(0, cols, 512):
        w = min(512, cols - c)
        last = nc.tensor.matmul(ap[:, c:c + w], m.zero_row[0:1, 0:rows], m.zero_row[0:1, 0:w], start=True, stop=True,
                                skip_group_check=True)
    return last


def aggregate_typed(nc, m):
    with ExitStack() as ctx:
        sb, ps, sem = makers(nc, ctx, "at")
        pair = lambda n: [sem(n + "0"), sem(n + "1")]
        idx, hot = sb("idx", [P, 2, TB], I32), sb("hot", [P, 2, TB, P])
        ring, extra = sb("ring", [P, 2, TB, D]), sb("extra", [P, 2, TB, 2])
        sums = ps("sums", [P, 512])
        idx_s, hot_s, used = pair("idx_s"), pair("hot_s"), pair("used")
        gathered = [pair("gathered0"), pair("gathered1")]
        done = sem("done")
        block = ctx.enter_context(nc.Block())

        @block.vector
        def _(dve):
            with dve.Fori(0, IT) as i:
                for h in range(2):
                    t0 = (2 * i + h) * TB
                    dve.wait_ge(used[h], i + 1)
                    nc.vector.tensor_copy(idx[:, h, :], slot_field(m, t0, TB, TIX)).then_inc(idx_s[h], 1)
                    nc.vector.tensor_copy(extra[:, h, :, 0], slot_field(m, t0, TB, WGT))
                    nc.vector.tensor_tensor(hot[:, h], slot_field(m, t0, TB, LO)[:, :, None].to_broadcast([P, TB, P]),
                                            m.iota_row[:, None, :].to_broadcast([P, TB, P]), ALU.is_equal).then_inc(hot_s[h], 1)
            for h in range(2):
                dve.wait_ge(used[h], IT + 1)
            nc.vector.tensor_copy(m.sums[:, :, :], sums[:, 0:NB * 20].rearrange("q (b c) -> q b c", b=NB)).then_inc(done, 1)

        @block.gpsimd
        def _(pool):
            with pool.Fori(0, IT) as i:
                for h in range(2):
                    pool.wait_ge(idx_s[h], i + 1)
                    pool.sem_inc(m.pool_passed, 1)
                    for j in range(TB):
                        pool.indirect_dma_start(ring[:, h, j, :], None, m.typed,
                                                bass.IndirectOffsetOnAxis(ap=idx[:, h, j:j + 1], axis=0)
                                                ).then_inc(gathered[h][j // (TB // 2)], 16)

        @block.tensor
        def _(pe):
            clear(nc, m, sums[:, :])
            for h in range(2):
                pe.sem_inc(used[h], 1)
            with pe.Fori(0, IT) as i:
                for h in range(2):
                    t0 = (2 * i + h) * TB
                    pe.wait_ge(hot_s[h], i + 1)
                    for j in range(TB):
                        if j % (TB // 2) == 0:
                            pe.wait_ge(gathered[h][j // (TB // 2)], (i + 1) * 16 * (TB // 2))
                        b = block_of(m, pe, t0 + j)
                        nc.tensor.matmul(sums[:, bass.ds(b * 20, D)], hot[:, h, j, :], ring[:, h, j, :], start=False, stop=True,
                                         skip_group_check=True)
                        last = nc.tensor.matmul(sums[:, bass.ds(b * 20 + D, 1)], hot[:, h, j, :], extra[:, h, j, 0:1], start=False,
                                                stop=True, skip_group_check=True)
                    last.then_inc(used[h], 1)


def gru(nc, m):
    with ExitStack() as ctx:
        sb, ps, sem = makers(nc, ctx, "gru")
        turned = ps("turned", [D, NP])
        mt = m.mt
        turned_s, one = sem("turned_s"), sem("one")
        block = ctx.enter_context(nc.Block())

        @block.tensor
        def _(pe):
            for b in range(NB):
                last = nc.tensor.transpose(turned[:, b * P:(b + 1) * P], m.sums[:, b, 0:D], m.ident[:, :])
            last.then_inc(turned_s, 1)

        @block.vector
        def _(dve):
            nc.vector.memset(mt[:, :], 1.0).then_inc(one, 1)
            dve.wait_ge(one, 1)
            dve.wait_ge(turned_s, 1)
            nc.vector.tensor_copy(mt[0:D, :], turned[:, :]).then_inc(one, 1)
    with ExitStack() as ctx:
        sb, ps, sem = makers(nc, ctx, "gat")
        gates = ps("gates", [P, 4, 8, 4 * D])
        rz, hn, tmp = sb("rz", [P, NB, 2 * D]), sb("hn", [P, NB, D]), sb("tmp", [P, NB, D])
        pos, safe = sb("pos", [P, NB]), sb("safe", [P, NB])
        made, act_s, step = sem("made"), sem("act_s"), sem("step")
        block = ctx.enter_context(nc.Block())
        gv = gates[:, :, :, :].rearrange("q a b c -> q (a b) c")[:, 0:NB, :]

        @block.tensor
        def _(pe):
            for b in range(NB):
                o = gates[:, b // 8, b % 8, :]
                nc.tensor.matmul(o, mt_block(m.mt, b), m.gru_i[:, :], start=b % 8 == 0, stop=False, skip_group_check=True)
                last = nc.tensor.matmul(o, mt_block(m.ht, b), m.gru_h[:, :], start=False, stop=True, skip_group_check=True)
            last.then_inc(made, 1)

        @block.scalar
        def _(act):
            act.wait_ge(made, 1)
            nc.scalar.activation(rz[:, :, :], gv[:, :, 0:2 * D], ACT.Sigmoid).then_inc(act_s, 1)
            act.wait_ge(step, 2)
            nc.scalar.activation(hn[:, :, :], hn[:, :, :], ACT.Tanh).then_inc(act_s, 1)
            act.wait_ge(step, 8)
            nc.scalar.activation(safe[:, :], safe[:, :], ACT.Sqrt).then_inc(act_s, 1)

        @block.vector
        def _(dve):
            dve.wait_ge(act_s, 1)
            nc.vector.tensor_tensor(hn[:, :, :], rz[:, :, 0:D], gv[:, :, 3 * D:4 * D], ALU.mult).then_inc(step, 1)
            dve.wait_ge(step, 1)
            nc.vector.tensor_tensor(hn[:, :, :], hn[:, :, :], gv[:, :, 2 * D:3 * D], ALU.add).then_inc(step, 1)
            dve.wait_ge(act_s, 2)
            nc.vector.tensor_tensor(tmp[:, :, :], m.h[:, :, :], hn[:, :, :], ALU.subtract).then_inc(step, 1)
            nc.vector.tensor_tensor(m.x[:, :, :], m.x[:, :, :], hn[:, :, :], ALU.add).then_inc(step, 1)
            nc.vector.tensor_scalar(safe[:, :], m.sums[:, :, D], 2.0, None, ALU.add).then_inc(step, 1)
            dve.wait_ge(step, 5)
            nc.vector.tensor_scalar(pos[:, :], safe[:, :], 0.0, None, ALU.is_gt).then_inc(step, 1)
            dve.wait_ge(step, 6)
            nc.vector.scalar_tensor_tensor(safe[:, :], safe[:, :], -1.0, pos[:, :], ALU.add, ALU.mult).then_inc(step, 1)
            dve.wait_ge(step, 7)
            nc.vector.tensor_scalar(safe[:, :], safe[:, :], 1.0, None, ALU.add).then_inc(step, 1)
            nc.vector.tensor_tensor(tmp[:, :, :], tmp[:, :, :], rz[:, :, D:2 * D], ALU.mult).then_inc(step, 1)
            dve.wait_ge(step, 9)
            nc.vector.tensor_tensor(m.x[:, :, :], m.x[:, :, :], tmp[:, :, :], ALU.add).then_inc(step, 1)
            dve.wait_ge(act_s, 3)
            nc.vector.reciprocal(safe[:, :], safe[:, :]).then_inc(step, 1)
            dve.wait_ge(step, 11)
            nc.vector.tensor_tensor(m.dinv[:, :], safe[:, :], pos[:, :], ALU.mult).then_inc(step, 1)


def mt_block(t, b):
    return t[:, b * P:(b + 1) * P]


HB = 4
W40 = D + 3 * D // 2
HT = NT // HB


def batches(eng, total, first, last, body):
    assert (total - first - last) % 2 == 0 and first % 2 == 1
    for n in range(first):
        body(n // 2, n % 2)
    with eng.Fori(0, (total - first - last) // 2) as i:
        body(i + first // 2, 1)
        body(i + first // 2 + 1, 0)
    for n in range(total - last, total):
        body(n // 2, n % 2)


def inside(n, total=HT):
    return not isinstance(n, int) or 0 <= n < total


def wait(eng, sem, value):
    if not isinstance(value, int) or value > 0:
        eng.wait_ge(sem, value)


def one_hot(nc, m, field, n, out):
    return nc.vector.tensor_tensor(out, slot_field(m, n * HB, HB, field)[:, :, None].to_broadcast([P, HB, P]),
                                   m.iota_row[:, None, :].to_broadcast([P, HB, P]), ALU.is_equal)


def gather(nc, m, pool, table, idx, ring, idx_s, gathered, tiles, turns):
    with pool.Fori(0, turns) as i:
        for h in range(2):
            pool.wait_ge(idx_s, 2 * i + h + 1)
            pool.sem_inc(m.pool_passed, 1)
            for j in range(tiles):
                part = gathered[h][j * len(gathered[h]) // tiles]
                pool.indirect_dma_start(ring[:, h, j, :], None, table,
                                        bass.IndirectOffsetOnAxis(ap=idx[:, h, j:j + 1], axis=0)).then_inc(part, 16)


def attention_rows(nc, m):
    with ExitStack() as ctx:
        sb, ps, sem = makers(nc, ctx, "ar")
        row, rest = sb("row", [P, NB, W40]), sb("rest", [P, NB, D])
        step, saved = sem("step"), sem("saved")
        parts = row[:, :, :].bitcast(BF16)[:, :, 2 * D:2 * W40]
        block = ctx.enter_context(nc.Block())

        @block.vector
        def _(dve):
            nc.vector.tensor_copy(row[:, :, 0:D], m.h[:, :, :])
            split(nc, dve, step, m.h[:, :, :], rest[:, :, :], [parts[:, :, k * D:(k + 1) * D] for k in range(3)])

        @block.sync
        def _(sp):
            sp.wait_ge(step, 4)
            sp.dma_start(m.node40.rearrange("(b q) d -> q b d", q=P), row[:, :, :]).then_inc(saved, 16)
            sp.wait_ge(saved, 16)


def split(nc, dve, step, x, rest, parts):
    nc.vector.tensor_copy(parts[0], x).then_inc(step, 1)
    dve.wait_ge(step, 1)
    nc.vector.tensor_tensor(rest, x, parts[0], ALU.subtract).then_inc(step, 1)
    dve.wait_ge(step, 2)
    nc.vector.tensor_copy(parts[1], rest).then_inc(step, 1)
    dve.wait_ge(step, 3)
    nc.vector.tensor_tensor(parts[2], rest, parts[1], ALU.subtract).then_inc(step, 1)


def segment_max(nc, m):
    with ExitStack() as ctx:
        sb, ps, sem = makers(nc, ctx, "mx")
        idx, ring = sb("idx", [P, 2, HB], I32), sb("ring", [P, 2, HB, W40])
        src_t, src_w = sb("src_t", [3 * D, 2, 512], BF16), sb("src_w", [P, 2, 512])
        feat, far, hot = sb("feat", [KP, 2, 512], BF16), sb("far", [P, 2, 512]), sb("hot", [P, 2, HB, P])
        logit, run, run_e = sb("logit", [P, 2, 512]), sb("run", [P, 2, 2, 512]), sb("run_e", [P, 2, HB, 256])
        src_ps, wide, net = ps("src_ps", [3 * D, 512], BF16), ps("wide", [P, 2, 512]), ps("net", [P, 2, 512])
        back, best = [ps("back0", [P, 2, 256]), ps("back1", [P, 2, 256])], ps("best", [P, 2, 256])
        gathered, loaded = [[sem("gathered0")], [sem("gathered1")]], [sem("loaded0"), sem("loaded1")]
        names = ("idx_s", "src_s", "src_t_s", "wide_s", "src_w_s", "net_s", "logit_s", "run_s", "back_s", "run_e_s", "hot_s",
                 "best_s", "kept", "cleared", "held")
        (idx_s, src_s, src_t_s, wide_s, src_w_s, net_s, logit_s, run_s, back_s, run_e_s, hot_s, best_s, kept, cleared,
         held) = map(sem, names)
        block = ctx.enter_context(nc.Block())
        ring_bf = ring[:, :, :, :].bitcast(BF16)

        @block.sync
        def _(sp):
            far_rows = m.far_row.rearrange("(c n) -> c n", n=512)
            feats = m.feat_t.rearrange("k (c n) -> k c n", n=512)

            def load(q, h):
                n = 2 * q + h
                wait(sp, run_s, n - 1)
                sp.dma_start(far[:, h], far_rows[bass.ds(n, 1)].to_broadcast([P, 512])).then_inc(loaded[h], 16)
                sp.dma_start(feat[:, h], feats[:, bass.ds(n, 1), :].rearrange("k o n -> k (o n)")).then_inc(loaded[h], 16)

            batches(sp, HT, 3, 1, load)

        @block.gpsimd
        def _(pool):
            gather(nc, m, pool, m.node40, idx, ring, idx_s, gathered, HB, HT // 2)

        @block.vector
        def _(dve):
            def indices(n, h):
                nc.vector.tensor_copy(idx[:, h, :], slot_field(m, n * HB, HB, SRC)).then_inc(idx_s, 1)

            def keep(n):
                dve.wait_ge(best_s, n + 1)
                for k in range(2):
                    b = block_of(m, dve, n * HB + 2 * k)
                    row = m.top[:, bass.ds(b, 1), :].rearrange("q o c -> q (o c)")
                    wait(dve, kept, 2 * n + k)
                    nc.vector.tensor_tensor(row, row, best[:, k, :], ALU.subtract).then_inc(kept, 1)

            def turn(q, h):
                n = 2 * q + h
                if inside(n + 2):
                    dve.wait_ge(held, n + 1)
                    indices(n + 2, h)
                dve.wait_ge(net_s, n + 1)
                dve.wait_ge(src_w_s, n + 1)
                wait(dve, run_s, n)
                nc.vector.tensor_tensor(logit[:, :, :], net[:, :, :], src_w[:, :, :], ALU.mult).then_inc(logit_s, 1)
                dve.wait_ge(loaded[h], (q + 1) * 32)
                dve.wait_ge(logit_s, n + 1)
                for c in range(2):
                    before = run[:, 1 - h, c, 511:512] if inside(n - 1) else 0.0
                    last = nc.vector.tensor_tensor_scan(run[:, h, c, :], far[:, h, :], logit[:, c, :], before, ALU.add, ALU.max)
                last.then_inc(run_s, 1)
                one_hot(nc, m, LOE, n, hot[:, h]).then_inc(hot_s, 1)
                if inside(n - 1):
                    keep(n - 1)

            nc.vector.memset(m.top[:, :, :], 0.0).then_inc(cleared, 1)
            dve.wait_ge(cleared, 1)
            for h in range(2):
                indices(h, h)
            batches(dve, HT, 3, 3, turn)
            keep(HT - 1)

        @block.scalar
        def _(act):
            def sources(q, h):
                n = 2 * q + h
                act.wait_ge(src_s, n + 1)
                nc.scalar.copy(src_t[:, h], src_ps[:, :]).then_inc(src_t_s, 1)
                nc.scalar.copy(m.held[:, bass.ds(n * HB, HB), :], ring[:, h, :, 0:D]).then_inc(held, 1)

            def widened(n):
                act.wait_ge(wide_s, n + 1)
                wait(act, logit_s, n)
                nc.scalar.copy(src_w[:, :, :], wide[:, :, :]).then_inc(src_w_s, 1)

            def turn(q, h):
                n = 2 * q + h
                if inside(n + 1):
                    sources(q + h, 1 - h)
                    widened(n + 1)
                for k in range(2):
                    act.wait_ge(back_s, 2 * n + k + 1)
                    nc.scalar.copy(run_e[:, h, 2 * k:2 * k + 2, :], back[k][:, :, :]).then_inc(run_e_s, 1)

            sources(0, 0)
            widened(0)
            batches(act, HT, 1, 1, turn)

        @block.tensor
        def _(pe):
            def sources(q, h):
                n = 2 * q + h
                pe.wait_ge(gathered[h][0], (q + 1) * 16 * HB)
                wait(pe, src_t_s, n)
                pe.sem_inc(m.pe_passed, 1)
                for j in range(HB):
                    last = nc.tensor.transpose(src_ps[:, j * P:(j + 1) * P], ring_bf[:, h, j, 2 * D:2 * W40], m.ident_bf[:, :])
                last.then_inc(src_s, 1)

            def logits(q, h):
                n = 2 * q + h
                pe.wait_ge(src_t_s, n + 1)
                wait(pe, src_w_s, n)
                for c in range(2):
                    last = nc.tensor.matmul(wide[:, c, :], m.widen[:, c * P:(c + 1) * P], src_t[:, h, :], start=True, stop=True)
                last.then_inc(wide_s, 1)
                pe.wait_ge(loaded[h], (q + 1) * 32)
                wait(pe, logit_s, n)
                for c in range(2):
                    last = nc.tensor.matmul(net[:, c, :], m.w6[:, 256 + c * P:256 + (c + 1) * P], feat[:, h, :], start=True, stop=True)
                last.then_inc(net_s, 1)

            def turn(q, h):
                n = 2 * q + h
                if inside(n + 1):
                    sources(q + h, 1 - h)
                    logits(q + h, 1 - h)
                pe.wait_ge(run_s, n + 1)
                for k in range(2):
                    wait(pe, run_e_s, 2 * n + k - 1)
                    for j in range(2):
                        for c in range(2):
                            last = nc.tensor.transpose(back[k][:, j, c * P:(c + 1) * P],
                                                       run[:, h, c, (2 * k + j) * P:(2 * k + j + 1) * P], m.ident[:, :])
                    last.then_inc(back_s, 1)
                pe.wait_ge(hot_s, n + 1)
                wait(pe, kept, 2 * n)
                for k in range(2):
                    pe.wait_ge(run_e_s, 2 * n + k + 1)
                    for j in range(2):
                        last = nc.tensor.matmul(best[:, k, :], hot[:, h, 2 * k + j, :], run_e[:, h, 2 * k + j, :], start=j == 0,
                                                stop=j == 1, skip_group_check=True)
                last.then_inc(best_s, 1)

            sources(0, 0)
            logits(0, 0)
            batches(pe, HT, 1, 1, turn)


def split_top(nc, m):
    with ExitStack() as ctx:
        sb, ps, sem = makers(nc, ctx, "spt")
        step = sem("step")
        block = ctx.enter_context(nc.Block())

        @block.vector
        def _(dve):
            nc.vector.tensor_copy(m.top3[:, :, 0, :], m.top[:, :, :]).then_inc(step, 1)
            dve.wait_ge(step, 1)
            nc.vector.tensor_tensor(m.top[:, :, :], m.top[:, :, :], m.top3[:, :, 0, :], ALU.subtract).then_inc(step, 1)
            dve.wait_ge(step, 2)
            nc.vector.tensor_copy(m.top3[:, :, 1, :], m.top[:, :, :]).then_inc(step, 1)
            dve.wait_ge(step, 3)
            nc.vector.tensor_tensor(m.top3[:, :, 2, :], m.top[:, :, :], m.top3[:, :, 1, :], ALU.subtract).then_inc(step, 1)


def soft_sums(nc, m):
    with ExitStack() as ctx:
        sb, ps, sem = makers(nc, ctx, "sm")
        feat, low = sb("feat", [KP, 2, 512], BF16), sb("low", [P, 2, 512], FP16)
        hot_t, hot = sb("hot_t", [P, 2, 512], BF16), sb("hot", [P, 2, HB, P])
        arg, mess = sb("arg", [P, 2, 2, 256]), sb("mess", [P, 2, 2, 256])
        both = sb("both", [P, 2, 2, 2, 256])
        net_a, net_m, tops, sums = ([ps(f"{n}{k}", [P, 2, 256]) for k in range(2)] for n in ("net_a", "net_m", "tops", "sums"))
        loaded = [sem("loaded0"), sem("loaded1")]
        names = ("hot_t_s", "hot_s", "net_s", "arg_s", "arg2_s", "exp_s", "mess_s", "both_s", "sums_s", "kept", "cleared")
        hot_t_s, hot_s, net_s, arg_s, arg2_s, exp_s, mess_s, both_s, sums_s, kept, cleared = map(sem, names)
        block = ctx.enter_context(nc.Block())

        @block.sync
        def _(sp):
            low_rows = m.low_row.rearrange("(c n) -> c n", n=512)
            feats = m.feat_t.rearrange("k (c n) -> k c n", n=512)

            def load(q, h):
                n = 2 * q + h
                wait(sp, net_s, 2 * (n - 1))
                sp.dma_start(low[:, h], low_rows[bass.ds(n, 1)].to_broadcast([P, 512])).then_inc(loaded[h], 16)
                sp.dma_start(feat[:, h], feats[:, bass.ds(n, 1), :].rearrange("k o n -> k (o n)")).then_inc(loaded[h], 16)

            batches(sp, HT, 3, 1, load)

        def by_source(n, k):
            return m.held[:, bass.ds(n * HB + 2 * k, 2), :][:, :, :, None].to_broadcast([P, 2, D, D])

        def four(ap):
            return ap.rearrange("q t (i o) -> q t i o", o=D)

        @block.vector
        def _(dve):
            def far_hot(q, h):
                dve.wait_ge(loaded[h], (q + 1) * 32)
                wait(dve, net_s, 2 * (2 * q + h - 1))
                nc.vector.tensor_scalar(hot_t[:, h], low[:, h], m.iota_col[:, 0:1], None, ALU.is_equal).then_inc(hot_t_s, 1)

            def spread_hot(n, h):
                wait(dve, sums_s, 2 * (n - 1))
                one_hot(nc, m, LO, n, hot[:, h]).then_inc(hot_s, 1)

            def enter(n, k):
                r = 2 * n + k
                dve.wait_ge(net_s, r + 1)
                wait(dve, both_s, r - 1)
                nc.vector.tensor_tensor(four(arg[:, k]), four(net_a[k][:, :, :]), by_source(n, k), ALU.mult).then_inc(arg_s, 1)
                nc.vector.tensor_tensor(four(mess[:, k]), four(net_m[k][:, :, :]), by_source(n, k), ALU.mult).then_inc(mess_s, 1)
                dve.wait_ge(arg_s, r + 1)
                nc.vector.tensor_tensor(arg[:, k], arg[:, k], tops[k][:, :, :], ALU.add).then_inc(arg2_s, 1)

            def add(n, k):
                r = 2 * n + k
                b = block_of(m, dve, n * HB + 2 * k)
                row = m.acc[:, bass.ds(b, 1), :].rearrange("q o c -> q (o c)")
                dve.wait_ge(sums_s, r + 1)
                wait(dve, kept, r)
                nc.vector.tensor_tensor(row, row, sums[k][:, :, :].rearrange("q a c -> q (a c)"), ALU.add).then_inc(kept, 1)

            def turn(q, h):
                n = 2 * q + h
                enter(n, 0)
                if inside(n - 1):
                    add(n - 1, 0)
                if inside(n + 1):
                    far_hot(q + h, 1 - h)
                enter(n, 1)
                if inside(n - 1):
                    add(n - 1, 1)
                if inside(n + 1):
                    spread_hot(n + 1, 1 - h)

            nc.vector.memset(m.acc[:, :, :], 0.0).then_inc(cleared, 1)
            dve.wait_ge(cleared, 1)
            far_hot(0, 0)
            spread_hot(0, 0)
            batches(dve, HT, 3, 1, turn)
            add(HT - 1, 0)
            add(HT - 1, 1)

        @block.scalar
        def _(act):
            def turn(q, h):
                n = 2 * q + h
                for k in range(2):
                    r = 2 * n + k
                    act.wait_ge(arg2_s, r + 1)
                    wait(act, sums_s, r - 1)
                    nc.scalar.activation(both[:, k, :, 0, :], arg[:, k], ACT.Exp).then_inc(exp_s, 1)

            batches(act, HT, 1, 1, turn)

        @block.gpsimd
        def _(pool):
            with pool.Fori(0, HT) as i:
                for k in range(2):
                    r = 2 * i + k
                    pool.wait_ge(mess_s, r + 1)
                    pool.wait_ge(exp_s, r + 1)
                    nc.gpsimd.tensor_tensor(both[:, k, :, 1, :], mess[:, k], both[:, k, :, 0, :], ALU.mult).then_inc(both_s, 1)

        @block.tensor
        def _(pe):
            def networks(q, h, k):
                n = 2 * q + h
                r = 2 * n + k
                if k == 0:
                    pe.wait_ge(loaded[h], (q + 1) * 32)
                    pe.wait_ge(hot_t_s, n + 1)
                b = block_of(m, pe, n * HB + 2 * k)
                wait(pe, arg2_s, r - 1)
                for j in range(2):
                    f = feat[:, h, (2 * k + j) * P:(2 * k + j + 1) * P]
                    nc.tensor.matmul(net_a[k][:, j, :], f, m.w6[:, 256:512], start=True, stop=True, skip_group_check=True)
                    nc.tensor.matmul(net_m[k][:, j, :], f, m.w6[:, 0:256], start=True, stop=True, skip_group_check=True)
                for j in range(2):
                    for part in range(3):
                        last = nc.tensor.matmul(tops[k][:, j, :], hot_t[:, h, (2 * k + j) * P:(2 * k + j + 1) * P],
                                                m.top3[:, bass.ds(b, 1), part, :].rearrange("q o c -> q (o c)"), start=part == 0,
                                                stop=part == 2, skip_group_check=True)
                last.then_inc(net_s, 1)

            def spread(n, h, k):
                r = 2 * n + k
                if k == 0:
                    pe.wait_ge(hot_s, n + 1)
                pe.wait_ge(both_s, r + 1)
                wait(pe, kept, r - 1)
                for j in range(2):
                    last = nc.tensor.matmul(sums[k][:, :, :].rearrange("q a c -> q (a c)"), hot[:, h, 2 * k + j, :],
                                            both[:, k, j].rearrange("q a c -> q (a c)"), start=j == 0, stop=j == 1)
                last.then_inc(sums_s, 1)

            def turn(q, h):
                n = 2 * q + h
                for k in range(2):
                    if inside(n + 1):
                        networks(q + h, 1 - h, k)
                    spread(n, h, k)

            for k in range(2):
                networks(0, 0, k)
            batches(pe, HT, 1, 1, turn)


def attend(nc, m):
    with ExitStack() as ctx:
        sb, ps, sem = makers(nc, ctx, "att")
        none, total = sb("none", [P, NB, 256]), sb("total", [P, NB, D])
        step = sem("step")
        den, num = m.acc[:, :, 0:256], m.acc[:, :, 256:512]
        block = ctx.enter_context(nc.Block())

        @block.vector
        def _(dve):
            nc.vector.tensor_scalar(none[:, :, :], den, 0.0, None, ALU.is_equal).then_inc(step, 1)
            dve.wait_ge(step, 1)
            nc.vector.tensor_tensor(none[:, :, :], none[:, :, :], den, ALU.add).then_inc(step, 1)
            dve.wait_ge(step, 2)
            nc.vector.reciprocal(none[:, :, :], none[:, :, :]).then_inc(step, 1)
            dve.wait_ge(step, 3)
            nc.vector.tensor_tensor(none[:, :, :], none[:, :, :], num, ALU.mult).then_inc(step, 1)
            dve.wait_ge(step, 4)
            nc.vector.tensor_reduce(total[:, :, :], none[:, :, :].rearrange("q b (i o) -> q b o i", i=D), AX.X, ALU.add).then_inc(step, 1)
            dve.wait_ge(step, 5)
            nc.vector.tensor_tensor(m.x[:, :, :], m.x[:, :, :], total[:, :, :], ALU.add).then_inc(step, 1)


def convolve(nc, m, stage, table, width):
    with ExitStack() as ctx:
        sb, ps, sem = makers(nc, ctx, stage)
        idx, hot = sb("idx", [P, 2, TB], I32), sb("hot", [P, 2, TB, P])
        ring = sb("ring", [P, 2, TB, width])
        sums = ps("sums", [width, NP])
        gathered = [[sem(f"gathered{h}{part}") for part in range(2)] for h in range(2)]
        idx_s, step, hot_s, used, done = sem("idx_s"), sem("step"), sem("hot_s"), sem("used"), sem("done")
        block = ctx.enter_context(nc.Block())
        total = NT // TB

        @block.vector
        def _(dve):
            def turn(q, h):
                n = 2 * q + h
                wait(dve, used, n - 1)
                nc.vector.tensor_copy(idx[:, h, :], slot_field(m, n * TB, TB, SRC)).then_inc(idx_s, 1)
                nc.vector.tensor_tensor(hot[:, h], slot_field(m, n * TB, TB, LO)[:, :, None].to_broadcast([P, TB, P]),
                                        m.iota_row[:, None, :].to_broadcast([P, TB, P]), ALU.is_equal).then_inc(step, 1)
                dve.wait_ge(step, n + 1)
                nc.vector.tensor_tensor(hot[:, h], slot_field(m, n * TB, TB, WGT)[:, :, None].to_broadcast([P, TB, P]),
                                        hot[:, h], ALU.mult).then_inc(hot_s, 1)

            batches(dve, total, 3, 1, turn)
            dve.wait_ge(used, total)
            nc.vector.tensor_tensor(m.agg[0:width, :], sums[:, :], m.dinv_row[0:width, :], ALU.mult).then_inc(done, 1)

        @block.gpsimd
        def _(pool):
            gather(nc, m, pool, table, idx, ring, idx_s, gathered, TB, total // 2)

        @block.tensor
        def _(pe):
            for b in range(NB):
                nc.tensor.matmul(sums[:, b * P:(b + 1) * P], m.g[:, b, 0:width], m.twice[:, :], start=b % 4 == 0, stop=True,
                                 skip_group_check=True)
            with pe.Fori(0, total // 2) as i:
                for h in range(2):
                    n = 2 * i + h
                    pe.wait_ge(hot_s, n + 1)
                    for j in range(TB):
                        if j % (TB // 2) == 0:
                            pe.wait_ge(gathered[h][j // (TB // 2)], (i + 1) * 16 * (TB // 2))
                        b = block_of(m, pe, n * TB + j)
                        last = nc.tensor.matmul(sums[:, bass.ds(b * P, P)], ring[:, h, j, :], hot[:, h, j, :], start=False,
                                                stop=True, skip_group_check=True)
                    last.then_inc(used, 1)


def dense(nc, m, stage, k):
    with ExitStack() as ctx:
        sb, ps, sem = makers(nc, ctx, stage)
        out = ps("out", [P, NP])
        made, done = sem("made"), sem("done")
        block = ctx.enter_context(nc.Block())

        @block.tensor
        def _(pe):
            for c in range(0, NP, 512):
                w = min(512, NP - c)
                last = nc.tensor.matmul(out[:, c:c + w], m.conv_w[k][:, :], m.agg[0:D, c:c + w], start=True, stop=True)
            last.then_inc(made, 1)

        @block.scalar
        def _(act):
            act.wait_ge(made, 1)
            nc.scalar.activation(m.hidden[:, :], out[:, :], ACT.Relu, bias=m.conv_b[k][:, 0:1]).then_inc(done, 1)


def project(nc, m, stage, k, table, width, activate):
    with ExitStack() as ctx:
        sb, ps, sem = makers(nc, ctx, stage)
        out = ps("out", [P, NB, width])
        made, scaled, saved, ready = sem("made"), sem("scaled"), sem("saved"), sem("ready")
        block = ctx.enter_context(nc.Block())

        @block.scalar
        def _(act):
            if activate:
                nc.scalar.activation(m.hidden[:, :], m.agg[:, :], ACT.Relu, bias=m.conv_b[k - 1][:, 0:1]).then_inc(ready, 1)

        @block.tensor
        def _(pe):
            if activate:
                pe.wait_ge(ready, 1)
            for b in range(NB):
                last = nc.tensor.matmul(out[:, b, :], m.hidden[:, b * P:(b + 1) * P], m.conv_w[k][:, :], start=True, stop=True,
                                        skip_group_check=True)
            last.then_inc(made, 1)

        @block.vector
        def _(dve):
            dve.wait_ge(made, 1)
            nc.vector.tensor_tensor(m.g[:, :, 0:width], out[:, :, :], m.dinv[:, :, None].to_broadcast([P, NB, width]),
                                    ALU.mult).then_inc(scaled, 1)

        @block.sync
        def _(sp):
            sp.wait_ge(scaled, 1)
            sp.dma_start(table.rearrange("(b q) d -> q b d", q=P), m.g[:, :, 0:width]).then_inc(saved, 16)
            sp.wait_ge(saved, 16)


def close_convolutions(nc, m):
    with ExitStack() as ctx:
        sb, ps, sem = makers(nc, ctx, "clo")
        out = ps("out", [P, 512])
        ready, made, done = sem("ready"), sem("made"), sem("done")
        block = ctx.enter_context(nc.Block())

        @block.scalar
        def _(act):
            nc.scalar.activation(m.hidden[0:D, :], m.agg[0:D, :], ACT.Identity, bias=m.conv_b[3][:, 0:1]).then_inc(ready, 1)

        @block.tensor
        def _(pe):
            pe.wait_ge(ready, 1)
            for b in range(NB):
                last = nc.tensor.transpose(out[:, b * D:(b + 1) * D], m.hidden[0:D, b * P:(b + 1) * P], m.ident[0:D, 0:D])
            last.then_inc(made, 1)

        @block.vector
        def _(dve):
            dve.wait_ge(made, 1)
            nc.vector.tensor_tensor(m.x[:, :, :], m.x[:, :, :], out[:, 0:NB * D].rearrange("q (b d) -> q b d", d=D),
                                    ALU.add).then_inc(done, 1)


def node_factors(nc, m):
    with ExitStack() as ctx:
        sb, ps, sem = makers(nc, ctx, "nf")
        saved, loaded, scaled = sem("saved"), sem("loaded"), sem("scaled")
        block = ctx.enter_context(nc.Block())

        @block.vector
        def _(dve):
            nc.vector.tensor_scalar(m.twice[:, :], m.ident[:, :], 2.0, None, ALU.mult).then_inc(scaled, 1)
            nc.vector.tensor_tensor(m.g[:, :, 0:D], m.h[:, :, :], m.dinv[:, :, None].to_broadcast([P, NB, D]), ALU.mult).then_inc(scaled, 1)

        @block.sync
        def _(sp):
            with nc.allow_non_contiguous_dma(reason="one factor to a node"):
                sp.dma_start(m.dinv_dram.rearrange("(b q) -> q b", q=P), m.dinv[:, :]).then_inc(saved, 16)
            sp.wait_ge(saved, 16)
            sp.dma_start(m.dinv_row[:, :], m.dinv_dram[None, :].to_broadcast([P, NP])).then_inc(loaded, 16)
            sp.wait_ge(scaled, 2)
            sp.dma_start(m.node16.rearrange("(b q) d -> q b d", q=P), m.g[:, :, 0:D]).then_inc(saved, 16)
            sp.wait_ge(saved, 32)
            sp.wait_ge(loaded, 16)


HW = D + 4


def sheaf_rows(nc, m):
    with ExitStack() as ctx:
        sb, ps, sem = makers(nc, ctx, "shr")
        wide, rest = sb("wide", [P, NB, HW]), sb("rest", [P, NB, HW])
        filled, step, saved = sem("filled"), sem("step"), sem("saved")
        block = ctx.enter_context(nc.Block())

        @block.vector
        def _(dve):
            nc.vector.memset(wide[:, :, :], 0.0).then_inc(filled, 1)
            dve.wait_ge(filled, 1)
            nc.vector.tensor_copy(wide[:, :, 0:D], m.h[:, :, :]).then_inc(filled, 1)
            nc.vector.tensor_copy(wide[:, :, D], m.dis[:, :]).then_inc(filled, 1)
            dve.wait_ge(filled, 3)
            split(nc, dve, step, wide[:, :, :], rest[:, :, :], [m.wide3[:, :, k, :] for k in range(3)])

        @block.sync
        def _(sp):
            sp.wait_ge(filled, 3)
            sp.dma_start(m.node20.rearrange("(b q) d -> q b d", q=P), wide[:, :, :]).then_inc(saved, 16)
            sp.wait_ge(saved, 16)


def sheaf_messages(nc, m):
    total = NT // TB
    with ExitStack() as ctx:
        sb, ps, sem = makers(nc, ctx, "sh")
        idx, ring, low = sb("idx", [P, 2, TB], I32), sb("ring", [P, 2, TB, HW]), sb("low", [P, 2, TB * P], FP16)
        hot, hot_t = sb("hot", [P, 2, TB, P], BF16), sb("hot_t", [P, TB * P], BF16)
        ends, ends_t, hid = sb("ends", [P, 2, TB, 2, D]), sb("ends_t", [2 * D, TB * P]), sb("hid", [P, TB * P])
        vec, sq, swap = sb("vec", [P, TB, 2, D]), sb("sq", [P, TB, 2, D]), sb("swap", [P, TB, 2, D])
        norm, dot, coef, msg = sb("norm", [P, TB, 2]), sb("dot", [P, TB, 2]), sb("coef", [P, 2, TB]), sb("msg", [P, TB, 2, D])
        rest, three = sb("rest", [P, TB, 2, D]), sb("three", [P, 2, TB, 2, 3 * D], BF16)
        xd, et_ps, hid_ps = ps("xd", [P, TB, HW]), ps("et_ps", [2 * D, TB * P]), ps("hid_ps", [P, TB * P])
        v_ps, sums = ps("v_ps", [P, TB, 2 * D]), ps("sums", [P, 512])
        gathered, loaded = [[sem("gathered0")], [sem("gathered1")]], [sem("loaded0"), sem("loaded1")]
        names = ("idx_s", "hot_t_s", "hot_s", "xd_s", "ends_s", "et_s", "ends_t_s", "hp_s", "hid_s", "v_s", "vec_s", "norm_s",
                 "root_s", "three_s", "kept_s", "used", "chain")
        (idx_s, hot_t_s, hot_s, xd_s, ends_s, et_s, ends_t_s, hp_s, hid_s, v_s, vec_s, norm_s, root_s, three_s,
         kept_s, used, chain) = map(sem, names)
        block = ctx.enter_context(nc.Block())
        LINKS = 17
        shape = [P, TB, 2, D]

        @block.gpsimd
        def _(pool):
            gather(nc, m, pool, m.node20, idx, ring, idx_s, gathered, TB, total // 2)

        @block.sync
        def _(sp):
            low_rows = m.low_row.rearrange("(c n) -> c n", n=TB * P)

            def load(q, h):
                n = 2 * q + h
                wait(sp, hot_t_s, n - 1)
                sp.dma_start(low[:, h], low_rows[bass.ds(n, 1)].to_broadcast([P, TB * P])).then_inc(loaded[h], 16)

            batches(sp, total, 3, 1, load)

        @block.vector
        def _(dve):
            def indices(n, h):
                nc.vector.tensor_copy(idx[:, h, :], slot_field(m, n * TB, TB, SRC)).then_inc(idx_s, 1)

            def far_hots(q, h):
                n = 2 * q + h
                dve.wait_ge(loaded[h], (q + 1) * 16)
                wait(dve, xd_s, n)
                nc.vector.tensor_scalar(hot_t[:, :], low[:, h], m.iota_col[:, 0:1], None, ALU.is_equal).then_inc(hot_t_s, 1)

            def spread_hots(n, h):
                wait(dve, used, n - 1)
                nc.vector.tensor_tensor(hot[:, h], slot_field(m, n * TB, TB, LO)[:, :, None].to_broadcast([P, TB, P]),
                                        m.iota_row[:, None, :].to_broadcast([P, TB, P]), ALU.is_equal).then_inc(hot_s, 1)

            def gather_ends(q, h):
                n = 2 * q + h
                dve.wait_ge(gathered[h][0], (q + 1) * 16 * TB)
                dve.wait_ge(xd_s, n + 1)
                nc.vector.tensor_copy(ends[:, h, :, 0, :], ring[:, h, :, 0:D])
                nc.vector.tensor_copy(coef[:, h, :], ring[:, h, :, D])
                nc.vector.tensor_copy(ends[:, h, :, 1, :], xd[:, :, 0:D]).then_inc(ends_s, 1)
                dve.wait_ge(ends_s, n + 1)
                nc.vector.tensor_tensor(coef[:, h, :], xd[:, :, D], coef[:, h, :], ALU.mult).then_inc(vec_s, 1)
                if inside(n + 2, total):
                    indices(n + 2, h)

            def turn(q, h):
                n = 2 * q + h
                c = [LINKS * n]

                def link(ins):
                    c[0] = c[0] + 1
                    ins.then_inc(chain, 1)
                    dve.wait_ge(chain, c[0])

                def flat(t):
                    return t[:, :, :, :].rearrange("q t a d -> q t (a d)")

                spread_hots(n, h)
                dve.wait_ge(v_s, 2 * n + 2)
                link(nc.vector.tensor_tensor(flat(vec), v_ps[:, :, :], m.mlp_b2[:, None, :].to_broadcast([P, TB, 2 * D]), ALU.add))
                link(nc.vector.tensor_tensor(sq[:, :, :, :], vec[:, :, :, :], vec[:, :, :, :], ALU.mult))
                nc.vector.tensor_reduce(norm[:, :, :], sq[:, :, :, :], AX.X, ALU.add).then_inc(norm_s, 1)
                if inside(n + 2, total):
                    far_hots(q + 1, h)
                dve.wait_ge(root_s, n + 1)
                link(nc.vector.tensor_scalar(norm[:, :, :], norm[:, :, :], 1e-12, None, ALU.max))
                link(nc.vector.reciprocal(norm[:, :, :], norm[:, :, :]))
                link(nc.vector.tensor_tensor(vec[:, :, :, :], vec[:, :, :, :], norm[:, :, :, None].to_broadcast(shape), ALU.mult))

                def reflect(y):
                    link(nc.vector.tensor_tensor(sq[:, :, :, :], vec[:, :, :, :], y, ALU.mult))
                    link(nc.vector.tensor_reduce(dot[:, :, :], sq[:, :, :, :], AX.X, ALU.add))
                    link(nc.vector.scalar_tensor_tensor(msg[:, :, :, :].rearrange("q t a d -> q (t a) d"),
                                                        vec[:, :, :, :].rearrange("q t a d -> q (t a) d"), 2.0,
                                                        dot[:, :, :].rearrange("q t a -> q (t a)")[:, :, None].to_broadcast([P, 2 * TB, D]),
                                                        ALU.mult, ALU.mult))

                reflect(ends[:, h])
                nc.vector.tensor_tensor(swap[:, :, 1, :], ends[:, h, :, 0, :], msg[:, :, 0, :], ALU.subtract)
                link(nc.vector.tensor_tensor(swap[:, :, 0, :], ends[:, h, :, 1, :], msg[:, :, 1, :], ALU.subtract))
                reflect(swap[:, :, :, :])
                link(nc.vector.tensor_tensor(msg[:, :, :, :], swap[:, :, :, :], msg[:, :, :, :], ALU.subtract))
                link(nc.vector.tensor_tensor(flat(msg), flat(msg), coef[:, h, :, None].to_broadcast([P, TB, 2 * D]), ALU.mult))
                wait(dve, used, n - 1)
                wait(dve, kept_s, n - 1)
                link(nc.vector.tensor_copy(three[:, h, :, :, 0:D], msg[:, :, :, :]))
                link(nc.vector.tensor_tensor(rest[:, :, :, :], msg[:, :, :, :], three[:, h, :, :, 0:D], ALU.subtract))
                link(nc.vector.tensor_copy(three[:, h, :, :, D:2 * D], rest[:, :, :, :]))
                nc.vector.tensor_tensor(three[:, h, :, :, 2 * D:3 * D], rest[:, :, :, :], three[:, h, :, :, D:2 * D],
                                        ALU.subtract).then_inc(three_s, 1)
                if inside(n + 2, total):
                    gather_ends(q + 1, h)

            for h in range(2):
                indices(h, h)
            far_hots(0, 0)
            gather_ends(0, 0)
            far_hots(0, 1)
            gather_ends(0, 1)
            batches(dve, total, 3, 5, turn)
            dve.wait_ge(used, total)
            nc.vector.tensor_tensor(m.h[:, :, :], m.h[:, :, :], sums[:, 0:NB * D].rearrange("q (b d) -> q b d", d=D), ALU.add).then_inc(norm_s, 1)

        @block.scalar
        def _(act):
            def network(n):
                act.wait_ge(et_s, n + 1)
                nc.scalar.copy(ends_t[:, :], et_ps[:, :]).then_inc(ends_t_s, 1)
                for half in range(2):
                    act.wait_ge(hp_s, 2 * n + half + 1)
                    nc.scalar.activation(hid[:, half * 512:(half + 1) * 512], hid_ps[:, half * 512:(half + 1) * 512], ACT.Relu,
                                         bias=m.mlp_b1[:, 0:1]).then_inc(hid_s, 1)

            def turn(q, h):
                n = 2 * q + h
                act.wait_ge(norm_s, n + 1)
                nc.scalar.activation(norm[:, :, :], norm[:, :, :], ACT.Sqrt).then_inc(root_s, 1)
                if inside(n + 1, total):
                    network(n + 1)
                act.wait_ge(three_s, n + 1)
                nc.scalar.copy(m.parts[:, bass.ds(n * TB, TB), :], three[:, h, :, 0, :]).then_inc(kept_s, 1)

            network(0)
            batches(act, total, 1, 1, turn)

        @block.tensor
        def _(pe):
            clear(nc, m, sums[:, :])

            def far_ends(q, h):
                n = 2 * q + h
                pe.wait_ge(hot_t_s, n + 1)
                wait(pe, vec_s, n)
                for k in range(TB // 2):
                    b = block_of(m, pe, n * TB + 2 * k)
                    for j in (2 * k, 2 * k + 1):
                        for part in range(3):
                            last = nc.tensor.matmul(xd[:, j, :], hot_t[:, j * P:(j + 1) * P],
                                                    m.wide3[:, bass.ds(b, 1), part, :].rearrange("q o c -> q (o c)"), start=part == 0,
                                                    stop=part == 2, skip_group_check=True)
                last.then_inc(xd_s, 1)

            def turned_ends(n, h):
                pe.wait_ge(ends_s, n + 1)
                pe.sem_inc(m.pe_passed, 1)
                for j in range(TB):
                    last = nc.tensor.transpose(et_ps[:, j * P:(j + 1) * P], ends[:, h, j, :, :].rearrange("q a d -> q (a d)"), m.ident[:, :])
                last.then_inc(et_s, 1)

            def network(n):
                pe.wait_ge(ends_t_s, n + 1)
                for c in range(0, TB * P, 512):
                    nc.tensor.matmul(hid_ps[:, c:c + 512], m.mlp1[:, :], ends_t[:, c:c + 512], start=True, stop=True).then_inc(hp_s, 1)

            def vectors(n, half):
                pe.wait_ge(hid_s, 2 * n + half + 1)
                if half == 0:
                    wait(pe, norm_s, n)
                for j in range(half * TB // 2, (half + 1) * TB // 2):
                    last = nc.tensor.matmul(v_ps[:, j, :], hid[:, j * P:(j + 1) * P], m.mlp2[:, :], start=True, stop=True,
                                            skip_group_check=True)
                last.then_inc(v_s, 1)

            def spread(n, h):
                pe.wait_ge(hot_s, n + 1)
                pe.wait_ge(three_s, n + 1)
                for k in range(TB // 2):
                    b = block_of(m, pe, n * TB + 2 * k)
                    for j in (2 * k, 2 * k + 1):
                        for part in range(3):
                            last = nc.tensor.matmul(sums[:, bass.ds(b * D, D)], hot[:, h, j, :],
                                                    three[:, h, j, 1, part * D:(part + 1) * D], start=False, stop=True,
                                                    skip_group_check=True)
                last.then_inc(used, 1)

            def turn(q, h):
                n = 2 * q + h
                if inside(n + 1, total):
                    turned_ends(n + 1, 1 - h)
                if inside(n - 1, total):
                    spread(n - 1, 1 - h)
                if inside(n + 1, total):
                    network(n + 1)
                if inside(n + 2, total):
                    far_ends(q + 1, h)
                if inside(n + 1, total):
                    for half in range(2):
                        vectors(n + 1, half)

            far_ends(0, 0)
            turned_ends(0, 0)
            network(0)
            far_ends(0, 1)
            for half in range(2):
                vectors(0, half)
            batches(pe, total, 1, 3, turn)
            spread(total - 1, (total - 1) % 2)


def to_sources(nc, m):
    with ExitStack() as outer:
        _, ps, _ = makers(nc, outer, "src")
        sums = ps("sums", [3 * D, NP])
        with ExitStack() as ctx:
            sb, _, sem = makers(nc, ctx, "srl")
            wide, hot = sb("wide", [P, N], FP16), sb("hot", [P, 2, N], BF16)
            ring = sb("ring", [P, 2, TB, 3 * D], BF16)
            iota_s, hot_s, used, ring_s = sem("iota_s"), sem("hot_s"), sem("used"), sem("ring_s")
            block = ctx.enter_context(nc.Block())

            @block.gpsimd
            def _(pool):
                pool.iota(wide[:, :], pattern=[[1, N]], base=-CENTRE, channel_multiplier=0,
                          allow_small_or_imprecise_dtypes=True).then_inc(iota_s, 1)

            @block.vector
            def _(dve):
                dve.wait_ge(iota_s, 1)

                def turn(q, h):
                    t = 2 * q + h
                    wait(dve, used, t - 1)
                    nc.vector.tensor_scalar(hot[:, h, :], wide[:, :], slot_field(m, t, 1, SRCC), None, ALU.is_equal).then_inc(hot_s, 1)

                batches(dve, NT, 3, 1, turn)

            @block.scalar
            def _(act):
                def turn(q, h):
                    n = 2 * q + h
                    wait(act, used, (n - 1) * TB)
                    nc.scalar.copy(ring[:, h], m.parts[:, bass.ds(n * TB, TB), :]).then_inc(ring_s, 1)

                batches(act, NT // TB, 3, 1, turn)

            @block.tensor
            def _(pe):
                clear(nc, m, sums[:, :])
                with pe.Fori(0, NT // TB // 2) as i:
                    for h in range(2):
                        pe.wait_ge(ring_s, 2 * i + h + 1)
                        for j in range(TB):
                            pe.wait_ge(hot_s, (2 * i + h) * TB + j + 1)
                            for c in range(0, N, 512):
                                w = min(512, N - c)
                                last = nc.tensor.matmul(sums[:, c:c + w], ring[:, h, j, :], hot[:, j % 2, c:c + w], start=False,
                                                        stop=True, skip_group_check=True)
                            last.then_inc(used, 1)
                pe.wait_ge(used, NT)
        with ExitStack() as ctx:
            sb, ps, sem = makers(nc, ctx, "srx")
            total = sb("total", [3 * D, NP])
            back = ps("back", [P, 10, 3 * D])
            copied, made, step = sem("copied"), sem("made"), sem("step")
            block = ctx.enter_context(nc.Block())

            @block.scalar
            def _(act):
                nc.scalar.copy(total[:, :], sums[:, :]).then_inc(copied, 1)

            @block.tensor
            def _(pe):
                pe.wait_ge(copied, 1)
                for b in range(NB):
                    if b % 10 == 0:
                        wait(pe, step, 3 * (b // 10))
                    last = nc.tensor.transpose(back[:, b % 10, :], total[:, b * P:(b + 1) * P], m.ident[0:3 * D, 0:3 * D])
                    if b % 10 == 9 or b == NB - 1:
                        last.then_inc(made, 1)

            @block.vector
            def _(dve):
                for n, b in enumerate(range(0, NB, 10)):
                    c = min(10, NB - b)
                    dve.wait_ge(made, n + 1)
                    for k in range(3):
                        wait(dve, step, 3 * n + k)
                        nc.vector.tensor_tensor(m.h[:, b:b + c, :], m.h[:, b:b + c, :], back[:, 0:c, k * D:(k + 1) * D],
                                                ALU.add).then_inc(step, 1)


def finish(nc, m, out):
    with ExitStack() as ctx:
        sb, ps, sem = makers(nc, ctx, "fin")
        done, saved = sem("done"), sem("saved")
        block = ctx.enter_context(nc.Block())

        @block.vector
        def _(dve):
            nc.vector.scalar_tensor_tensor(m.x[:, :, :].rearrange("q b d -> q (b d)"), m.h[:, :, :].rearrange("q b d -> q (b d)"), 0.0,
                                           m.x[:, :, :].rearrange("q b d -> q (b d)"), ALU.max, ALU.add).then_inc(done, 1)

        @block.sync
        def _(sp):
            sp.wait_ge(done, 1)
            sp.dma_start(out[0:(NB - 1) * P, :].rearrange("(b q) d -> q b d", q=P), m.x[:, 0:NB - 1, :]).then_inc(saved, 16)
            sp.dma_start(out[(NB - 1) * P:N, :], m.x[0:TAIL, NB - 1, :]).then_inc(saved, 16)
            sp.wait_ge(saved, 32)


_INS = ['x', 'src', 'dst', 'edge_attr_16', 'edge_type_8', 'edge_weight', 'L0_gnn_edge_emb', 'L0_gnn_w_ih', 'L0_gnn_w_hh',
        'L0_gnn_b_ih', 'L0_gnn_b_hh', 'L1_gnn_W_msg', 'L1_gnn_b_msg', 'L1_gnn_W_attn', 'L1_gnn_b_attn', 'L2_gnn_w0',
        'L2_gnn_b0', 'L2_gnn_w1', 'L2_gnn_b1', 'L2_gnn_w2', 'L2_gnn_b2', 'L2_gnn_w3', 'L2_gnn_b3', 'L3_gnn_W1',
        'L3_gnn_b1', 'L3_gnn_W2', 'L3_gnn_b2']

def build(nc, a, out):
    PAST.clear()
    m = Net()

    def dram(name, shape):
        return nc.dram_tensor(name, shape, F32).ap()

    m.key_rows, m.hi_rows = dram("key_rows", [EC, EP]), dram("hi_rows", [EC, EP])
    m.slots, m.spare = dram("slots", [SLOTS, REC]), dram("spare", [2, D])
    m.slot_keys, m.far_row, m.end_row = dram("slot_keys", [SLOTS + 2]), dram("far_row", [SLOTS]), dram("end_row", [SLOTS])
    m.feat_t = nc.dram_tensor("feat_t", [KP, SLOTS], BF16).ap()
    m.low_row = nc.dram_tensor("low_row", [SLOTS], FP16).ap()
    m.node40 = dram("node40", [NP, W40])
    m.typed, m.node16, m.node20 = dram("typed", [NP * 8, D]), dram("node16", [NP, D]), dram("node20", [NP, HW])
    m.node_g3 = dram("node_g3", [NP, D])
    m.node128 = [dram("node128a", [NP, P]), dram("node128b", [NP, P])]
    m.dinv_dram = dram("dinv_dram", [NP])
    with ExitStack() as ctx:
        def on(scope):
            return lambda name, shape, dt=F32: scope.enter_context(nc.sbuf_tensor(name, shape, dt))

        sb = on(ctx)
        m.pool_passed, m.pe_passed = ctx.enter_context(nc.semaphore("pool_passed")), ctx.enter_context(nc.semaphore("pe_passed"))
        m.fields = sb("fields", [P, NT, NF])
        m.ident_bf, m.widen, m.w6 = sb("ident_bf", [P, P], BF16), sb("widen", [3 * D, 256], BF16), sb("w6", [KP, 512], BF16)
        m.ident, m.below, m.above, m.twice = (sb(n, [P, P]) for n in ("ident", "below", "above", "twice"))
        m.iota_row, m.iota_col = sb("iota_row", [P, P]), sb("iota_col", [P, 1])
        m.zero_row = sb("zero_row", [1, 512])
        m.blk = sb("blk", [1, NT], I32)
        m.dis, m.dinv = sb("dis", [P, NB]), sb("dinv", [P, NB])
        m.x, m.h = sb("x", [P, NB, D]), sb("h", [P, NB, D])
        m.emb = sb("emb", [D, 8 * D])
        m.gru_i, m.gru_h = sb("gru_i", [D + 1, 4 * D]), sb("gru_h", [D + 1, 4 * D])
        shapes = [(D, P), (P, P), (P, P), (P, D)]
        m.conv_w = [sb(f"conv_w{k}", list(s)) for k, s in enumerate(shapes)]
        m.conv_b = [sb(f"conv_b{k}", [s[1], 1]) for k, s in enumerate(shapes)]
        m.mlp1, m.mlp_b1, m.mlp2, m.mlp_b2 = sb("mlp1", [2 * D, P]), sb("mlp_b1", [P, 1]), sb("mlp2", [P, 2 * D]), sb("mlp_b2", [P, 2 * D])
        with ExitStack() as scope:
            rb = on(scope)
            m.iota_tiles, m.edges = rb("iota_tiles", [P, NT]), rb("edges", [EP, EC * REC])
            m.key_f, m.hi_f, m.lo_f, m.src_hi_f, m.src_lo_f = (rb(n, [EP, EC]) for n in ("key_f", "hi_f", "lo_f", "src_hi_f", "src_lo_f"))
            m.first = rb("first", [NB, NS, P])
            record_keys(nc, a, m)
            histogram(nc, m)
            rank_and_scatter(nc, m)
        weights(nc, a, m)
        unpack(nc, m)
        segments(nc, m)
        with ExitStack() as scope:
            rb = on(scope)
            m.ht, m.mt, m.sums = rb("ht", [D + 1, NP]), rb("mt", [D + 1, NP]), rb("sums", [P, NB, 20])
            normalise(nc, m, "n0")
            type_table(nc, m)
            aggregate_typed(nc, m)
            gru(nc, m)
        with ExitStack() as scope:
            rb = on(scope)
            m.top3, m.held = rb("top3", [P, NB, 3, 256], BF16), rb("held", [P, NT, D])
            normalise(nc, m, "n1")
            attention_rows(nc, m)
            with ExitStack() as tops:
                m.top = on(tops)("top", [P, NB, 256])
                segment_max(nc, m)
                split_top(nc, m)
            m.acc = rb("acc", [P, NB, 512])
            soft_sums(nc, m)
            attend(nc, m)
        renew_semaphores(nc)
        with ExitStack() as scope:
            rb = on(scope)
            m.g, m.agg, m.hidden, m.dinv_row = rb("g", [P, NB, P]), rb("agg", [P, NP]), rb("hidden", [P, NP]), rb("dinv_row", [P, NP])
            normalise(nc, m, "n2")
            node_factors(nc, m)
            convolve(nc, m, "c0", m.node16, D)
            dense(nc, m, "d0", 0)
            project(nc, m, "p1", 1, m.node128[0], P, False)
            convolve(nc, m, "c1", m.node128[0], P)
            project(nc, m, "p2", 2, m.node128[1], P, True)
            convolve(nc, m, "c2", m.node128[1], P)
            project(nc, m, "p3", 3, m.node_g3, D, True)
            convolve(nc, m, "c3", m.node_g3, D)
            close_convolutions(nc, m)
        with ExitStack() as scope:
            rb = on(scope)
            m.parts, m.wide3 = rb("parts", [P, NT, 3 * D], BF16), rb("wide3", [P, NB, 3, HW], BF16)
            normalise(nc, m, "n3")
            sheaf_rows(nc, m)
            sheaf_messages(nc, m)
            to_sources(nc, m)
            finish(nc, m, out)


def kernel(**inputs):
    import numpy as _np
    import concourse.bacc as _bacc
    from concourse import mybir as _mybir
    from concourse.bass_utils import run_bass_kernel_spmd as _run

    nc = _bacc.Bacc("TRN2", target_bir_lowering=False, num_devices=1)
    arrays, aps = {}, {}
    for name in _INS:
        arr = _np.ascontiguousarray(inputs[name])
        arrays[f"in_{name}"] = arr
        aps[name] = nc.dram_tensor(f"in_{name}", arr.shape, _mybir.dt.from_np(arr.dtype), kind="ExternalInput").ap()
    out = nc.dram_tensor("out_0", (N, D), _mybir.dt.float32, kind="ExternalOutput").ap()
    build(nc, aps, out)
    r = _run(nc, [arrays], core_ids=[0])
    return r.results[0]["out_0"]
```
